# Optimizing a Trainium2 kernel written in Bass

```python
import numpy as np
import jax
import jax.numpy as jnp

def _softmax(x, axis=-1):
    return jax.nn.softmax(x, axis=axis)

def _gelu(x):
    return jax.nn.gelu(x, approximate=True)

def _silu(x):
    return jax.nn.silu(x)

def _sigmoid(x):
    return jax.nn.sigmoid(x)

def _layernorm(x, axis=-1, eps=1e-05):
    m = jnp.mean(x, axis=axis, keepdims=True)
    v = jnp.var(x, axis=axis, keepdims=True)
    return (x - m) / jnp.sqrt(v + eps)

def _scatter_add(tgt, idx, src, axis=0):
    return tgt.at[idx].add(src)

def _segment_sum(src, seg, n):
    return jax.ops.segment_sum(src, seg, n)
kernel_name = 'mk_xattn_ffn_d2_seqx_r8_679c92'

def setup_inputs(seed: int=0):
    np.random.seed(seed)
    _w = jnp.asarray

    def _rec_inputs():
        import jax
        import jax.numpy as jnp
        _rk = jax.random.key(seed)
        x = -0.0002928 + 1 * jax.random.normal(jax.random.fold_in(_rk, 1), (16, 256, 128), jnp.float32)
        _lenS = 256 - jax.random.randint(jax.random.fold_in(_rk, 7), (16,), 0, max(1, 256 // 4) + 1, jnp.int32)
        _lenS2 = 1601 - jax.random.randint(jax.random.fold_in(_rk, 8), (16,), 0, max(1, 1601 // 4) + 1, jnp.int32)
        _ctx_1024P = jax.random.normal(jax.random.fold_in(_rk, 11), (16, 16, 128), jnp.float32)
        _ctx_1024c = jax.random.dirichlet(jax.random.fold_in(_rk, 511), 0.3 * jnp.ones((16,), jnp.float32), (16, 1601))
        _ctx_1024t = jnp.einsum('bsk,bkd->bsd', _ctx_1024c, _ctx_1024P)
        _ctx_1024t = _ctx_1024t * jax.lax.rsqrt(jnp.mean(jnp.square(_ctx_1024t)) + 1e-12) * 0.953939
        ctx_1024 = -1.52775e-05 + 0.999936 * (_ctx_1024t + 0.3 * jax.random.normal(jax.random.fold_in(_rk, 611), (16, 1601, 128), jnp.float32))
        return (x, ctx_1024, _lenS2)
    x, ctx_1024, _lenS2 = _rec_inputs()

    def _L0_xattn_setup():
        import jax, jax.numpy as jnp
        import numpy as np
        DIM = 128
        NUM_HEADS = 8
        HEAD_DIM = 64
        INNER = NUM_HEADS * HEAD_DIM
        key = jax.random.key(seed)
        ks = jax.random.split(key, 7)
        B, N, M = (8, 64, 512)
        x = jax.random.normal(ks[0], (B, N, DIM), dtype=jnp.float32)
        context = jax.random.normal(ks[1], (B, M, DIM), dtype=jnp.float32)
        s_in = 1.0 / np.sqrt(DIM)
        s_inner = 1.0 / np.sqrt(INNER)
        Wq = jax.random.normal(ks[2], (DIM, INNER), dtype=jnp.float32) * s_in
        Wk = jax.random.normal(ks[3], (DIM, INNER), dtype=jnp.float32) * s_in
        Wv = jax.random.normal(ks[4], (DIM, INNER), dtype=jnp.float32) * s_in
        Wo = jax.random.normal(ks[5], (INNER, DIM), dtype=jnp.float32) * s_inner
        bo = jax.random.normal(ks[6], (DIM,), dtype=jnp.float32) * 0.01
        return {'x': x, 'context': context, 'Wq': Wq, 'Wk': Wk, 'Wv': Wv, 'Wo': Wo, 'bo': bo}
    _L0_xattn_all = _L0_xattn_setup()
    _L0_xattn_in = {k: v for k, v in _L0_xattn_all.items() if k in ('Wq', 'Wk', 'Wv', 'Wo', 'bo')}
    del _L0_xattn_all

    def _L0_ffn_setup():
        import jax, jax.numpy as jnp
        import numpy as np

        def _bitlinear(x, w_latent):
            scale = jax.lax.stop_gradient(jnp.clip(jnp.mean(jnp.abs(w_latent), axis=1, keepdims=True), 1e-05, None))
            tern = jnp.clip(jnp.round(w_latent / scale), -1.0, 1.0)
            w = w_latent + jax.lax.stop_gradient(tern - w_latent)
            return x @ (w * scale).T
        key = jax.random.key(seed)
        ks = jax.random.split(key, 6)
        dim, hidden, rank = (128, 512, 16)
        B, S = (4, 512)
        x = jax.random.normal(ks[0], (B, S, dim), dtype=jnp.float32)
        w_fc = 0.02 * jax.random.normal(ks[1], (hidden, dim), dtype=jnp.float32)
        w_proj = 0.02 * jax.random.normal(ks[2], (dim, hidden), dtype=jnp.float32)
        u = 0.02 * jax.random.normal(ks[3], (hidden, rank), dtype=jnp.float32)
        v = 0.02 * jax.random.normal(ks[4], (rank, dim), dtype=jnp.float32)
        fast_b = jax.random.normal(ks[5], (rank, rank), dtype=jnp.float32)
        gate = jnp.float32(0.05)
        return {'x': x, 'fast_b': fast_b, 'w_fc': w_fc, 'w_proj': w_proj, 'u': u, 'v': v, 'gate': gate}
    _L0_ffn_all = _L0_ffn_setup()
    _L0_ffn_in = {k: v for k, v in _L0_ffn_all.items() if k in ('fast_b', 'w_fc', 'w_proj', 'u', 'v', 'gate')}
    del _L0_ffn_all

    def _L1_xattn_setup():
        import jax, jax.numpy as jnp
        import numpy as np
        B, S, D, H = (4, 256, 128, 16)
        NEG = -1000000.0
        key = jax.random.key(seed)
        ks = jax.random.split(key, 9)
        scale = 1.0 / np.sqrt(D)
        return {'queries': jax.random.normal(ks[0], (B, S, D), jnp.float32), 'keys': jax.random.normal(ks[1], (B, S, D), jnp.float32), 'values': jax.random.normal(ks[2], (B, S, D), jnp.float32), 'valid_lens': jax.random.randint(ks[3], (B,), 1, S + 1, jnp.int32), 'Wq': jax.random.normal(ks[4], (D, D), jnp.float32) * scale, 'Wk': jax.random.normal(ks[5], (D, D), jnp.float32) * scale, 'Wv': jax.random.normal(ks[6], (D, D), jnp.float32) * scale, 'Wo': jax.random.normal(ks[7], (D, D), jnp.float32) * scale}
    _L1_xattn_all = _L1_xattn_setup()
    _L1_xattn_in = {k: v for k, v in _L1_xattn_all.items() if k in ('Wq', 'Wk', 'Wv', 'Wo')}
    del _L1_xattn_all

    def _L1_ffn_setup():
        import jax, jax.numpy as jnp
        import numpy as np
        N_HEAD = 16
        NUM_EXPERTS = 8
        TOP_K = 2
        LN_EPS = 1e-05

        def _layernorm(x, g, b):
            mu = jnp.mean(x, axis=-1, keepdims=True)
            var = jnp.mean(jnp.square(x - mu), axis=-1, keepdims=True)
            return (x - mu) * jax.lax.rsqrt(var + LN_EPS) * g + b

        def _attention(h, Wq, bq, Wk, bk, Wv, bv, Wp, bp):
            B, T, D = h.shape
            hd = D // N_HEAD

            def split(z):
                return z.reshape(B, T, N_HEAD, hd).transpose(0, 2, 1, 3)
            q = split(h @ Wq + bq)
            k = split(h @ Wk + bk)
            v = split(h @ Wv + bv)
            att = jnp.einsum('bhqd,bhkd->bhqk', q, k) / jnp.sqrt(jnp.float32(hd))
            causal = jnp.tril(jnp.ones((T, T), bool))
            att = jnp.where(causal, att, -jnp.inf)
            att = jax.nn.softmax(att, axis=-1)
            y = jnp.einsum('bhqk,bhkd->bhqd', att, v)
            y = y.transpose(0, 2, 1, 3).reshape(B, T, D)
            return y @ Wp + bp

        def _token_moe(h, gate_W, gate_b, exp_W1, exp_b1, exp_W2, exp_b2):
            B, T, D = h.shape
            flat = h.reshape(-1, D)
            N = flat.shape[0]
            logits = flat @ gate_W + gate_b
            top_v, top_i = jax.lax.top_k(logits, TOP_K)
            w = jax.nn.softmax(top_v, axis=-1)
            w_full = jnp.zeros((N, NUM_EXPERTS), flat.dtype)
            w_full = w_full.at[jnp.arange(N)[:, None], top_i].add(w)
            out = jnp.zeros_like(flat)
            for e in range(NUM_EXPERTS):
                mid = jax.nn.gelu(flat @ exp_W1[e] + exp_b1[e], approximate=False)
                y_e = mid @ exp_W2[e] + exp_b2[e]
                out = out + w_full[:, e:e + 1] * y_e
            return out.reshape(B, T, D)
        key = jax.random.key(seed)
        B, T, D = (8, 128, 128)
        H = 4 * D
        E = NUM_EXPERTS
        ks = jax.random.split(key, 24)
        s = 0.02
        inp = {'x': jax.random.normal(ks[0], (B, T, D), jnp.float32), 'ln1_g': jnp.ones((D,), jnp.float32), 'ln1_b': jnp.zeros((D,), jnp.float32), 'ln2_g': jnp.ones((D,), jnp.float32), 'ln2_b': jnp.zeros((D,), jnp.float32), 'Wq': jax.random.normal(ks[1], (D, D), jnp.float32) * s, 'bq': jnp.zeros((D,), jnp.float32), 'Wk': jax.random.normal(ks[2], (D, D), jnp.float32) * s, 'bk': jnp.zeros((D,), jnp.float32), 'Wv': jax.random.normal(ks[3], (D, D), jnp.float32) * s, 'bv': jnp.zeros((D,), jnp.float32), 'Wp': jax.random.normal(ks[4], (D, D), jnp.float32) * s, 'bp': jnp.zeros((D,), jnp.float32), 'gate_W': jax.random.normal(ks[5], (D, E), jnp.float32) * s, 'gate_b': jnp.zeros((E,), jnp.float32), 'exp_W1': jax.random.normal(ks[6], (E, D, H), jnp.float32) * s, 'exp_b1': jnp.zeros((E, H), jnp.float32), 'exp_W2': jax.random.normal(ks[7], (E, H, D), jnp.float32) * s, 'exp_b2': jnp.zeros((E, D), jnp.float32)}
        return inp
    _L1_ffn_all = _L1_ffn_setup()
    _L1_ffn_in = {k: v for k, v in _L1_ffn_all.items() if k in ('ln1_g', 'ln1_b', 'ln2_g', 'ln2_b', 'Wq', 'bq', 'Wk', 'bk', 'Wv', 'bv', 'Wp', 'bp', 'gate_W', 'gate_b', 'exp_W1', 'exp_b1', 'exp_W2', 'exp_b2')}
    del _L1_ffn_all
    return {'x': x, 'ctx_1024': ctx_1024, '_lenS2': _lenS2, 'L0_xattn_Wq': _L0_xattn_in['Wq'], 'L0_xattn_Wk': _L0_xattn_in['Wk'], 'L0_xattn_Wv': _L0_xattn_in['Wv'], 'L0_xattn_Wo': _L0_xattn_in['Wo'], 'L0_xattn_bo': _L0_xattn_in['bo'], 'L0_ffn_fast_b': _L0_ffn_in['fast_b'], 'L0_ffn_w_fc': _L0_ffn_in['w_fc'], 'L0_ffn_w_proj': _L0_ffn_in['w_proj'], 'L0_ffn_u': _L0_ffn_in['u'], 'L0_ffn_v': _L0_ffn_in['v'], 'L0_ffn_gate': _L0_ffn_in['gate'], 'L1_xattn_Wq': _L1_xattn_in['Wq'], 'L1_xattn_Wk': _L1_xattn_in['Wk'], 'L1_xattn_Wv': _L1_xattn_in['Wv'], 'L1_xattn_Wo': _L1_xattn_in['Wo'], 'L1_ffn_ln1_g': _L1_ffn_in['ln1_g'], 'L1_ffn_ln1_b': _L1_ffn_in['ln1_b'], 'L1_ffn_ln2_g': _L1_ffn_in['ln2_g'], 'L1_ffn_ln2_b': _L1_ffn_in['ln2_b'], 'L1_ffn_Wq': _L1_ffn_in['Wq'], 'L1_ffn_bq': _L1_ffn_in['bq'], 'L1_ffn_Wk': _L1_ffn_in['Wk'], 'L1_ffn_bk': _L1_ffn_in['bk'], 'L1_ffn_Wv': _L1_ffn_in['Wv'], 'L1_ffn_bv': _L1_ffn_in['bv'], 'L1_ffn_Wp': _L1_ffn_in['Wp'], 'L1_ffn_bp': _L1_ffn_in['bp'], 'L1_ffn_gate_W': _L1_ffn_in['gate_W'], 'L1_ffn_gate_b': _L1_ffn_in['gate_b'], 'L1_ffn_exp_W1': _L1_ffn_in['exp_W1'], 'L1_ffn_exp_b1': _L1_ffn_in['exp_b1'], 'L1_ffn_exp_W2': _L1_ffn_in['exp_W2'], 'L1_ffn_exp_b2': _L1_ffn_in['exp_b2']}

def reference(x, ctx_1024, _lenS2, L0_xattn_Wq, L0_xattn_Wk, L0_xattn_Wv, L0_xattn_Wo, L0_xattn_bo, L0_ffn_fast_b, L0_ffn_w_fc, L0_ffn_w_proj, L0_ffn_u, L0_ffn_v, L0_ffn_gate, L1_xattn_Wq, L1_xattn_Wk, L1_xattn_Wv, L1_xattn_Wo, L1_ffn_ln1_g, L1_ffn_ln1_b, L1_ffn_ln2_g, L1_ffn_ln2_b, L1_ffn_Wq, L1_ffn_bq, L1_ffn_Wk, L1_ffn_bk, L1_ffn_Wv, L1_ffn_bv, L1_ffn_Wp, L1_ffn_bp, L1_ffn_gate_W, L1_ffn_gate_b, L1_ffn_exp_W1, L1_ffn_exp_b1, L1_ffn_exp_W2, L1_ffn_exp_b2):
    import jax
    import jax.numpy as jnp

    def _L0_xattn_ref(x, context, Wq, Wk, Wv, Wo, bo):
        import jax, jax.numpy as jnp
        import numpy as np
        DIM = 128
        NUM_HEADS = 8
        HEAD_DIM = 64
        INNER = NUM_HEADS * HEAD_DIM
        B, N, _ = x.shape
        M = context.shape[1]
        scale = HEAD_DIM ** (-0.5)
        q = (x @ Wq).reshape(B, N, NUM_HEADS, HEAD_DIM).transpose(0, 2, 1, 3)
        k = (context @ Wk).reshape(B, M, NUM_HEADS, HEAD_DIM).transpose(0, 2, 1, 3)
        v = (context @ Wv).reshape(B, M, NUM_HEADS, HEAD_DIM).transpose(0, 2, 1, 3)
        attn = jax.nn.softmax(jnp.einsum('bhnd,bhmd->bhnm', q, k) * scale, axis=-1)
        out = jnp.einsum('bhnm,bhmd->bhnd', attn, v)
        out = out.transpose(0, 2, 1, 3).reshape(B, N, INNER)
        return out @ Wo + bo

    def _L0_ffn_ref(x, fast_b, w_fc, w_proj, u, v, gate):
        import jax, jax.numpy as jnp
        import numpy as np

        def _bitlinear(x, w_latent):
            scale = jax.lax.stop_gradient(jnp.clip(jnp.mean(jnp.abs(w_latent), axis=1, keepdims=True), 1e-05, None))
            tern = jnp.clip(jnp.round(w_latent / scale), -1.0, 1.0)
            w = w_latent + jax.lax.stop_gradient(tern - w_latent)
            return x @ (w * scale).T
        h = _bitlinear(x, w_fc) + gate * (x @ v.T @ fast_b.T @ u.T)
        r = jnp.maximum(h, 0.0)
        return _bitlinear(r * r, w_proj)

    def _L1_xattn_ref(queries, keys, values, valid_lens, Wq, Wk, Wv, Wo):
        import jax, jax.numpy as jnp
        import numpy as np
        B, S, D, H = (4, 256, 128, 16)
        NEG = -1000000.0
        b, sq, _ = queries.shape
        skv = keys.shape[1]
        hd = D // H

        def split_heads(x):
            return x.reshape(b, -1, H, hd).transpose(0, 2, 1, 3)
        q = split_heads(queries @ Wq)
        k = split_heads(keys @ Wk)
        v = split_heads(values @ Wv)
        scores = jnp.einsum('bhqd,bhkd->bhqk', q, k) / jnp.sqrt(jnp.float32(hd))
        mask = jnp.arange(skv)[None, None, None, :] < valid_lens[:, None, None, None]
        scores = jnp.where(mask, scores, NEG)
        p_attn = jax.nn.softmax(scores, axis=-1)
        out = jnp.einsum('bhqk,bhkd->bhqd', p_attn, v)
        out = out.transpose(0, 2, 1, 3).reshape(b, sq, D)
        return out @ Wo

    def _L1_ffn_ref(x, ln1_g, ln1_b, ln2_g, ln2_b, Wq, bq, Wk, bk, Wv, bv, Wp, bp, gate_W, gate_b, exp_W1, exp_b1, exp_W2, exp_b2):
        import jax, jax.numpy as jnp
        import numpy as np
        N_HEAD = 16
        NUM_EXPERTS = 8
        TOP_K = 2
        LN_EPS = 1e-05

        def _layernorm(x, g, b):
            mu = jnp.mean(x, axis=-1, keepdims=True)
            var = jnp.mean(jnp.square(x - mu), axis=-1, keepdims=True)
            return (x - mu) * jax.lax.rsqrt(var + LN_EPS) * g + b

        def _attention(h, Wq, bq, Wk, bk, Wv, bv, Wp, bp):
            B, T, D = h.shape
            hd = D // N_HEAD

            def split(z):
                return z.reshape(B, T, N_HEAD, hd).transpose(0, 2, 1, 3)
            q = split(h @ Wq + bq)
            k = split(h @ Wk + bk)
            v = split(h @ Wv + bv)
            att = jnp.einsum('bhqd,bhkd->bhqk', q, k) / jnp.sqrt(jnp.float32(hd))
            causal = jnp.tril(jnp.ones((T, T), bool))
            att = jnp.where(causal, att, -jnp.inf)
            att = jax.nn.softmax(att, axis=-1)
            y = jnp.einsum('bhqk,bhkd->bhqd', att, v)
            y = y.transpose(0, 2, 1, 3).reshape(B, T, D)
            return y @ Wp + bp

        def _token_moe(h, gate_W, gate_b, exp_W1, exp_b1, exp_W2, exp_b2):
            B, T, D = h.shape
            flat = h.reshape(-1, D)
            N = flat.shape[0]
            logits = flat @ gate_W + gate_b
            top_v, top_i = jax.lax.top_k(logits, TOP_K)
            w = jax.nn.softmax(top_v, axis=-1)
            w_full = jnp.zeros((N, NUM_EXPERTS), flat.dtype)
            w_full = w_full.at[jnp.arange(N)[:, None], top_i].add(w)
            out = jnp.zeros_like(flat)
            for e in range(NUM_EXPERTS):
                mid = jax.nn.gelu(flat @ exp_W1[e] + exp_b1[e], approximate=False)
                y_e = mid @ exp_W2[e] + exp_b2[e]
                out = out + w_full[:, e:e + 1] * y_e
            return out.reshape(B, T, D)
        x = x + _attention(_layernorm(x, ln1_g, ln1_b), Wq, bq, Wk, bk, Wv, bv, Wp, bp)
        x = x + _token_moe(_layernorm(x, ln2_g, ln2_b), gate_W, gate_b, exp_W1, exp_b1, exp_W2, exp_b2)
        return x
    x = x + _L0_xattn_ref(_layernorm(x, axis=-1), ctx_1024, L0_xattn_Wq, L0_xattn_Wk, L0_xattn_Wv, L0_xattn_Wo, L0_xattn_bo)
    x = x + _L0_ffn_ref(_layernorm(x, axis=-1), L0_ffn_fast_b, L0_ffn_w_fc, L0_ffn_w_proj, L0_ffn_u, L0_ffn_v, L0_ffn_gate)
    x = x + _L1_xattn_ref(_layernorm(x, axis=-1), ctx_1024, ctx_1024, _lenS2, L1_xattn_Wq, L1_xattn_Wk, L1_xattn_Wv, L1_xattn_Wo)
    x = x + _L1_ffn_ref(_layernorm(x, axis=-1), L1_ffn_ln1_g, L1_ffn_ln1_b, L1_ffn_ln2_g, L1_ffn_ln2_b, L1_ffn_Wq, L1_ffn_bq, L1_ffn_Wk, L1_ffn_bk, L1_ffn_Wv, L1_ffn_bv, L1_ffn_Wp, L1_ffn_bp, L1_ffn_gate_W, L1_ffn_gate_b, L1_ffn_exp_W1, L1_ffn_exp_b1, L1_ffn_exp_W2, L1_ffn_exp_b2)
    return x

_drawn_inputs = setup_inputs


def setup_inputs(seed=0):
    import zlib

    import numpy as np

    out = dict(_drawn_inputs(seed))
    spreads = {'L1_ffn_ln1_g': (1.0, 0.6),
     'L1_ffn_ln1_b': (0.0, 0.8),
     'L1_ffn_ln2_g': (1.0, 0.6),
     'L1_ffn_ln2_b': (0.0, 0.728),
     'L1_ffn_bq': (0.0, 0.8),
     'L1_ffn_bk': (0.0, 2.0),
     'L1_ffn_bv': (0.0, 0.711),
     'L1_ffn_bp': (0.0, 0.37),
     'L1_ffn_gate_b': (0.0, 0.389),
     'L1_ffn_exp_b1': (0.0, 0.8),
     'L1_ffn_exp_b2': (0.0, 0.8)}
    factors = {'L0_xattn_bo': 6.16,
     'L0_ffn_fast_b': 8.0,
     'L0_ffn_w_fc': 6.804,
     'L0_ffn_w_proj': 5.639,
     'L0_ffn_u': 8.0,
     'L0_ffn_v': 8.0,
     'L1_ffn_Wq': 8.0,
     'L1_ffn_Wk': 8.0,
     'L1_ffn_Wv': 3.815,
     'L1_ffn_Wp': 3.248,
     'L1_ffn_exp_W1': 3.263,
     'L1_ffn_exp_W2': 2.954}
    for name, (base, spread) in spreads.items():
        noise = np.random.default_rng([zlib.crc32(name.encode()), seed]).standard_normal(out[name].shape)
        drawn = base * np.exp(spread * noise) if base else spread * noise
        out[name] = jnp.asarray(drawn.astype(out[name].dtype))
    for name, factor in factors.items():
        out[name] = (out[name] * factor).astype(out[name].dtype)
    return out
```

```python
from contextlib import ExitStack

import concourse.bass as bass
import numpy as np
from concourse import mybir

F32 = mybir.dt.float32
F32R = mybir.dt.float32r
BF16 = mybir.dt.bfloat16
F16 = mybir.dt.float16
I32 = mybir.dt.int32
U32 = mybir.dt.uint32
ALU = mybir.AluOpType
ACT = mybir.ActivationFunctionType
AX = mybir.AxisListType

B, T, D, S = 16, 256, 128, 1601
QT = T // 128
C = 13
ROWS = [-(-(S - c) // C) for c in range(C)]
OFF = [sum(ROWS[:c]) for c in range(C + 1)]
SP = S + 1
H0, HD0 = 8, 64
H1, HD1 = 16, 8
G0, G1 = H0 // 4, H1 // 4
SCALE0, SCALE1 = HD0 ** -0.5, HD1 ** -0.5
MASK = -1e6 * HD1 ** 0.5
CAUSAL = -1e30
EPS = 1e-5
RSQRT_SEED = float(0x5F3759DF)
HID, E = 512, 8
RANK = 16

NT = (G0 + G1) * C + G1 * 2
TILE1, TILE3 = G0 * C, (G0 + G1) * C
MXW = [402, 400, 400, 400]
MXO = [sum(MXW[:i]) for i in range(4)]
NU = (G0 + G1) * 32 + G1 * 3
UNIT1, UNIT3 = G0 * 32, (G0 + G1) * 32
NG = G0 + 2 * G1
CTX_U, QP_U, V0_U, K1_U, V1_U, UP_U, Q1_U, Q3_U, K3_U, V3_U = 0, 4, 8, 21, 37, 41, 43, 45, 47, 49
NP = 50
CTX_UNITS = [(0, 4), (4, 8), (8, 12), (12, 13)]
V1_UNITS = [(0, 2), (2, 6), (6, 10), (10, 13)]
BY_ACT = [k for k in range(NP) if V0_U <= k < K1_U or Q1_U <= k < V3_U]
BY_DVE = [k for k in range(NP) if k not in BY_ACT]
NPA, NPD = len(BY_ACT), len(BY_DVE)
MISC = (["xnT0", "shift0", "shift1", "norm0", "norm1", "wo0", "xnT1", "ffn", "xnT2"]
        + ["shift2", "shift3", "norm2", "shift4", "norm3", "shift5", "norm4", "norm5", "wo1", "xnT3"]
        + ["shift6", "shift7", "shift8", "shift9", "norm6", "norm7", "norm8", "norm9", "wo3", "xnT4", "router"])
NM = len(MISC)
M = {name: i for i, name in enumerate(MISC)}
NX = 5
NHI = 4 + 4 + 16
ND = 135
TT, NTT = 512, B * T // 512


def units_at(t):
    return range(min(32, 32 * t // 12), min(32, 32 * (t + 1) // 12))


NSETUP, S_LR, S_FC, S_PR, NPOOL = 60, 3, 49, 58, 22


def build(nc, a, out):
    ctx = ExitStack()
    with ctx:
        def sb(name, shape, dt=F32):
            return ctx.enter_context(nc.sbuf_tensor(name, shape, dt))

        def sem(name):
            return ctx.enter_context(nc.semaphore(name))

        x_keep = nc.dram_tensor("x_keep", [B, 128, QT * D], F32).ap()
        h_keep = nc.dram_tensor("h_keep", [B, D, T], F32).ap()

        ident = sb("ident", [128, 128])
        ident_bf = sb("ident_bf", [128, 128], BF16)
        ones = sb("ones", [128, 64])
        ones_bf = sb("ones_bf", [128, 128], BF16)
        spread = sb("spread", [128, 128])
        mask_k = sb("mask_k", [128, 256], BF16)
        mask_q = sb("mask_q", [128, 256], BF16)
        key_id = sb("key_id", [1, SP], F16)
        lens_i = sb("lens_i", [1, B], I32)
        lens = sb("lens", [1, B])
        aug_w = sb("aug_w", [128, 128], BF16)
        aug_x = sb("aug_x", [128, SP], BF16)
        slot_c = sb("slot_c", [128, 2 + 3 * G1])
        low_q, low_k = slot_c[:, 0:1], slot_c[:, 1:2]
        bias_q1, bias_q3, bias_k3 = (slot_c[:, 2 + i * G1:2 + (i + 1) * G1] for i in range(3))
        rows = sb("rows", [128, 7 * 128 + E])
        bo, bv, bp, g1, b1, g2, b2 = (rows[:, i * 128:(i + 1) * 128] for i in range(7))
        gate_b = rows[:, 7 * 128:7 * 128 + E]
        m_qk = sb("m_qk", [128, H0, 128])
        wv0 = sb("wv0", [128, 2, 512], F32R)
        wk1 = sb("wk1", [128, 2, G1 * 128], F32R)
        wv1 = sb("wv1", [128, 2, 128], F32R)
        wq1 = sb("wq1", [128, G1 * 128])
        wo0 = sb("wo0", [128, 4, 128])
        wo1 = sb("wo1", [128, G1, 128])
        wfc = sb("wfc", [128, HID])
        wpr = sb("wpr", [128, 4, 128])
        wq3 = sb("wq3", [128, G1 * 128])
        wk3 = sb("wk3", [128, G1 * 128])
        wv3 = sb("wv3", [128, 128])
        wp3 = sb("wp3", [128, G1, 128])
        gate_w = sb("gate_w", [128, E])
        expert_id = sb("expert_id", [128, E])

        w_all = sb("w_all", [128, B * QT, E])

        layers = ctx.enter_context(ExitStack())

        def sb(name, shape, dt=F32):
            return layers.enter_context(nc.sbuf_tensor(name, shape, dt))

        ctx_raw = sb("ctx_raw", [128, C, 128])
        ctx_hi = sb("ctx_hi", [128, SP], F32R)
        ctx_lo = sb("ctx_lo", [128, SP], F32R)
        q0_hi = sb("q0_hi", [128, H0, T], F32R)
        q0_lo = sb("q0_lo", [128, H0, T], F32R)
        q1 = sb("q1", [128, G1, 4, T], F32R)
        k1 = sb("k1", [128, G1, SP], F32R)
        k3 = ctx_lo[:, 0:G1 * T].rearrange("p (g t) -> p g t", g=G1)
        v0 = sb("v0", [128, C, 512])
        v1 = sb("v1", [128, C, H1, 32])
        v3 = sb("v3", [128, 2, H1, 32])
        probs = sb("probs", [128, 2, 4 * T])
        prob_sum = sb("prob_sum", [128, 2, 4 * T])
        neg_shift = sb("neg_shift", [128, 4, T], BF16)
        mpart = sb("mpart", [128, 8, 4])
        mx0 = sb("mx0", [128, QT, 32])
        mx1 = sb("mx1", [128, QT, 128])
        av_sb = sb("av_sb", [128, 2, T])
        rden = sb("rden", [128, 2, T])
        att = sb("att", [128, 4, T])
        x_in = sb("x_in", [128, QT, D])
        x_bo = sb("x_bo", [128, QT, D])
        xr = sb("xr", [128, QT, D])
        xn = rden[:, 0, :].rearrange("p (q d) -> p q d", q=QT)
        xnT = sb("xnT", [128, T])
        xb = prob_sum[:, :, :].rearrange("p w (g t) -> p w g t", g=G1)
        hi_tmp = att[:, :, :].bitcast(F32R)
        relu = xb[:, 0, :, :]
        relu2 = xb[:, 1, :, :]
        stats = sb("stats", [128, QT, 6])
        mv = sb("mv", [128, QT, 2])
        veps = sb("veps", [128, QT])
        rs = sb("rs", [128, QT])
        rt = sb("rt", [128, QT])
        logit = sb("logit", [128, QT, E])
        top = sb("top", [128, QT, 8])
        top_i = sb("top_i", [128, QT, 8], U32)
        top_f = sb("top_f", [128, QT, 8])
        gap = sb("gap", [128, QT])
        wgt = sb("wgt", [128, QT, 2])
        sel = sb("sel", [128, QT, 2, E])
        st = layers.enter_context(nc.psum_tensor("st", [128, 4, 512], F32))
        mx = layers.enter_context(nc.psum_tensor("mx", [128, 2, 512], F32))
        av = layers.enter_context(nc.psum_tensor("av", [128, 512], F32))
        misc = layers.enter_context(nc.psum_tensor("misc", [128, 512], F32))

        w_loaded = sem("w_loaded")
        ctx_loaded = sem("ctx_loaded")
        x_loaded = sem("x_loaded")
        setup_mm = sem("setup_mm")
        setup_dve = sem("setup_dve")
        setup_pool = sem("setup_pool")
        pj_ready = sem("pj_ready")
        pj_used_act = sem("pj_used_act")
        pj_used_dve = sem("pj_used_dve")
        hi_ready = sem("hi_ready")
        misc_ready = sem("misc_ready")
        misc_used = sem("misc_used")
        xn_ready = sem("xn_ready")
        aug_ready = sem("aug_ready")
        relu_ready = sem("relu_ready")
        q_ready = sem("q_ready")
        mx_ready = sem("mx_ready")
        mx_used = sem("mx_used")
        negmax_ready = sem("negmax_ready")
        shift_ready = sem("shift_ready")
        st_ready = sem("st_ready")
        p_ready = sem("p_ready")
        av_done = sem("av_done")
        sum_done = sem("sum_done")
        av_copied = sem("av_copied")
        att_ready = sem("att_ready")
        xbo_ready = sem("xbo_ready")
        x4_ready = sem("x4_ready")
        kept = sem("kept")
        gap_exp = sem("gap_exp")
        gap_ready = sem("gap_ready")
        chain = sem("chain")
        idle = sem("idle")

        block = layers.enter_context(nc.Block())

        ctx_v = a["ctx"]

        def load_ctx(e, b):
            full = ROWS[-1]
            e.dma_start(ctx_raw[0:full, :, :], ctx_v[b, 0:full * C, :].rearrange("(p c) d -> p c d", c=C)).then_inc(ctx_loaded, 16)
            e.dma_start(ctx_raw[full:full + 1, 0:S - full * C, :],
                        ctx_v[b, full * C:S, :].unsqueeze(0)).then_inc(ctx_loaded, 16)

        stage = v0[:, :, :].rearrange("p c n -> p (c n)")
        raw = {}
        at = 0
        for name, width in (("wqT0", 512), ("wkT0", 512), ("wv0", 512), ("wk1", 512), ("wv1", 128),
                            ("wfc", 512), ("wproj", 512), ("uT", 512), ("fastT", RANK), ("v", 128), ("gate", 1), ("aug_w", 128)):
            raw[name] = stage[:, at:at + width]
            at += width
        stage1 = v1[:, :, :, :].rearrange("p c h n -> p (c h n)")
        pT0 = stage1[:, 0:512]
        t_a, t_b, t_c = (stage1[:, 512 * i:512 * (i + 1)] for i in range(1, 4))
        low_rank = stage1[:, 2048:2176]

        LOADS = [
            (raw["wqT0"].rearrange("p (a d) -> p a d", a=4), a["wqT0"].rearrange("(a p) d -> p a d", p=128)),
            (raw["wkT0"].rearrange("p (a d) -> p a d", a=4), a["wkT0"].rearrange("(a p) d -> p a d", p=128)),
            (raw["wv0"], a["wv0"]), (raw["wk1"], a["wk1"]), (raw["wv1"], a["wv1"]),
            (raw["wfc"].rearrange("p (a d) -> p a d", a=4), a["wfc"].rearrange("(a p) d -> p a d", p=128)),
            (raw["wproj"], a["wproj"]), (raw["uT"][0:RANK, :], a["uT"]), (raw["fastT"][0:RANK, :], a["fastT"]),
            (raw["v"][0:RANK, :], a["v"]), (raw["gate"], a["gate"]),
            (wo0[:, :, :], a["wo0"].rearrange("(a p) d -> p a d", p=128)),
            (wq1[:, :], a["wq1"]), (wo1[:, :, :], a["wo1"].rearrange("g p d -> p g d")),
            (wq3[:, :], a["wq3"]), (wk3[:, :], a["wk3"]), (wv3[:, :], a["wv3"]),
            (wp3[:, :, :], a["wp3"].rearrange("g p d -> p g d")), (gate_w[:, :], a["gate_w"]),
            (rows[:, :], a["rows"]), (slot_c[:, :], a["slot_c"]), (raw["aug_w"], a["aug_w"]), (lens_i[:, :], a["lens"]),
        ]
        W_ALL = 16 * len(LOADS)

        @block.sync
        def _(e):
            for dst, src in LOADS:
                e.dma_start(dst, src).then_inc(w_loaded, 16)
            load_ctx(e, 0)
            e.dma_start(x_in[:, :, :], a["x"][0].rearrange("(q p) d -> p q d", p=128)).then_inc(x_loaded, 16)
            with e.Fori(0, B - 1) as b:
                e.wait_ge(pj_ready, b * NP + QP_U)
                load_ctx(e, b + 1)
                e.wait_ge(misc_used, b * NM + M["wo0"] + 1)
                e.dma_start(x_in[:, :, :], a["x"][b + 1].rearrange("(q p) d -> p q d", p=128)).then_inc(x_loaded, 16)

        @block.gpsimd
        def _(e):
            def step(ins):
                ins.then_inc(setup_pool, 1)
                step.n += 1
                e.wait_ge(setup_pool, step.n)
            step.n = 0
            step(e.memset(ident[:, :], 0.0))
            step(e.affine_select(out=ident[:, :], in_=ident[:, :], compare_op=ALU.not_equal, fill=1.0, base=0,
                                 pattern=[[-1, 128]], channel_multiplier=1))
            step(e.memset(spread[:, :], 0.0))
            sv = spread[:, :].rearrange("p (j r) -> p j r", j=4)
            step(e.affine_select(out=sv, in_=sv, compare_op=ALU.not_equal, fill=1.0, base=-HD1,
                                 pattern=[[-32, 4], [0, 32]], channel_multiplier=1))
            step(e.memset(mask_k[:, :], 0.0))
            step(e.affine_select(out=mask_k[:, 0:128], in_=mask_k[:, 0:128], compare_op=ALU.is_ge, fill=CAUSAL,
                                 base=0, pattern=[[1, 128]], channel_multiplier=-1))
            step(e.memset(mask_q[:, :], 0.0))
            step(e.affine_select(out=mask_q[:, 128:256], in_=mask_q[:, 128:256], compare_op=ALU.is_ge, fill=CAUSAL,
                                 base=0, pattern=[[-1, 128]], channel_multiplier=1))
            two = ROWS[0] * 2
            step(e.iota(key_id[:, 0:two], [[1, 2], [C, ROWS[0]]], base=0, channel_multiplier=0,
                        allow_small_or_imprecise_dtypes=True))
            step(e.iota(key_id[:, two:S], [[1, C - 2], [C, ROWS[-1]]], base=2, channel_multiplier=0,
                        allow_small_or_imprecise_dtypes=True))
            step(e.iota(key_id[:, S:SP], [[1, 1]], base=(ROWS[-1] - 1) * C + C - 1, channel_multiplier=0,
                        allow_small_or_imprecise_dtypes=True))
            step(e.iota(expert_id[:, :], [[1, E]], base=0, channel_multiplier=0, allow_small_or_imprecise_dtypes=True))
            step(e.memset(ones[:, :], 1.0))
            step(e.memset(ones_bf[:, :], 1.0))
            step(e.memset(aug_x[:, :], 0.0))
            step(e.memset(aug_x[32:33, :], 1.0))
            step(e.memset(neg_shift[:, :, :], 0.0))
            step(e.memset(mx0[:, :, :], 0.0))
            step(e.memset(mx1[:, :, :], 0.0))
            step(e.memset(v3[:, :, :, :], 0.0))
            step(e.memset(v3[:, :, :, HD1:HD1 + 1], 1.0))
            step(e.memset(q1[:, :, :, :].bitcast(F32), 0.0))
            assert step.n == NPOOL
            e.wait_ge(setup_dve, NSETUP)
            step(e.memset(v1[:, :, :, :], 0.0))
            step(e.memset(v1[:, :, :, HD1:HD1 + 1], 1.0))
            with e.Fori(0, B) as b:
                e.wait_ge(x_loaded, b * 16 + 16)
                e.wait_ge(misc_used, b * NM)
                e.tensor_tensor(x_bo[:, :, :], x_in[:, :, :], bo.unsqueeze(1).broadcast_to([128, QT, D]),
                                ALU.add).then_inc(xbo_ready, 1)
                for g in range(G0):
                    for c in range(C):
                        i = g * C + c
                        n = ROWS[c]
                        e.wait_ge(p_ready, b * NT + i + 1)
                        if c == 0:
                            e.sem_inc(idle, 1)
                            e.tensor_copy(prob_sum[0:n, g, :], probs[0:n, i % 2, :]).then_inc(sum_done, 1)
                        else:
                            e.wait_ge(sum_done, b * TILE1 + i)
                            e.tensor_tensor(prob_sum[0:n, g, :], prob_sum[0:n, g, :], probs[0:n, i % 2, :],
                                            ALU.add).then_inc(sum_done, 1)

        @block.tensor
        def _(e):
            mm = e.matmul
            e.wait_ge(w_loaded, W_ALL)
            e.wait_ge(setup_pool, NPOOL)
            for h in range(H0):
                r, p = 64 * (h % 2), h // 2
                ins = mm(st[:, 2 * (h % 2) + h // 4, (p % 2) * 128:(p % 2) * 128 + 128],
                         raw["wqT0"][r:r + 64, p * 128:(p + 1) * 128], raw["wkT0"][r:r + 64, p * 128:(p + 1) * 128],
                         start=True, stop=True)
            ins.then_inc(setup_mm, 1)
            mm(misc[0:RANK, 0:128], raw["fastT"][0:RANK, :], raw["v"][0:RANK, :], start=True, stop=True).then_inc(setup_mm, 1)
            e.wait_ge(setup_dve, S_LR)
            for k in range(4):
                ins = mm(mx[:, 0, k * 128:(k + 1) * 128], raw["uT"][0:RANK, k * 128:(k + 1) * 128],
                         low_rank[0:RANK, :], start=True, stop=True)
            ins.then_inc(setup_mm, 1)
            e.wait_ge(setup_dve, S_FC)
            for k in range(4):
                ins = e.transpose(av[:, k * 128:(k + 1) * 128], t_a[:, k * 128:(k + 1) * 128], ident[:, :])
            ins.then_inc(setup_mm, 1)
            e.wait_ge(setup_dve, S_PR)
            for k in range(4):
                ins = e.transpose(mx[:, 1, k * 128:(k + 1) * 128], t_b[:, k * 128:(k + 1) * 128], ident[:, :])
            ins.then_inc(setup_mm, 1)
            e.wait_ge(setup_dve, NSETUP)
            e.wait_ge(setup_pool, NPOOL + 2)

            with e.Fori(0, B) as b:
                def misc_free(name):
                    e.wait_ge(misc_used, b * NM + M[name])

                def bank_free(k):
                    if k - 4 in BY_ACT:
                        e.wait_ge(pj_used_act, b * NPA + BY_ACT.index(k - 4) + 1)
                    else:
                        e.wait_ge(pj_used_dve, b * NPD + BY_DVE.index(k - 4) + 1)

                def units_done(k):
                    e.wait_ge(pj_used_act, b * NPA + sum(u < k for u in BY_ACT))
                    e.wait_ge(pj_used_dve, b * NPD + sum(u < k for u in BY_DVE))

                def transpose_xn(n, name):
                    e.wait_ge(xn_ready, b * NX + n + 1)
                    misc_free(name)
                    for q in range(QT):
                        ins = e.transpose(misc[:, q * 128:(q + 1) * 128], xn[:, q, :], ident[:, :])
                    ins.then_inc(misc_ready, 1)

                def max_unit(base, layer, g, n):
                    i = base + g * 32 + n
                    hq, u = n // 4, n % 4
                    h, q = hq // QT, hq % QT
                    cols = slice(MXO[u], MXO[u] + MXW[u])
                    e.wait_ge(mx_used, b * NU + max(i - 1, 0))
                    if layer == 0:
                        w, m = q0_hi[:, 4 * g + h, q * 128:(q + 1) * 128], ctx_hi[:, cols]
                    else:
                        w, m = q1[:, g, h, q * 128:(q + 1) * 128], k1[:, g, cols]
                    mm(mx[:, i % 2, 0:MXW[u]], w, m, start=True, stop=True).then_inc(mx_ready, 1)

                def shift_t(gg):
                    e.wait_ge(negmax_ready, b * NG + gg + 1)
                    misc_free(f"shift{gg}")
                    for q in range(QT):
                        if gg < G0:
                            ins = e.transpose(misc[0:32, q * 128:(q + 1) * 128], mx0[:, q, :], ident[:, :])
                        else:
                            ins = e.transpose(misc[:, q * 128:(q + 1) * 128], mx1[:, q, :], ident[:, :])
                    ins.then_inc(misc_ready, 1)

                def values(i):
                    if i < TILE1:
                        g, c = divmod(i, C)
                        gg = g
                    elif i < TILE3:
                        g, c = divmod(i - TILE1, C)
                        gg = G0 + g
                    else:
                        g, c = divmod(i - TILE3, 2)
                        gg = G0 + G1 + g
                    e.wait_ge(p_ready, b * NT + i + 1)
                    if c == 0:
                        e.wait_ge(av_copied, b * NG + gg)
                    pr = probs[:, i % 2, :]
                    for j in range(4):
                        if i < TILE1:
                            n = ROWS[c]
                            h = 4 * g + j
                            ins = mm(av[64 * (j % 2):64 * (j % 2) + 64, (j // 2) * T:(j // 2 + 1) * T],
                                     v0[0:n, c, h * HD0:(h + 1) * HD0], pr[0:n, j * T:(j + 1) * T],
                                     start=(c == 0 and j < 2), stop=(c == C - 1), skip_group_check=True)
                        elif i < TILE3:
                            n = ROWS[c]
                            ins = mm(av[32 * j:32 * j + 32, 0:T], v1[0:n, c, 4 * g + j, :], pr[0:n, j * T:(j + 1) * T],
                                     start=(c == 0), stop=(c == C - 1), tile_position=(0, 32 * j), skip_group_check=True)
                        elif c == 0:
                            ins = mm(av[32 * j:32 * j + 32, 0:T], v3[:, 0, 4 * g + j, :], pr[:, j * T:(j + 1) * T],
                                     start=True, stop=False, tile_position=(0, 32 * j), skip_group_check=True)
                        else:
                            ins = mm(av[32 * j:32 * j + 32, 128:T], v3[:, 1, 4 * g + j, :], pr[:, j * 128:(j + 1) * 128],
                                     start=False, stop=True, tile_position=(0, 32 * j), skip_group_check=True)
                    ins.then_inc(av_done, 1)

                def norm(gg):
                    misc_free(f"norm{gg}")
                    if gg < G0:
                        e.wait_ge(sum_done, b * TILE1 + (gg + 1) * C)
                        for j in range(4):
                            n = ROWS[0]
                            ins = mm(misc[64 * (j % 2):64 * (j % 2) + 64, (j // 2) * T:(j // 2 + 1) * T],
                                     ones[0:n, :], prob_sum[0:n, gg, j * T:(j + 1) * T],
                                     start=True, stop=True, skip_group_check=True)
                    else:
                        e.wait_ge(av_copied, b * NG + gg + 1)
                        ins = mm(misc[:, 0:T], spread[:, :], av_sb[:, 0, :], start=True, stop=True)
                    ins.then_inc(misc_ready, 1)

                def scores(i, layer, g, c):
                    k = i % 2
                    e.wait_ge(p_ready, b * NT + max(i - 1, 0))
                    if layer == 0:
                        n = ROWS[c]
                        keys = slice(OFF[c], OFF[c] + n)
                        for half in range(2):
                            o = st[0:n, 2 * k + half, :]
                            hs = slice(4 * g + 2 * half, 4 * g + 2 * half + 2)
                            mm(o, ctx_hi[:, keys], q0_hi[:, hs, :], start=True, stop=False)
                            mm(o, ctx_hi[:, keys], q0_lo[:, hs, :], start=False, stop=False)
                            mm(o, ctx_lo[:, keys], q0_hi[:, hs, :], start=False, stop=False)
                            ins = mm(o, ones_bf[:, 0:n], neg_shift[:, 2 * half:2 * half + 2, :], start=False, stop=True)
                    elif layer == 1:
                        n = ROWS[c]
                        for half in range(2):
                            ins = mm(st[0:n, 2 * k + half, :], k1[:, g, OFF[c]:OFF[c] + n],
                                     q1[:, g, 2 * half:2 * half + 2, :], start=True, stop=True)
                    elif c == 0:
                        for half in range(2):
                            o = st[:, 2 * k + half, :]
                            mm(o, ident_bf[:, :], mask_k[:, :].unsqueeze(1).broadcast_to([128, 2, T]), start=True, stop=False)
                            ins = mm(o, k3[:, g, 0:128], q1[:, g, 2 * half:2 * half + 2, :], start=False, stop=True)
                    else:
                        o = st[:, 2 * k, :]
                        mm(o, ident_bf[:, :], mask_k[:, 0:128].unsqueeze(1).broadcast_to([128, 4, 128]), start=True, stop=False)
                        ins = mm(o, k3[:, g, 128:256], q1[:, g, :, 128:256], start=False, stop=True)
                    ins.then_inc(st_ready, 1)

                def attention(layer, groups, tile0, group0, unit0):
                    behind = None
                    for g in range(groups):
                        for c in range(C):
                            i = tile0 + g * C + c
                            if c == 0:
                                e.wait_ge(shift_ready, b * NG + group0 + g + 1)
                            scores(i, layer, g, c)
                            if c == 1 and g > 0:
                                norm(group0 + g - 1)
                            if g + 1 < groups:
                                for n in units_at(c):
                                    max_unit(unit0, layer, g + 1, n)
                            if behind is not None:
                                values(behind)
                            behind = i
                        if g + 1 < groups:
                            shift_t(group0 + g + 1)
                        values(behind)
                        behind = None
                    norm(group0 + groups - 1)

                e.wait_ge(ctx_loaded, b * 32 + 32)
                e.wait_ge(p_ready, b * NT)
                for k, (c0, c1) in enumerate(CTX_UNITS):
                    for c in range(c0, c1):
                        n = ROWS[c]
                        ins = e.transpose(st[:, k, OFF[c] - OFF[c0]:OFF[c] - OFF[c0] + n], ctx_raw[0:n, c, :], ident[0:n, 0:n])
                    ins.then_inc(pj_ready, 1)
                transpose_xn(0, "xnT0")
                e.wait_ge(misc_used, b * NM + M["xnT0"] + 1)
                for k in range(4):
                    bank_free(QP_U + k)
                    for h in (2 * k, 2 * k + 1):
                        ins = mm(st[:, k, (h % 2) * T:(h % 2 + 1) * T], m_qk[:, h, :], xnT[:, :], start=True, stop=True)
                    ins.then_inc(pj_ready, 1)
                e.wait_ge(aug_ready, b + 1)
                e.wait_ge(hi_ready, b * NHI + 8)
                for k in range(V0_U, UP_U):
                    bank_free(k)
                    o = st[:, k % 4, :]
                    if k < K1_U:
                        c = k - V0_U
                        n, keys = ROWS[c], slice(OFF[c], OFF[c + 1])
                        mm(o[0:n, :], ctx_hi[:, keys], wv0[:, 0, :], start=True, stop=False)
                        mm(o[0:n, :], ctx_hi[:, keys], wv0[:, 1, :], start=False, stop=False)
                        ins = mm(o[0:n, :], ctx_lo[:, keys], wv0[:, 0, :], start=False, stop=True)
                    elif k < V1_U:
                        g, u = divmod(k - K1_U, 4)
                        cols = slice(MXO[u], MXO[u] + MXW[u])
                        w = slice(g * 128, (g + 1) * 128)
                        mm(o[:, 0:MXW[u]], wk1[:, 0, w], ctx_hi[:, cols], start=True, stop=False)
                        mm(o[:, 0:MXW[u]], wk1[:, 0, w], ctx_lo[:, cols], start=False, stop=False)
                        mm(o[:, 0:MXW[u]], wk1[:, 1, w], ctx_hi[:, cols], start=False, stop=False)
                        ins = mm(o[:, 0:MXW[u]], aug_w[:, :], aug_x[:, cols], start=False, stop=True)
                    else:
                        c0, c1 = V1_UNITS[k - V1_U]
                        for c in range(c0, c1):
                            n, keys = ROWS[c], slice(OFF[c], OFF[c + 1])
                            oc = o[0:n, (c - c0) * 128:(c - c0 + 1) * 128]
                            mm(oc, ctx_hi[:, keys], wv1[:, 0, :], start=True, stop=False)
                            mm(oc, ctx_hi[:, keys], wv1[:, 1, :], start=False, stop=False)
                            ins = mm(oc, ctx_lo[:, keys], wv1[:, 0, :], start=False, stop=True)
                    ins.then_inc(pj_ready, 1)
                    if k - V0_U < 32:
                        max_unit(0, 0, 0, k - V0_U)
                shift_t(0)
                units_done(UP_U)
                attention(0, G0, 0, 0, 0)
                e.wait_ge(att_ready, b * NG + G0)
                misc_free("wo0")
                for q in range(QT):
                    for p in range(4):
                        ins = mm(misc[:, q * 128:(q + 1) * 128], att[:, p, q * 128:(q + 1) * 128], wo0[:, p, :],
                                 start=(p == 0), stop=(p == 3))
                ins.then_inc(misc_ready, 1)
                transpose_xn(1, "xnT1")
                e.wait_ge(misc_used, b * NM + M["xnT1"] + 1)
                e.wait_ge(p_ready, b * NT + TILE1)
                for k in (UP_U, UP_U + 1):
                    for j in range(2):
                        m = 2 * (k - UP_U) + j
                        ins = mm(st[:, k % 4, j * T:(j + 1) * T], wfc[:, m * 128:(m + 1) * 128], xnT[:, :], start=True, stop=True)
                    ins.then_inc(pj_ready, 1)
                e.wait_ge(pj_used_dve, b * NPD + sum(u < Q1_U for u in BY_DVE))
                misc_free("ffn")
                for q in range(QT):
                    for m in range(4):
                        ins = mm(misc[:, q * 128:(q + 1) * 128], relu2[:, m, q * 128:(q + 1) * 128], wpr[:, m, :],
                                 start=(m == 0), stop=(m == 3))
                ins.then_inc(misc_ready, 1)
                transpose_xn(2, "xnT2")
                e.wait_ge(misc_used, b * NM + M["xnT2"] + 1)
                for k in (Q1_U, Q1_U + 1):
                    for j in range(2):
                        g = 2 * (k - Q1_U) + j
                        ins = mm(st[:, k % 4, j * T:(j + 1) * T], wq1[:, g * 128:(g + 1) * 128], xnT[:, :], start=True, stop=True)
                    ins.then_inc(pj_ready, 1)
                e.wait_ge(q_ready, b * 3 + 1)
                for n in range(32):
                    max_unit(UNIT1, 1, 0, n)
                shift_t(G0)
                units_done(Q3_U)
                attention(1, G1, TILE1, G0, UNIT1)
                e.wait_ge(att_ready, b * NG + G0 + G1)
                misc_free("wo1")
                for q in range(QT):
                    for g in range(G1):
                        ins = mm(misc[:, q * 128:(q + 1) * 128], att[:, g, q * 128:(q + 1) * 128], wo1[:, g, :],
                                 start=(g == 0), stop=(g == G1 - 1))
                ins.then_inc(misc_ready, 1)
                transpose_xn(3, "xnT3")
                e.wait_ge(misc_used, b * NM + M["xnT3"] + 1)
                e.wait_ge(p_ready, b * NT + TILE3)
                for k in range(Q3_U, V3_U):
                    if k >= Q3_U + 4:
                        bank_free(k)
                    w = wq3 if k < K3_U else wk3
                    for j in range(2):
                        g = 2 * ((k - Q3_U) % 2) + j
                        ins = mm(st[:, k % 4, j * T:(j + 1) * T], w[:, g * 128:(g + 1) * 128], xnT[:, :], start=True, stop=True)
                    ins.then_inc(pj_ready, 1)
                bank_free(V3_U)
                for q in range(2):
                    ins = mm(st[:, V3_U % 4, q * 128:(q + 1) * 128], xnT[:, q * 128:(q + 1) * 128], wv3[:, :], start=True, stop=True)
                ins.then_inc(pj_ready, 1)
                e.wait_ge(q_ready, b * 3 + 3)
                for g in range(G1):
                    for n in range(3):
                        i = UNIT3 + 3 * g + n
                        e.wait_ge(mx_used, b * NU + i - 1)
                        if n == 0:
                            mm(mx[:, i % 2, :], ident_bf[:, :], mask_q[:, 128:256].unsqueeze(1).broadcast_to([128, 4, 128]),
                               start=True, stop=False, skip_group_check=True)
                            for j in range(4):
                                ins = mm(mx[:, i % 2, j * 128:(j + 1) * 128], q1[:, g, j, 0:128], k3[:, g, 0:128],
                                         start=False, stop=True, skip_group_check=True)
                        else:
                            mm(mx[:, i % 2, :], ident_bf[:, :], mask_q[:, :].unsqueeze(1).broadcast_to([128, 2, T]),
                               start=True, stop=False, skip_group_check=True)
                            for j in range(2):
                                ins = mm(mx[:, i % 2, j * T:(j + 1) * T], q1[:, g, 2 * (n - 1) + j, 128:256], k3[:, g, :],
                                         start=False, stop=True, skip_group_check=True)
                        ins.then_inc(mx_ready, 1)
                    shift_t(G0 + G1 + g)
                units_done(NP)
                behind = None
                for g in range(G1):
                    e.wait_ge(shift_ready, b * NG + G0 + G1 + g + 1)
                    for c in range(2):
                        i = TILE3 + 2 * g + c
                        scores(i, 3, g, c)
                        if behind is not None:
                            values(behind)
                            if c == 0:
                                norm(G0 + G1 + g - 1)
                        behind = i
                values(behind)
                norm(NG - 1)
                e.wait_ge(att_ready, b * NG + NG)
                misc_free("wo3")
                for q in range(QT):
                    for g in range(G1):
                        ins = mm(misc[:, q * 128:(q + 1) * 128], att[:, g, q * 128:(q + 1) * 128], wp3[:, g, :],
                                 start=(g == 0), stop=(g == G1 - 1))
                ins.then_inc(misc_ready, 1)
                transpose_xn(4, "xnT4")
                misc_free("router")
                for q in range(QT):
                    ins = mm(misc[:, q * E:(q + 1) * E], xnT[:, q * 128:(q + 1) * 128], gate_w[:, :], start=True, stop=True)
                ins.then_inc(misc_ready, 1)

        @block.scalar
        def _(e):
            with e.Fori(0, B) as b:
                def exps(i, n, width, scale):
                    e.wait_ge(st_ready, b * NT + i + 1)
                    e.wait_ge(av_done, b * NT + max(i - 1, 0))
                    if 2 <= i < TILE1:
                        e.wait_ge(sum_done, b * TILE1 + i - 1)
                    elif TILE1 <= i < TILE1 + 2:
                        e.wait_ge(sum_done, b * TILE1 + TILE1)
                    e.activation(probs[0:n, i % 2, 0:width],
                                 st[0:n, 2 * (i % 2):2 * (i % 2) + 2, :].rearrange("p a n -> p (a n)")[:, 0:width],
                                 ACT.Exp, scale=scale).then_inc(p_ready, 1)

                def copy_xnT(n):
                    e.wait_ge(misc_ready, b * NM + M[f"xnT{n}"] + 1)
                    if n == 0:
                        e.wait_ge(kept, b * 32)
                    e.copy(xnT[:, :], misc[:, 0:T]).then_inc(misc_used, 1)

                def slots(k, bias, which):
                    e.wait_ge(pj_ready, b * NP + k + 1)
                    for j in range(2):
                        g = 2 * ((k - Q1_U) % 2) + j
                        ins = e.activation(xb[:, which, g, :], st[:, k % 4, j * T:(j + 1) * T], ACT.Identity, bias=bias[:, g:g + 1])
                    ins.then_inc(pj_used_act, 1)

                for k, (c0, c1) in enumerate(CTX_UNITS):
                    e.wait_ge(pj_ready, b * NP + k + 1)
                    w = OFF[c1] - OFF[c0]
                    ins = e.copy(ctx_hi[:, OFF[c0]:OFF[c1]], st[:, k, 0:w])
                    if c1 == C:
                        ins = e.copy(ctx_hi[:, S:SP], st[:, k, w - 1:w])
                    ins.then_inc(hi_ready, 1)
                copy_xnT(0)
                for k in range(4):
                    e.wait_ge(pj_ready, b * NP + QP_U + k + 1)
                    e.copy(q0_hi[:, 2 * k:2 * k + 2, :].rearrange("p h t -> p (h t)"), st[:, k, :]).then_inc(hi_ready, 1)
                for k in range(V0_U, V1_U):
                    e.wait_ge(pj_ready, b * NP + k + 1)
                    if k < K1_U:
                        c = k - V0_U
                        e.copy(v0[0:ROWS[c], c, :], st[0:ROWS[c], k % 4, :]).then_inc(pj_used_act, 1)
                    else:
                        g, u = divmod(k - K1_U, 4)
                        e.copy(k1[:, g, MXO[u]:MXO[u] + MXW[u]], st[:, k % 4, 0:MXW[u]]).then_inc(hi_ready, 1)
                for i in range(TILE1):
                    exps(i, ROWS[i % C], 4 * T, SCALE0)
                copy_xnT(1)
                for k in range(2):
                    e.wait_ge(pj_ready, b * NP + UP_U + k + 1)
                    e.activation(relu[:, 2 * k:2 * k + 2, :].rearrange("p m t -> p (m t)"), st[:, (UP_U + k) % 4, :],
                                 ACT.Relu).then_inc(relu_ready, 1)
                copy_xnT(2)
                slots(Q1_U, bias_q1, 0)
                slots(Q1_U + 1, bias_q1, 0)
                for i in range(TILE1, TILE3):
                    exps(i, ROWS[(i - TILE1) % C], 4 * T, SCALE1)
                copy_xnT(3)
                for k in range(Q3_U, V3_U):
                    slots(k, bias_q3 if k < K3_U else bias_k3, 0 if k < K3_U else 1)
                for i in range(TILE3, NT):
                    exps(i, 128, 4 * T if i % 2 == 0 else 4 * 128, SCALE1)
                copy_xnT(4)
                e.wait_ge(misc_used, b * NM + M["xnT4"] + 1)
                e.dma_start(h_keep[b], xnT[:, :]).then_inc(kept, 16)
                e.wait_ge(x4_ready, b + 1)
                e.dma_start(x_keep[b], xr[:, :, :].rearrange("p q d -> p (q d)")).then_inc(kept, 16)
                e.wait_ge(gap_ready, b + 1)
                e.activation(gap[:, :], gap[:, :], ACT.Exp).then_inc(gap_exp, 1)

        @block.vector
        def _(e):
            def step(ins):
                ins.then_inc(setup_dve, 1)
                step.n += 1
                e.wait_ge(setup_dve, step.n)
            step.n = 0
            e.wait_ge(w_loaded, W_ALL)
            e.wait_ge(setup_pool, NPOOL)
            e.wait_ge(setup_mm, 2)
            for r in range(2):
                step(e.tensor_copy(m_qk[:, :, :].rearrange("p (a c r) d -> p a c r d", a=2, r=2)[:, :, :, r, :],
                                   st[:, 2 * r:2 * r + 2, 0:256].rearrange("p a (c d) -> p a c d", c=2)))
            step(e.tensor_scalar(low_rank[0:RANK, :], misc[0:RANK, 0:128], raw["gate"][0:RANK, :], None, ALU.mult))
            assert step.n == S_LR
            step(e.tensor_copy(ident_bf[:, :], ident[:, :]))
            step(e.tensor_copy(aug_w[:, :], raw["aug_w"]))
            step(e.tensor_copy(lens[:, :], lens_i[:, :]))
            for w, r in ((wv0, raw["wv0"]), (wk1, raw["wk1"]), (wv1, raw["wv1"])):
                step(e.tensor_copy(w[:, 0, :], r))
                step(e.tensor_tensor(w[:, 1, :], r, w[:, 0, :].bitcast(F32), ALU.subtract))

            def ternary(dst, src, scale):
                width = src.shape[-1]
                step(e.tensor_reduce(scale, src, AX.X, ALU.add, apply_absolute_value=True))
                step(e.tensor_scalar(scale, scale, 1.0 / width, 1e-5, ALU.mult, ALU.max))
                step(e.tensor_scalar(t_c[:, 8:9], scale, 0.5, None, ALU.mult))
                step(e.tensor_scalar(t_c[:, 9:10], scale, -0.5, None, ALU.mult))
                step(e.tensor_scalar(dst, src, t_c[:, 9:10], None, ALU.is_lt))
                step(e.scalar_tensor_tensor(dst, src, t_c[:, 8:9], dst, ALU.is_gt, ALU.subtract))
                step(e.tensor_tensor(dst, dst, src, ALU.subtract))
                step(e.tensor_tensor(dst, dst, src, ALU.add))
                step(e.tensor_scalar(dst, dst, scale, None, ALU.mult))

            for k in range(4):
                ternary(t_a[:, k * 128:(k + 1) * 128], raw["wfc"][:, k * 128:(k + 1) * 128], t_c[:, k:k + 1])
            e.wait_ge(setup_mm, 3)
            step(e.tensor_tensor(t_a, t_a, mx[:, 0, :], ALU.add))
            assert step.n == S_FC, step.n
            ternary(t_b, raw["wproj"], t_c[:, 4:5])
            assert step.n == S_PR, step.n
            e.wait_ge(setup_mm, 4)
            step(e.tensor_copy(wfc[:, :], av[:, :]))
            e.wait_ge(setup_mm, 5)
            step(e.tensor_copy(wpr[:, :, :].rearrange("p m d -> p (m d)"), mx[:, 1, :]))
            assert step.n == NSETUP, step.n

            with e.Fori(0, B) as b:
                def link(ins):
                    ins.then_inc(chain, 1)
                    link.n += 1
                    e.wait_ge(chain, b * ND + link.n)
                link.n = 0

                def layernorm(x, gain=None, offset=None, to=xn):
                    for q in range(QT):
                        ins = e.bn_stats(stats[:, q, :], x[:, q, :])
                    link(ins)
                    e.sem_inc(idle, 1)
                    for q in range(QT):
                        ins = e.bn_aggr(mv[:, q, :], stats[:, q, :])
                    link(ins)
                    link(e.tensor_scalar(veps[:, :], mv[:, :, 1], EPS, None, ALU.add))
                    link(e.tensor_scalar(rt[:, :].bitcast(I32), veps[:, :].bitcast(I32), 1, None, ALU.logical_shift_right))
                    link(e.tensor_scalar(rs[:, :].bitcast(I32), rt[:, :].bitcast(I32), -1.0, RSQRT_SEED, ALU.mult, ALU.add))
                    for _ in range(4):
                        link(e.scalar_tensor_tensor(rt[:, :], rs[:, :], -0.5, rs[:, :], ALU.mult, ALU.mult))
                        link(e.tensor_tensor(rt[:, :], rt[:, :], veps[:, :], ALU.mult))
                        link(e.scalar_tensor_tensor(rs[:, :], rt[:, :], 1.5, rs[:, :], ALU.add, ALU.mult))
                    for q in range(QT):
                        ins = e.tensor_scalar(to[:, q, :], x[:, q, :], mv[:, q, 0:1], rs[:, q:q + 1], ALU.subtract, ALU.mult)
                        if gain is not None or to is not xn:
                            link(ins)
                    if to is not xn:
                        return
                    if gain is not None:
                        link(e.tensor_tensor(xn[:, :, :], xn[:, :, :], gain.unsqueeze(1).broadcast_to([128, QT, D]), ALU.mult))
                        ins = e.tensor_tensor(xn[:, :, :], xn[:, :, :], offset.unsqueeze(1).broadcast_to([128, QT, D]), ALU.add)
                    ins.then_inc(xn_ready, 1)

                def max_unit(i, n):
                    e.wait_ge(mx_ready, b * NU + i + 1)
                    hq, u = divmod(n, 4)
                    e.tensor_reduce(mpart[:, hq, u:u + 1], mx[:, i % 2, 0:MXW[u]], AX.X, ALU.max).then_inc(mx_used, 1)

                def negmax(gg, i_end):
                    e.wait_ge(mx_used, b * NU + i_end)
                    if gg < G0:
                        o = mx0[:, :, 0:4].rearrange("p q h -> p h q")
                    else:
                        o = mx1[:, :, :].rearrange("p q (j s) -> p j q s", s=32)[:, :, :, 25]
                    e.tensor_reduce(o, mpart[:, :, :].rearrange("p (h q) u -> p h q u", h=4), AX.X, ALU.max,
                                    negate=True).then_inc(negmax_ready, 1)

                def shift(gg):
                    e.wait_ge(misc_ready, b * NM + M[f"shift{gg}"] + 1)
                    if gg < G0:
                        link(e.tensor_tensor(neg_shift[0:32, :, :], misc[0:32, 0:T].unsqueeze(1).broadcast_to([32, 4, T]),
                                             ident[0:32, 0:4].unsqueeze(2).broadcast_to([32, 4, T]), ALU.mult))
                    else:
                        g = (gg - G0) % G1
                        for j in range(4):
                            r = slice(32 * j, 32 * j + 32)
                            ins = e.tensor_tensor(q1[r, g, j, :], misc[r, 0:T], q1[r, g, j, :].bitcast(F32), ALU.add)
                        link(ins)
                    e.sem_inc(shift_ready, 1)
                    e.sem_inc(misc_used, 1)

                def av_copy(gg):
                    last = C * (gg + 1) if gg < G0 + G1 else TILE3 + 2 * (gg - G0 - G1 + 1)
                    e.wait_ge(av_done, b * NT + last)
                    w = 2 if gg < G0 else 1
                    e.wait_ge(att_ready, b * NG + gg)
                    e.tensor_copy(av_sb[:, 0:w, :].rearrange("p a t -> p (a t)"), av[:, 0:w * T]).then_inc(av_copied, 1)

                def norm(gg):
                    w = 2 if gg < G0 else 1
                    e.wait_ge(misc_ready, b * NM + M[f"norm{gg}"] + 1)
                    e.reciprocal(rden[:, 0:w, :].rearrange("p a t -> p (a t)"), misc[:, 0:w * T]).then_inc(misc_used, 1)
                    e.wait_ge(misc_used, b * NM + M[f"norm{gg}"] + 1)
                    e.wait_ge(av_copied, b * NG + gg + 1)
                    if gg < G0:
                        o = att[:, 2 * gg:2 * gg + 2, :]
                    else:
                        g = (gg - G0) % G1
                        o = att[:, g:g + 1, :]
                    e.tensor_tensor(o, av_sb[:, 0:w, :], rden[:, 0:w, :], ALU.mult).then_inc(att_ready, 1)

                def attention(groups, group0, unit0):
                    for g in range(groups):
                        if g + 1 < groups:
                            for c in range(C):
                                if c == 1 and g > 0:
                                    norm(group0 + g - 1)
                                for n in units_at(c):
                                    max_unit(unit0 + (g + 1) * 32 + n, n)
                            negmax(group0 + g + 1, unit0 + (g + 2) * 32)
                            shift(group0 + g + 1)
                        elif g > 0:
                            norm(group0 + g - 1)
                        av_copy(group0 + g)
                    norm(group0 + groups - 1)

                def residual(name, base):
                    e.wait_ge(misc_ready, b * NM + M[name] + 1)
                    return e.tensor_tensor(xr[:, :, :], misc[:, 0:T].rearrange("p (q d) -> p q d", q=QT), base, ALU.add)

                e.wait_ge(x_loaded, b * 16 + 16)
                layernorm(x_in)
                e.tensor_scalar(aug_x[0:1, :], key_id[:, :], lens[:, bass.ds(b, 1)], MASK, ALU.is_ge, ALU.mult).then_inc(aug_ready, 1)
                for k, (c0, c1) in enumerate(CTX_UNITS):
                    e.wait_ge(hi_ready, b * NHI + k + 1)
                    w = OFF[c1] - OFF[c0]
                    ins = e.tensor_tensor(ctx_lo[:, OFF[c0]:OFF[c1]], st[:, k, 0:w], ctx_hi[:, OFF[c0]:OFF[c1]].bitcast(F32), ALU.subtract)
                    if c1 == C:
                        ins = e.tensor_tensor(ctx_lo[:, S:SP], st[:, k, w - 1:w], ctx_hi[:, S:SP].bitcast(F32), ALU.subtract)
                    ins.then_inc(pj_used_dve, 1)
                for k in range(4):
                    e.wait_ge(hi_ready, b * NHI + 4 + k + 1)
                    e.tensor_tensor(q0_lo[:, 2 * k:2 * k + 2, :].rearrange("p h t -> p (h t)"), st[:, k, :],
                                    q0_hi[:, 2 * k:2 * k + 2, :].rearrange("p h t -> p (h t)").bitcast(F32),
                                    ALU.subtract).then_inc(pj_used_dve, 1)
                for k in range(V0_U, UP_U):
                    if K1_U <= k < V1_U:
                        g, u = divmod(k - K1_U, 4)
                        kk = k1[:, g, MXO[u]:MXO[u] + MXW[u]]
                        e.wait_ge(hi_ready, b * NHI + 8 + k - K1_U + 1)
                        e.scalar_tensor_tensor(kk, kk.bitcast(F32), low_k, st[:, k % 4, 0:MXW[u]], ALU.mult, ALU.add).then_inc(pj_used_dve, 1)
                    elif k >= V1_U:
                        c0, c1 = V1_UNITS[k - V1_U]
                        n = ROWS[c0]
                        e.wait_ge(pj_ready, b * NP + k + 1)
                        e.tensor_copy(v1[0:n, c0:c1, :, 0:HD1],
                                      st[0:n, k % 4, 0:(c1 - c0) * 128].rearrange("p (c h d) -> p c h d", h=H1, d=HD1)).then_inc(pj_used_dve, 1)
                    if k - V0_U < 32:
                        max_unit(k - V0_U, k - V0_U)
                negmax(0, 32)
                shift(0)
                attention(G0, 0, 0)
                e.wait_ge(kept, b * 32)
                e.wait_ge(xbo_ready, b + 1)
                residual("wo0", x_bo[:, :, :]).then_inc(misc_used, 1)
                e.wait_ge(misc_used, b * NM + M["wo0"] + 1)
                layernorm(xr)
                for k in range(2):
                    e.wait_ge(relu_ready, b * 2 + k + 1)
                    e.scalar_tensor_tensor(relu2[:, 2 * k:2 * k + 2, :].rearrange("p m t -> p (m t)"), st[:, (UP_U + k) % 4, :], 0.0,
                                           relu[:, 2 * k:2 * k + 2, :].rearrange("p m t -> p (m t)"), ALU.max, ALU.mult).then_inc(pj_used_dve, 1)
                residual("ffn", xr[:, :, :]).then_inc(misc_used, 1)
                e.wait_ge(misc_used, b * NM + M["ffn"] + 1)
                layernorm(xr)

                def halves(which, seen):
                    e.wait_ge(pj_used_act, b * NPA + seen)
                    link(e.tensor_copy(hi_tmp, xb[:, which, :, :]))

                def block_diagonal():
                    for j in range(4):
                        r = slice(32 * j, 32 * j + 32)
                        ins = e.scalar_tensor_tensor(q1[r, :, j, :], hi_tmp[r, :, :].bitcast(F32), low_q[r, :], xb[r, 0, :, :], ALU.mult, ALU.add)
                    ins.then_inc(q_ready, 1)

                halves(0, C + 2)
                block_diagonal()
                for n in range(32):
                    max_unit(UNIT1 + n, n)
                negmax(G0, UNIT1 + 32)
                shift(G0)
                attention(G1, G0, UNIT1)
                residual("wo1", xr[:, :, :]).then_inc(misc_used, 1)
                e.wait_ge(misc_used, b * NM + M["wo1"] + 1)
                layernorm(xr, to=x_bo)
                layernorm(x_bo, g1, b1)
                halves(0, C + 4)
                block_diagonal()
                e.wait_ge(q_ready, b * 3 + 2)
                halves(1, C + 6)
                e.scalar_tensor_tensor(k3[:, :, :], hi_tmp[:, :, :].bitcast(F32), low_k, xb[:, 1, :, :], ALU.mult, ALU.add).then_inc(q_ready, 1)
                e.wait_ge(pj_ready, b * NP + NP)
                e.tensor_tensor(v3[:, :, :, 0:HD1], st[:, V3_U % 4, 0:256].rearrange("p (c h d) -> p c h d", c=2, d=HD1),
                                bv.rearrange("p (h d) -> p h d", d=HD1).unsqueeze(1).broadcast_to([128, 2, H1, HD1]), ALU.add).then_inc(pj_used_dve, 1)
                for g in range(G1):
                    mj = mx1[:, :, :].rearrange("p q (j s) -> p q j s", s=32)
                    for n in range(3):
                        i = UNIT3 + 3 * g + n
                        e.wait_ge(mx_ready, b * NU + i + 1)
                        if n == 0:
                            e.tensor_reduce(mj[:, 0, :, 25], mx[:, i % 2, :].rearrange("p (j k) -> p j k", j=4), AX.X, ALU.max,
                                            negate=True).then_inc(mx_used, 1)
                        else:
                            e.tensor_reduce(mj[:, 1, 2 * (n - 1):2 * n, 25], mx[:, i % 2, :].rearrange("p (j k) -> p j k", j=2), AX.X, ALU.max,
                                            negate=True).then_inc(mx_used, 1)
                    e.wait_ge(mx_used, b * NU + UNIT3 + 3 * (g + 1))
                    e.sem_inc(negmax_ready, 1)
                    shift(G0 + G1 + g)
                for g in range(G1):
                    if g > 0:
                        norm(G0 + G1 + g - 1)
                    av_copy(G0 + G1 + g)
                norm(NG - 1)
                link(e.tensor_tensor(x_bo[:, :, :], x_bo[:, :, :], bp.unsqueeze(1).broadcast_to([128, QT, D]), ALU.add))
                e.wait_ge(misc_ready, b * NM + M["wo3"] + 1)
                e.tensor_tensor(x_bo[:, :, :], misc[:, 0:T].rearrange("p (q d) -> p q d", q=QT), x_bo[:, :, :], ALU.add).then_inc(misc_used, 1)
                e.wait_ge(misc_used, b * NM + M["wo3"] + 1)
                layernorm(x_bo, g2, b2)
                e.tensor_tensor(xr[:, :, :], xr[:, :, :], x_bo[:, :, :], ALU.add).then_inc(x4_ready, 1)
                e.wait_ge(misc_ready, b * NM + M["router"] + 1)
                e.tensor_tensor(logit[:, :, :], misc[:, 0:QT * E].rearrange("p (q x) -> p q x", q=QT),
                                gate_b.unsqueeze(1).broadcast_to([128, QT, E]), ALU.add).then_inc(misc_used, 1)
                e.wait_ge(misc_used, b * NM + NM)
                e.sem_inc(idle, 1)
                for q in range(QT):
                    ins = e.max(top[:, q, :], logit[:, q, :])
                link(ins)
                e.sem_inc(idle, 1)
                for q in range(QT):
                    ins = e.max_index(top_i[:, q, :], top[:, q, :], logit[:, q, :])
                link(ins)
                link(e.tensor_copy(top_f[:, :, :], top_i[:, :, :]))
                e.tensor_tensor(gap[:, :], top[:, :, 1], top[:, :, 0], ALU.subtract).then_inc(gap_ready, 1)
                e.wait_ge(gap_exp, b + 1)
                link(e.tensor_scalar(wgt[:, :, 1], gap[:, :], 1.0, None, ALU.add))
                link(e.reciprocal(wgt[:, :, 0], wgt[:, :, 1]))
                link(e.tensor_tensor(wgt[:, :, 1], wgt[:, :, 0], gap[:, :], ALU.mult))
                for q in range(QT):
                    for t in range(2):
                        link(e.tensor_scalar(sel[:, q, t, :], expert_id[:, :], top_f[:, q, t:t + 1], wgt[:, q, t:t + 1], ALU.is_equal, ALU.mult))
                link(e.tensor_tensor(w_all[:, bass.ds(b * QT, QT), :], sel[:, :, 0, :], sel[:, :, 1, :], ALU.add))
                assert link.n == ND, link.n

        layers.close()
        experts(nc, a, out, x_keep, h_keep, w_all)


def experts(nc, a, out, x_keep, h_keep, w_all):
    with ExitStack() as ctx:
        def sb(name, shape, dt=F32):
            return ctx.enter_context(nc.sbuf_tensor(name, shape, dt))

        def sem(name):
            return ctx.enter_context(nc.semaphore(name))

        KB = HID // 128
        w1 = sb("w1", [128, E, HID])
        w2 = sb("w2", [128, E, KB, 128])
        eb1 = sb("eb1", [128, E * KB])
        eb2 = sb("eb2", [128, E, 128])
        h_t = sb("h_t", [128, 2, TT])
        acc = sb("acc", [128, 2, 4, D])
        mid = sb("mid", [128, 2, KB, TT])
        up = ctx.enter_context(nc.psum_tensor("up", [128, 4, TT], F32))
        down = ctx.enter_context(nc.psum_tensor("down", [128, 2, 4, D], F32))

        bias_loaded = sem("bias_loaded")
        w1_loaded = sem("w1_loaded")
        w2_loaded = sem("w2_loaded")
        h_loaded = [sem(f"h_loaded{s}") for s in range(2)]
        acc_loaded = [sem(f"acc_loaded{s}") for s in range(2)]
        up_ready = sem("up_ready")
        mid_ready = sem("mid_ready")
        down_ready = sem("down_ready")
        down_used = sem("down_used")
        chain2 = sem("chain2")
        stored = sem("stored")
        NL = E

        with nc.Block() as block:
            @block.sync
            def _(e):
                e.dma_start(eb1[:, :], a["eb1"]).then_inc(bias_loaded, 16)
                e.dma_start(eb2[:, :, :].rearrange("p e d -> p (e d)"), a["eb2"]).then_inc(bias_loaded, 16)
                with e.Fori(0, NTT // 2) as tt:
                    for s in range(2):
                        t = tt * 2 + s
                        e.wait_ge(down_ready, tt * 2 * E)
                        e.dma_start(h_t[:, s, :].rearrange("p (b t) -> p b t", b=2),
                                    h_keep[bass.ds(t * 2, 2), :, :].rearrange("b d t -> d b t")).then_inc(h_loaded[s], 16)
                        e.wait_ge(stored, tt * 64)
                        e.dma_start(acc[:, s, :, :].rearrange("p (b q) d -> p b (q d)", b=2),
                                    x_keep[bass.ds(t * 2, 2), :, :].rearrange("b p n -> p b n")).then_inc(acc_loaded[s], 16)

            @block.gpsimd
            def _(e):
                for x in range(E):
                    e.dma_start(w2[:, x, :, :], a["w2"][x].rearrange("(k p) d -> p k d", p=128)).then_inc(w2_loaded, 16)
                with e.Fori(0, NTT // 2) as tt:
                    for s in range(2):
                        n = tt * 2 + s
                        e.wait_ge(down_used, (n + 1) * E)
                        for h in range(2):
                            e.dma_start(out[bass.ds(n * 2 + h, 1), :, :].rearrange("b (q p) d -> p (b q) d", p=128),
                                        acc[:, s, 2 * h:2 * h + 2, :]).then_inc(stored, 16)
                e.wait_ge(stored, NTT * 32)

            @block.tensor
            def _(e):
                with e.Fori(0, NTT // 2) as tt:
                    for s in range(2):
                        n = tt * 2 + s

                        def down_products(x):
                            e.wait_ge(mid_ready, (n * E + x + 1) * KB)
                            e.wait_ge(down_used, n * E + max(x - 1, 0))
                            e.wait_ge(w2_loaded, 16 * E)
                            for q in range(4):
                                for k in range(KB):
                                    ins = e.matmul(down[:, x % 2, q, :], mid[:, x % 2, k, q * 128:(q + 1) * 128], w2[:, x, k, :],
                                                   start=(k == 0), stop=(k == KB - 1))
                            ins.then_inc(down_ready, 1)

                        e.wait_ge(h_loaded[s], tt * 16 + 16)
                        for x in range(E):
                            if x == 0:
                                e.wait_ge(w1_loaded, 16 * E)
                            for k in range(KB):
                                i = x * KB + k
                                e.wait_ge(mid_ready, n * E * KB + max(i - 3, 0))
                                e.matmul(up[:, k, :], w1[:, x, k * 128:(k + 1) * 128], h_t[:, s, :],
                                         start=True, stop=True).then_inc(up_ready, 1)
                            if x > 0:
                                down_products(x - 1)
                        down_products(E - 1)

            @block.scalar
            def _(e):
                for x in range(E):
                    e.dma_start(w1[:, x, :], a["w1"][x]).then_inc(w1_loaded, 16)
                e.wait_ge(bias_loaded, 32)
                with e.Fori(0, NTT) as t:
                    for x in range(E):
                        e.wait_ge(down_ready, t * E + max(x - 1, 0))
                        for k in range(KB):
                            i = x * KB + k
                            e.wait_ge(up_ready, t * E * KB + i + 1)
                            e.activation(mid[:, x % 2, k, :], up[:, k, :], ACT.Gelu, bias=eb1[:, i:i + 1]).then_inc(mid_ready, 1)

            @block.vector
            def _(e):
                e.wait_ge(bias_loaded, 32)
                with e.Fori(0, NTT // 2) as tt:
                    for s in range(2):
                        n = tt * 2 + s

                        def weight(q, x):
                            return w_all[:, bass.ds(n * 4 + q, 1), x:x + 1].rearrange("p a b -> p (a b)")

                        e.wait_ge(acc_loaded[s], tt * 16 + 16)
                        for x in range(E):
                            for q in range(4):
                                ins = e.scalar_tensor_tensor(acc[:, s, q, :], eb2[:, x, :], weight(q, x), acc[:, s, q, :], ALU.mult, ALU.add)
                            ins.then_inc(chain2, 1)
                            e.wait_ge(chain2, n * NL + x + 1)
                        for x in range(E):
                            e.wait_ge(down_ready, n * E + x + 1)
                            e.wait_ge(down_used, n * E + x)
                            for q in range(4):
                                ins = e.scalar_tensor_tensor(acc[:, s, q, :], down[:, x % 2, q, :], weight(q, x), acc[:, s, q, :], ALU.mult, ALU.add)
                            ins.then_inc(down_used, 1)


_IN = ["x", "ctx", "lens", "wqT0", "wkT0", "wv0", "wo0", "wfc", "wproj", "uT", "fastT", "v", "gate",
       "wq1", "wk1", "wv1", "wo1", "wq3", "wk3", "wv3", "wp3", "gate_w", "rows", "slot_c", "aug_w",
       "w1", "w2", "eb1", "eb2"]


def _slots(w, places):
    w = np.asarray(w)
    o = np.zeros((w.shape[0], H1, 32), w.dtype)
    for at in places:
        o[:, :, at:at + HD1] = w.reshape(w.shape[0], H1, HD1)
    return o.reshape(w.shape[0], H1 * 32)


def kernel(**inputs):
    import concourse.bacc as bacc
    from concourse.bass_utils import run_bass_kernel_spmd

    i = {k: np.asarray(v) for k, v in inputs.items()}
    f = i["x"].dtype
    three, one = (0, HD1, 2 * HD1), (0,)

    def columns(v):
        return v.reshape(G1, 128).T

    signs = np.zeros((128, 2), f)
    const = np.zeros((128, 3 * G1), f)
    aug = np.zeros((128, 128), f)
    for j in range(4):
        signs[32 * j + HD1:32 * j + 2 * HD1, 0] = -1
        signs[32 * j + 2 * HD1:32 * j + 3 * HD1, 1] = -1
        const[32 * j + 24, 0:G1] = 1
        const[32 * j + 25, 2 * G1:] = 1
        aug[0, 32 * j + 24] = 1
        aug[32, 32 * j + 25] = 1
    biases = np.concatenate([np.zeros((128, G1), f), columns(_slots(i["L1_ffn_bq"][None], three)),
                             columns(_slots(i["L1_ffn_bk"][None], three))], axis=1)
    slot_c = np.concatenate([signs, np.where(const != 0, const, biases)], axis=1)
    every = lambda v: np.broadcast_to(v.reshape(1, -1), (128, v.size))
    rows_of_slots = lambda w: _slots(w.T, one).T.reshape(G1, 128, D)
    arrays = {
        "x": i["x"], "ctx": i["ctx_1024"], "lens": i["_lenS2"].reshape(1, B),
        "wqT0": i["L0_xattn_Wq"].T, "wkT0": i["L0_xattn_Wk"].T, "wv0": i["L0_xattn_Wv"], "wo0": i["L0_xattn_Wo"],
        "wfc": i["L0_ffn_w_fc"], "wproj": i["L0_ffn_w_proj"], "uT": i["L0_ffn_u"].T, "fastT": i["L0_ffn_fast_b"].T,
        "v": i["L0_ffn_v"], "gate": every(i["L0_ffn_gate"]),
        "wq1": _slots(i["L1_xattn_Wq"], three), "wk1": _slots(i["L1_xattn_Wk"], three), "wv1": i["L1_xattn_Wv"],
        "wo1": rows_of_slots(i["L1_xattn_Wo"]),
        "wq3": _slots(i["L1_ffn_Wq"], three), "wk3": _slots(i["L1_ffn_Wk"], three), "wv3": i["L1_ffn_Wv"],
        "wp3": rows_of_slots(i["L1_ffn_Wp"]), "gate_w": i["L1_ffn_gate_W"],
        "rows": np.concatenate([every(i[k]) for k in (
            "L0_xattn_bo", "L1_ffn_bv", "L1_ffn_bp", "L1_ffn_ln1_g", "L1_ffn_ln1_b", "L1_ffn_ln2_g", "L1_ffn_ln2_b",
            "L1_ffn_gate_b")], axis=1),
        "slot_c": slot_c, "aug_w": aug,
        "w1": i["L1_ffn_exp_W1"], "w2": i["L1_ffn_exp_W2"],
        "eb1": i["L1_ffn_exp_b1"].reshape(E * 4, 128).T, "eb2": every(i["L1_ffn_exp_b2"]),
    }
    nc = bacc.Bacc("TRN2", target_bir_lowering=False, num_devices=1)
    given, aps = {}, {}
    for name in _IN:
        v = np.ascontiguousarray(arrays[name])
        given[f"in_{name}"] = v
        aps[name] = nc.dram_tensor(f"in_{name}", v.shape, mybir.dt.from_np(v.dtype), kind="ExternalInput").ap()
    out = nc.dram_tensor("out", (B, T, D), F32, kind="ExternalOutput").ap()
    build(nc, aps, out)
    r = run_bass_kernel_spmd(nc, [given], core_ids=[0])
    return r.results[0]["out"]
```

```python
from contextlib import ExitStack

import concourse.bass as bass
import numpy as np
from concourse import mybir

F32 = mybir.dt.float32
F32R = mybir.dt.float32r
BF16 = mybir.dt.bfloat16
F16 = mybir.dt.float16
I32 = mybir.dt.int32
U32 = mybir.dt.uint32
ALU = mybir.AluOpType
ACT = mybir.ActivationFunctionType
AX = mybir.AxisListType

B, T, D, S = 16, 256, 128, 1601
QT = T // 128
C = 13
ROWS = [-(-(S - c) // C) for c in range(C)]
OFF = [sum(ROWS[:c]) for c in range(C + 1)]
SP = S + 1
H0, HD0 = 8, 64
H1, HD1 = 16, 8
G0, G1 = H0 // 4, H1 // 4
SCALE0, SCALE1 = HD0 ** -0.5, HD1 ** -0.5
MASK = -1e6 * HD1 ** 0.5
CAUSAL = -1e30
EPS = 1e-5
RSQRT_SEED = float(0x5F3759DF)
HID, E = 512, 8
RANK = 16

NT = (G0 + G1) * C + G1 * 2
TILE1, TILE3 = G0 * C, (G0 + G1) * C
MXW = [402, 400, 400, 400]
MXO = [sum(MXW[:i]) for i in range(4)]
NU = (G0 + G1) * 32 + G1 * 3
UNIT1, UNIT3 = G0 * 32, (G0 + G1) * 32
NG = G0 + 2 * G1
CTX_U, QP_U, V0_U, K1_U, V1_U, UP_U, Q1_U, Q3_U, K3_U, V3_U = 0, 4, 8, 21, 37, 41, 43, 45, 47, 49
NP = 50
CTX_UNITS = [(0, 4), (4, 8), (8, 12), (12, 13)]
V1_UNITS = [(0, 2), (2, 6), (6, 10), (10, 13)]
BY_ACT = [k for k in range(NP) if V0_U <= k < K1_U or Q1_U <= k < V3_U]
BY_DVE = [k for k in range(NP) if k not in BY_ACT]
NPA, NPD = len(BY_ACT), len(BY_DVE)
MISC = (["xnT0", "shift0", "shift1", "norm0", "norm1", "wo0", "xnT1", "ffn", "xnT2"]
        + ["shift2", "shift3", "norm2", "shift4", "norm3", "shift5", "norm4", "norm5", "wo1", "xnT3"]
        + ["shift6", "shift7", "shift8", "shift9", "norm6", "norm7", "norm8", "norm9", "wo3", "xnT4", "router"])
NM = len(MISC)
M = {name: i for i, name in enumerate(MISC)}
NX = 5
NHI = 4 + 4 + 16
ND = 117
TT, NTT = 512, B * T // 512
FREE = 1


def units_at(t):
    return range(min(32, 32 * t // 12), min(32, 32 * (t + 1) // 12))


NSETUP, S_LR, S_FC, S_PR, NPOOL = 60, 3, 49, 58, 22


def build(nc, a, out):
    ctx = ExitStack()
    with ctx:
        def sb(name, shape, dt=F32):
            return ctx.enter_context(nc.sbuf_tensor(name, shape, dt))

        def sem(name):
            return ctx.enter_context(nc.semaphore(name))

        x_keep = nc.dram_tensor("x_keep", [B, 128, QT * D], F32).ap()
        h_keep = nc.dram_tensor("h_keep", [B, D, T], F32).ap()

        ident = sb("ident", [128, 128])
        w_all = sb("w_all", [128, B * QT, E])

        layers = ctx.enter_context(ExitStack())

        def sb(name, shape, dt=F32):
            return layers.enter_context(nc.sbuf_tensor(name, shape, dt))

        ident_bf = sb("ident_bf", [128, 128], BF16)
        ones = sb("ones", [128, 64])
        ones_bf = sb("ones_bf", [128, 128], BF16)
        spread = sb("spread", [128, 128])
        mask_k = sb("mask_k", [128, 256], BF16)
        mask_q = sb("mask_q", [128, 256], BF16)
        key_id = sb("key_id", [1, SP], F16)
        lens_i = sb("lens_i", [1, B], I32)
        lens = sb("lens", [1, B])
        aug_w = sb("aug_w", [128, 128], BF16)
        aug_x = sb("aug_x", [128, SP], BF16)
        slot_c = sb("slot_c", [128, 2 + 3 * G1])
        low_q, low_k = slot_c[:, 0:1], slot_c[:, 1:2]
        bias_q1, bias_q3, bias_k3 = (slot_c[:, 2 + i * G1:2 + (i + 1) * G1] for i in range(3))
        rows = sb("rows", [128, 7 * 128 + E])
        bo, bv, bp, g1, b1, g2, b2 = (rows[:, i * 128:(i + 1) * 128] for i in range(7))
        gate_b = rows[:, 7 * 128:7 * 128 + E]
        m_qk = sb("m_qk", [128, H0, 128])
        wv0 = sb("wv0", [128, 2, 512], F32R)
        wk1 = sb("wk1", [128, 2, G1 * 128], F32R)
        wv1 = sb("wv1", [128, 2, 128], F32R)
        wq1 = sb("wq1", [128, G1 * 128])
        wo0 = sb("wo0", [128, 4, 128])
        wo1 = sb("wo1", [128, G1, 128])
        wfc = sb("wfc", [128, HID])
        wpr = sb("wpr", [128, 4, 128])
        wq3 = sb("wq3", [128, G1 * 128])
        wk3 = sb("wk3", [128, G1 * 128])
        wv3 = sb("wv3", [128, 128])
        wp3 = sb("wp3", [128, G1, 128])
        gate_w = sb("gate_w", [128, E])
        expert_id = sb("expert_id", [128, E])

        ctx_raw = sb("ctx_raw", [128, C, 128])
        ctx_hi = sb("ctx_hi", [128, SP], F32R)
        ctx_lo = sb("ctx_lo", [128, SP], F32R)
        q0_hi = sb("q0_hi", [128, H0, T], F32R)
        q0_lo = sb("q0_lo", [128, H0, T], F32R)
        q1 = sb("q1", [128, G1, 4, T], F32R)
        k1 = sb("k1", [128, G1, SP], F32R)
        k3 = ctx_lo[:, 0:G1 * T].rearrange("p (g t) -> p g t", g=G1)
        v0 = sb("v0", [128, C, 512])
        v1 = sb("v1", [128, C, H1, 32])
        v3 = sb("v3", [128, 2, H1, 32])
        probs = sb("probs", [128, 2, 4 * T])
        prob_sum = sb("prob_sum", [128, 2, 4 * T])
        neg_shift = sb("neg_shift", [128, 4, T], BF16)
        mpart = sb("mpart", [128, 8, 4])
        mx0 = sb("mx0", [128, QT, 32])
        mx1 = sb("mx1", [128, QT, 128])
        av_sb = sb("av_sb", [128, 2, T])
        rden = sb("rden", [128, 2, T])
        att = sb("att", [128, 4, T])
        x_in = sb("x_in", [128, QT, D])
        x_bo = sb("x_bo", [128, QT, D])
        xr = sb("xr", [128, QT, D])
        xn = rden[:, 0, :].rearrange("p (q d) -> p q d", q=QT)
        xnT = sb("xnT", [128, T])
        xb = prob_sum[:, :, :].rearrange("p w (g t) -> p w g t", g=G1)
        hi_tmp = att[:, :, :].bitcast(F32R)
        relu = xb[:, 0, :, :]
        relu2 = xb[:, 1, :, :]
        stats = sb("stats", [128, QT, 6])
        mv = sb("mv", [128, QT, 2])
        veps = sb("veps", [128, QT])
        rs = sb("rs", [128, QT])
        rt = sb("rt", [128, QT])
        logit = sb("logit", [128, QT, E])
        top = sb("top", [128, QT, 8])
        top_i = sb("top_i", [128, QT, 8], U32)
        top_f = sb("top_f", [128, QT, 8])
        gap = sb("gap", [128, QT])
        wgt = sb("wgt", [128, QT, 2])
        sel = sb("sel", [128, QT, 2, E])
        st = layers.enter_context(nc.psum_tensor("st", [128, 4, 512], F32))
        mx = layers.enter_context(nc.psum_tensor("mx", [128, 2, 512], F32))
        av = layers.enter_context(nc.psum_tensor("av", [128, 512], F32))
        misc = layers.enter_context(nc.psum_tensor("misc", [128, 512], F32))

        w_loaded = sem("w_loaded")
        ctx_loaded = sem("ctx_loaded")
        x_loaded = sem("x_loaded")
        setup_mm = sem("setup_mm")
        setup_dve = sem("setup_dve")
        setup_pool = sem("setup_pool")
        pj_ready = sem("pj_ready")
        pj_used_act = sem("pj_used_act")
        pj_used_dve = sem("pj_used_dve")
        hi_ready = sem("hi_ready")
        misc_ready = sem("misc_ready")
        misc_used = sem("misc_used")
        xn_ready = sem("xn_ready")
        aug_ready = sem("aug_ready")
        relu_ready = sem("relu_ready")
        q_ready = sem("q_ready")
        mx_ready = sem("mx_ready")
        mx_used = sem("mx_used")
        negmax_ready = sem("negmax_ready")
        shift_ready = sem("shift_ready")
        st_ready = sem("st_ready")
        p_ready = sem("p_ready")
        av_done = sem("av_done")
        sum_done = sem("sum_done")
        av_copied = sem("av_copied")
        att_ready = sem("att_ready")
        xbo_ready = sem("xbo_ready")
        x4_ready = sem("x4_ready")
        kept = sem("kept")
        gap_exp = sem("gap_exp")
        gap_ready = sem("gap_ready")
        chain = sem("chain")
        idle = sem("idle")

        block = layers.enter_context(nc.Block())

        ctx_v = a["ctx"]

        def load_ctx(e, b):
            full = ROWS[-1]
            e.dma_start(ctx_raw[0:full, :, :], ctx_v[b, 0:full * C, :].rearrange("(p c) d -> p c d", c=C)).then_inc(ctx_loaded, 16)
            e.dma_start(ctx_raw[full:full + 1, 0:S - full * C, :],
                        ctx_v[b, full * C:S, :].unsqueeze(0)).then_inc(ctx_loaded, 16)

        stage = v0[:, :, :].rearrange("p c n -> p (c n)")
        raw = {}
        at = 0
        for name, width in (("wqT0", 512), ("wkT0", 512), ("wv0", 512), ("wk1", 512), ("wv1", 128),
                            ("wfc", 512), ("wproj", 512), ("uT", 512), ("fastT", RANK), ("v", 128), ("gate", 1), ("aug_w", 128)):
            raw[name] = stage[:, at:at + width]
            at += width
        stage1 = v1[:, :, :, :].rearrange("p c h n -> p (c h n)")
        pT0 = stage1[:, 0:512]
        t_a, t_b, t_c = (stage1[:, 512 * i:512 * (i + 1)] for i in range(1, 4))
        low_rank = stage1[:, 2048:2176]

        LOADS = [
            (raw["wqT0"].rearrange("p (a d) -> p a d", a=4), a["wqT0"].rearrange("(a p) d -> p a d", p=128)),
            (raw["wkT0"].rearrange("p (a d) -> p a d", a=4), a["wkT0"].rearrange("(a p) d -> p a d", p=128)),
            (raw["wv0"], a["wv0"]), (raw["wk1"], a["wk1"]), (raw["wv1"], a["wv1"]),
            (raw["wfc"].rearrange("p (a d) -> p a d", a=4), a["wfc"].rearrange("(a p) d -> p a d", p=128)),
            (raw["wproj"], a["wproj"]), (raw["uT"][0:RANK, :], a["uT"]), (raw["fastT"][0:RANK, :], a["fastT"]),
            (raw["v"][0:RANK, :], a["v"]), (raw["gate"], a["gate"]),
            (wo0[:, :, :], a["wo0"].rearrange("(a p) d -> p a d", p=128)),
            (wq1[:, :], a["wq1"]), (wo1[:, :, :], a["wo1"].rearrange("g p d -> p g d")),
            (wq3[:, :], a["wq3"]), (wk3[:, :], a["wk3"]), (wv3[:, :], a["wv3"]),
            (wp3[:, :, :], a["wp3"].rearrange("g p d -> p g d")), (gate_w[:, :], a["gate_w"]),
            (rows[:, :], a["rows"]), (slot_c[:, :], a["slot_c"]), (raw["aug_w"], a["aug_w"]), (lens_i[:, :], a["lens"]),
        ]
        W_ALL = 16 * len(LOADS)

        @block.sync
        def _(e):
            for dst, src in LOADS:
                e.dma_start(dst, src).then_inc(w_loaded, 16)
            load_ctx(e, 0)
            e.dma_start(x_in[:, :, :], a["x"][0].rearrange("(q p) d -> p q d", p=128)).then_inc(x_loaded, 16)
            with e.Fori(0, B - 1) as b:
                e.wait_ge(pj_ready, b * NP + QP_U)
                load_ctx(e, b + 1)
                e.wait_ge(misc_used, b * NM + M["wo0"] + 1 + FREE)
                e.dma_start(x_in[:, :, :], a["x"][b + 1].rearrange("(q p) d -> p q d", p=128)).then_inc(x_loaded, 16)

        @block.gpsimd
        def _(e):
            def step(ins):
                ins.then_inc(setup_pool, 1)
                step.n += 1
                e.wait_ge(setup_pool, step.n)
            step.n = 0
            step(e.memset(ident[:, :], 0.0))
            step(e.affine_select(out=ident[:, :], in_=ident[:, :], compare_op=ALU.not_equal, fill=1.0, base=0,
                                 pattern=[[-1, 128]], channel_multiplier=1))
            step(e.memset(spread[:, :], 0.0))
            sv = spread[:, :].rearrange("p (j r) -> p j r", j=4)
            step(e.affine_select(out=sv, in_=sv, compare_op=ALU.not_equal, fill=1.0, base=-HD1,
                                 pattern=[[-32, 4], [0, 32]], channel_multiplier=1))
            step(e.memset(mask_k[:, :], 0.0))
            step(e.affine_select(out=mask_k[:, 0:128], in_=mask_k[:, 0:128], compare_op=ALU.is_ge, fill=CAUSAL,
                                 base=0, pattern=[[1, 128]], channel_multiplier=-1))
            step(e.memset(mask_q[:, :], 0.0))
            step(e.affine_select(out=mask_q[:, 128:256], in_=mask_q[:, 128:256], compare_op=ALU.is_ge, fill=CAUSAL,
                                 base=0, pattern=[[-1, 128]], channel_multiplier=1))
            two = ROWS[0] * 2
            step(e.iota(key_id[:, 0:two], [[1, 2], [C, ROWS[0]]], base=0, channel_multiplier=0,
                        allow_small_or_imprecise_dtypes=True))
            step(e.iota(key_id[:, two:S], [[1, C - 2], [C, ROWS[-1]]], base=2, channel_multiplier=0,
                        allow_small_or_imprecise_dtypes=True))
            step(e.iota(key_id[:, S:SP], [[1, 1]], base=(ROWS[-1] - 1) * C + C - 1, channel_multiplier=0,
                        allow_small_or_imprecise_dtypes=True))
            step(e.iota(expert_id[:, :], [[1, E]], base=0, channel_multiplier=0, allow_small_or_imprecise_dtypes=True))
            step(e.memset(ones[:, :], 1.0))
            step(e.memset(ones_bf[:, :], 1.0))
            step(e.memset(aug_x[:, :], 0.0))
            step(e.memset(aug_x[32:33, :], 1.0))
            step(e.memset(neg_shift[:, :, :], 0.0))
            step(e.memset(mx0[:, :, :], 0.0))
            step(e.memset(mx1[:, :, :], 0.0))
            step(e.memset(v3[:, :, :, :], 0.0))
            step(e.memset(v3[:, :, :, HD1:HD1 + 1], 1.0))
            step(e.memset(q1[:, :, :, :].bitcast(F32), 0.0))
            assert step.n == NPOOL
            e.wait_ge(setup_dve, NSETUP)
            step(e.memset(v1[:, :, :, :], 0.0))
            step(e.memset(v1[:, :, :, HD1:HD1 + 1], 1.0))
            with e.Fori(0, B) as b:
                e.wait_ge(x_loaded, b * 16 + 16)
                e.wait_ge(misc_used, b * NM + FREE)
                e.tensor_tensor(x_bo[:, :, :], x_in[:, :, :], bo.unsqueeze(1).broadcast_to([128, QT, D]),
                                ALU.add).then_inc(xbo_ready, 1)
                for g in range(G0):
                    for c in range(C):
                        i = g * C + c
                        n = ROWS[c]
                        e.wait_ge(p_ready, b * NT + i + 1 + FREE)
                        if c == 0:
                            e.sem_inc(idle, 1)
                            e.tensor_copy(prob_sum[0:n, g, :], probs[0:n, i % 2, :]).then_inc(sum_done, 1)
                        else:
                            e.wait_ge(sum_done, b * TILE1 + i)
                            e.tensor_tensor(prob_sum[0:n, g, :], prob_sum[0:n, g, :], probs[0:n, i % 2, :],
                                            ALU.add).then_inc(sum_done, 1)

        @block.tensor
        def _(e):
            mm = e.matmul
            e.sem_inc(av_done, FREE)
            e.wait_ge(w_loaded, W_ALL)
            e.wait_ge(setup_pool, NPOOL)
            for h in range(H0):
                r, p = 64 * (h % 2), h // 2
                ins = mm(st[:, 2 * (h % 2) + h // 4, (p % 2) * 128:(p % 2) * 128 + 128],
                         raw["wqT0"][r:r + 64, p * 128:(p + 1) * 128], raw["wkT0"][r:r + 64, p * 128:(p + 1) * 128],
                         start=True, stop=True)
            ins.then_inc(setup_mm, 1)
            mm(misc[0:RANK, 0:128], raw["fastT"][0:RANK, :], raw["v"][0:RANK, :], start=True, stop=True).then_inc(setup_mm, 1)
            e.wait_ge(setup_dve, S_LR)
            for k in range(4):
                ins = mm(mx[:, 0, k * 128:(k + 1) * 128], raw["uT"][0:RANK, k * 128:(k + 1) * 128],
                         low_rank[0:RANK, :], start=True, stop=True)
            ins.then_inc(setup_mm, 1)
            e.wait_ge(setup_dve, S_FC)
            for k in range(4):
                ins = e.transpose(av[:, k * 128:(k + 1) * 128], t_a[:, k * 128:(k + 1) * 128], ident[:, :])
            ins.then_inc(setup_mm, 1)
            e.wait_ge(setup_dve, S_PR)
            for k in range(4):
                ins = e.transpose(mx[:, 1, k * 128:(k + 1) * 128], t_b[:, k * 128:(k + 1) * 128], ident[:, :])
            ins.then_inc(setup_mm, 1)
            e.wait_ge(setup_dve, NSETUP)
            e.wait_ge(setup_pool, NPOOL + 2)

            with e.Fori(0, B) as b:
                def misc_free(name):
                    e.wait_ge(misc_used, b * NM + M[name] + FREE)

                def bank_free(k):
                    if k - 4 in BY_ACT:
                        e.wait_ge(pj_used_act, b * NPA + BY_ACT.index(k - 4) + 1)
                    else:
                        e.wait_ge(pj_used_dve, b * NPD + BY_DVE.index(k - 4) + 1)

                def units_done(k):
                    e.wait_ge(pj_used_act, b * NPA + sum(u < k for u in BY_ACT))
                    e.wait_ge(pj_used_dve, b * NPD + sum(u < k for u in BY_DVE))

                def transpose_xn(n, name):
                    e.wait_ge(xn_ready, b * NX + n + 1)
                    misc_free(name)
                    for q in range(QT):
                        ins = e.transpose(misc[:, q * 128:(q + 1) * 128], xn[:, q, :], ident[:, :])
                    ins.then_inc(misc_ready, 1)

                def max_unit(base, layer, g, n):
                    i = base + g * 32 + n
                    hq, u = n // 4, n % 4
                    h, q = hq // QT, hq % QT
                    cols = slice(MXO[u], MXO[u] + MXW[u])
                    e.wait_ge(mx_used, b * NU + max(i - 1, 0) + FREE)
                    if layer == 0:
                        w, m = q0_hi[:, 4 * g + h, q * 128:(q + 1) * 128], ctx_hi[:, cols]
                    else:
                        w, m = q1[:, g, h, q * 128:(q + 1) * 128], k1[:, g, cols]
                    mm(mx[:, i % 2, 0:MXW[u]], w, m, start=True, stop=True).then_inc(mx_ready, 1)

                def shift_t(gg):
                    e.wait_ge(negmax_ready, b * NG + gg + 1)
                    misc_free(f"shift{gg}")
                    for q in range(QT):
                        if gg < G0:
                            ins = e.transpose(misc[0:32, q * 128:(q + 1) * 128], mx0[:, q, :], ident[:, :])
                        else:
                            ins = e.transpose(misc[:, q * 128:(q + 1) * 128], mx1[:, q, :], ident[:, :])
                    ins.then_inc(misc_ready, 1)

                def values(i):
                    if i < TILE1:
                        g, c = divmod(i, C)
                        gg = g
                    elif i < TILE3:
                        g, c = divmod(i - TILE1, C)
                        gg = G0 + g
                    else:
                        g, c = divmod(i - TILE3, 2)
                        gg = G0 + G1 + g
                    e.wait_ge(p_ready, b * NT + i + 1 + FREE)
                    if c == 0:
                        e.wait_ge(av_copied, b * NG + gg + FREE)
                    pr = probs[:, i % 2, :]
                    for j in range(4):
                        if i < TILE1:
                            n = ROWS[c]
                            h = 4 * g + j
                            ins = mm(av[64 * (j % 2):64 * (j % 2) + 64, (j // 2) * T:(j // 2 + 1) * T],
                                     v0[0:n, c, h * HD0:(h + 1) * HD0], pr[0:n, j * T:(j + 1) * T],
                                     start=(c == 0 and j < 2), stop=(c == C - 1), skip_group_check=True)
                        elif i < TILE3:
                            n = ROWS[c]
                            ins = mm(av[32 * j:32 * j + 32, 0:T], v1[0:n, c, 4 * g + j, :], pr[0:n, j * T:(j + 1) * T],
                                     start=(c == 0), stop=(c == C - 1), tile_position=(0, 32 * j), skip_group_check=True)
                        elif c == 0:
                            ins = mm(av[32 * j:32 * j + 32, 0:T], v3[:, 0, 4 * g + j, :], pr[:, j * T:(j + 1) * T],
                                     start=True, stop=False, tile_position=(0, 32 * j), skip_group_check=True)
                        else:
                            ins = mm(av[32 * j:32 * j + 32, 128:T], v3[:, 1, 4 * g + j, :], pr[:, j * 128:(j + 1) * 128],
                                     start=False, stop=True, tile_position=(0, 32 * j), skip_group_check=True)
                    ins.then_inc(av_done, 1)

                def norm(gg):
                    misc_free(f"norm{gg}")
                    if gg < G0:
                        e.wait_ge(sum_done, b * TILE1 + (gg + 1) * C)
                        for j in range(4):
                            n = ROWS[0]
                            ins = mm(misc[64 * (j % 2):64 * (j % 2) + 64, (j // 2) * T:(j // 2 + 1) * T],
                                     ones[0:n, :], prob_sum[0:n, gg, j * T:(j + 1) * T],
                                     start=True, stop=True, skip_group_check=True)
                    else:
                        e.wait_ge(av_copied, b * NG + gg + 1 + FREE)
                        ins = mm(misc[:, 0:T], spread[:, :], av_sb[:, 0, :], start=True, stop=True)
                    ins.then_inc(misc_ready, 1)

                def scores(i, layer, g, c):
                    k = i % 2
                    e.wait_ge(p_ready, b * NT + max(i - 1, 0) + FREE)
                    if layer == 0:
                        n = ROWS[c]
                        keys = slice(OFF[c], OFF[c] + n)
                        for half in range(2):
                            o = st[0:n, 2 * k + half, :]
                            hs = slice(4 * g + 2 * half, 4 * g + 2 * half + 2)
                            mm(o, ctx_hi[:, keys], q0_hi[:, hs, :], start=True, stop=False)
                            mm(o, ctx_hi[:, keys], q0_lo[:, hs, :], start=False, stop=False)
                            mm(o, ctx_lo[:, keys], q0_hi[:, hs, :], start=False, stop=False)
                            ins = mm(o, ones_bf[:, 0:n], neg_shift[:, 2 * half:2 * half + 2, :], start=False, stop=True)
                    elif layer == 1:
                        n = ROWS[c]
                        for half in range(2):
                            ins = mm(st[0:n, 2 * k + half, :], k1[:, g, OFF[c]:OFF[c] + n],
                                     q1[:, g, 2 * half:2 * half + 2, :], start=True, stop=True)
                    elif c == 0:
                        for half in range(2):
                            o = st[:, 2 * k + half, :]
                            mm(o, ident_bf[:, :], mask_k[:, :].unsqueeze(1).broadcast_to([128, 2, T]), start=True, stop=False)
                            ins = mm(o, k3[:, g, 0:128], q1[:, g, 2 * half:2 * half + 2, :], start=False, stop=True)
                    else:
                        o = st[:, 2 * k, :]
                        mm(o, ident_bf[:, :], mask_k[:, 0:128].unsqueeze(1).broadcast_to([128, 4, 128]), start=True, stop=False)
                        ins = mm(o, k3[:, g, 128:256], q1[:, g, :, 128:256], start=False, stop=True)
                    ins.then_inc(st_ready, 1)

                def attention(layer, groups, tile0, group0, unit0):
                    behind = None
                    for g in range(groups):
                        for c in range(C):
                            i = tile0 + g * C + c
                            if c == 0:
                                e.wait_ge(shift_ready, b * NG + group0 + g + 1)
                            units = list(units_at(c)) if g + 1 < groups else []
                            for n in units[:1]:
                                max_unit(unit0, layer, g + 1, n)
                            scores(i, layer, g, c)
                            for n in units[1:2]:
                                max_unit(unit0, layer, g + 1, n)
                            if c == 1 and g > 0:
                                norm(group0 + g - 1)
                            if behind is not None:
                                values(behind)
                            for n in units[2:]:
                                max_unit(unit0, layer, g + 1, n)
                            behind = i
                        if g + 1 < groups:
                            shift_t(group0 + g + 1)
                        values(behind)
                        behind = None
                    norm(group0 + groups - 1)

                e.wait_ge(ctx_loaded, b * 32 + 32)
                e.wait_ge(p_ready, b * NT + FREE)
                for k, (c0, c1) in enumerate(CTX_UNITS):
                    for c in range(c0, c1):
                        n = ROWS[c]
                        ins = e.transpose(st[:, k, OFF[c] - OFF[c0]:OFF[c] - OFF[c0] + n], ctx_raw[0:n, c, :], ident[0:n, 0:n])
                    ins.then_inc(pj_ready, 1)
                transpose_xn(0, "xnT0")
                e.wait_ge(misc_used, b * NM + M["xnT0"] + 1 + FREE)
                for k in range(4):
                    bank_free(QP_U + k)
                    for h in (2 * k, 2 * k + 1):
                        ins = mm(st[:, k, (h % 2) * T:(h % 2 + 1) * T], m_qk[:, h, :], xnT[:, :], start=True, stop=True)
                    ins.then_inc(pj_ready, 1)
                e.wait_ge(aug_ready, b + 1)
                e.wait_ge(hi_ready, b * NHI + 8)
                for k in range(V0_U, UP_U):
                    bank_free(k)
                    o = st[:, k % 4, :]
                    if k < K1_U:
                        c = k - V0_U
                        n, keys = ROWS[c], slice(OFF[c], OFF[c + 1])
                        mm(o[0:n, :], ctx_hi[:, keys], wv0[:, 0, :], start=True, stop=False)
                        mm(o[0:n, :], ctx_hi[:, keys], wv0[:, 1, :], start=False, stop=False)
                        ins = mm(o[0:n, :], ctx_lo[:, keys], wv0[:, 0, :], start=False, stop=True)
                    elif k < V1_U:
                        g, u = divmod(k - K1_U, 4)
                        cols = slice(MXO[u], MXO[u] + MXW[u])
                        w = slice(g * 128, (g + 1) * 128)
                        mm(o[:, 0:MXW[u]], wk1[:, 0, w], ctx_hi[:, cols], start=True, stop=False)
                        mm(o[:, 0:MXW[u]], wk1[:, 0, w], ctx_lo[:, cols], start=False, stop=False)
                        mm(o[:, 0:MXW[u]], wk1[:, 1, w], ctx_hi[:, cols], start=False, stop=False)
                        ins = mm(o[:, 0:MXW[u]], aug_w[:, :], aug_x[:, cols], start=False, stop=True)
                    else:
                        c0, c1 = V1_UNITS[k - V1_U]
                        for c in range(c0, c1):
                            n, keys = ROWS[c], slice(OFF[c], OFF[c + 1])
                            oc = o[0:n, (c - c0) * 128:(c - c0 + 1) * 128]
                            mm(oc, ctx_hi[:, keys], wv1[:, 0, :], start=True, stop=False)
                            mm(oc, ctx_hi[:, keys], wv1[:, 1, :], start=False, stop=False)
                            ins = mm(oc, ctx_lo[:, keys], wv1[:, 0, :], start=False, stop=True)
                    ins.then_inc(pj_ready, 1)
                    if k - V0_U < 32:
                        max_unit(0, 0, 0, k - V0_U)
                shift_t(0)
                units_done(UP_U)
                attention(0, G0, 0, 0, 0)
                e.wait_ge(att_ready, b * NG + G0 + FREE)
                misc_free("wo0")
                for q in range(QT):
                    for p in range(4):
                        ins = mm(misc[:, q * 128:(q + 1) * 128], att[:, p, q * 128:(q + 1) * 128], wo0[:, p, :],
                                 start=(p == 0), stop=(p == 3))
                ins.then_inc(misc_ready, 1)
                transpose_xn(1, "xnT1")
                e.wait_ge(misc_used, b * NM + M["xnT1"] + 1 + FREE)
                e.wait_ge(p_ready, b * NT + TILE1 + FREE)
                for k in (UP_U, UP_U + 1):
                    for j in range(2):
                        m = 2 * (k - UP_U) + j
                        ins = mm(st[:, k % 4, j * T:(j + 1) * T], wfc[:, m * 128:(m + 1) * 128], xnT[:, :], start=True, stop=True)
                    ins.then_inc(pj_ready, 1)
                e.wait_ge(pj_used_dve, b * NPD + sum(u < Q1_U for u in BY_DVE))
                misc_free("ffn")
                for q in range(QT):
                    for m in range(4):
                        ins = mm(misc[:, q * 128:(q + 1) * 128], relu2[:, m, q * 128:(q + 1) * 128], wpr[:, m, :],
                                 start=(m == 0), stop=(m == 3))
                ins.then_inc(misc_ready, 1)
                transpose_xn(2, "xnT2")
                e.wait_ge(misc_used, b * NM + M["xnT2"] + 1 + FREE)
                for k in (Q1_U, Q1_U + 1):
                    for j in range(2):
                        g = 2 * (k - Q1_U) + j
                        ins = mm(st[:, k % 4, j * T:(j + 1) * T], wq1[:, g * 128:(g + 1) * 128], xnT[:, :], start=True, stop=True)
                    ins.then_inc(pj_ready, 1)
                e.wait_ge(q_ready, b * 3 + 1)
                for n in range(32):
                    max_unit(UNIT1, 1, 0, n)
                shift_t(G0)
                units_done(Q3_U)
                attention(1, G1, TILE1, G0, UNIT1)
                e.wait_ge(att_ready, b * NG + G0 + G1 + FREE)
                misc_free("wo1")
                for q in range(QT):
                    for g in range(G1):
                        ins = mm(misc[:, q * 128:(q + 1) * 128], att[:, g, q * 128:(q + 1) * 128], wo1[:, g, :],
                                 start=(g == 0), stop=(g == G1 - 1))
                ins.then_inc(misc_ready, 1)
                transpose_xn(3, "xnT3")
                e.wait_ge(misc_used, b * NM + M["xnT3"] + 1 + FREE)
                e.wait_ge(p_ready, b * NT + TILE3 + FREE)
                for k in range(Q3_U, V3_U):
                    if k >= Q3_U + 4:
                        bank_free(k)
                    w = wq3 if k < K3_U else wk3
                    for j in range(2):
                        g = 2 * ((k - Q3_U) % 2) + j
                        ins = mm(st[:, k % 4, j * T:(j + 1) * T], w[:, g * 128:(g + 1) * 128], xnT[:, :], start=True, stop=True)
                    ins.then_inc(pj_ready, 1)
                bank_free(V3_U)
                for q in range(2):
                    ins = mm(st[:, V3_U % 4, q * 128:(q + 1) * 128], xnT[:, q * 128:(q + 1) * 128], wv3[:, :], start=True, stop=True)
                ins.then_inc(pj_ready, 1)
                e.wait_ge(q_ready, b * 3 + 3)
                for g in range(G1):
                    for n in range(3):
                        i = UNIT3 + 3 * g + n
                        e.wait_ge(mx_used, b * NU + i - 1 + FREE)
                        if n == 0:
                            mm(mx[:, i % 2, :], ident_bf[:, :], mask_q[:, 128:256].unsqueeze(1).broadcast_to([128, 4, 128]),
                               start=True, stop=False, skip_group_check=True)
                            for j in range(4):
                                ins = mm(mx[:, i % 2, j * 128:(j + 1) * 128], q1[:, g, j, 0:128], k3[:, g, 0:128],
                                         start=False, stop=True, skip_group_check=True)
                        else:
                            mm(mx[:, i % 2, :], ident_bf[:, :], mask_q[:, :].unsqueeze(1).broadcast_to([128, 2, T]),
                               start=True, stop=False, skip_group_check=True)
                            for j in range(2):
                                ins = mm(mx[:, i % 2, j * T:(j + 1) * T], q1[:, g, 2 * (n - 1) + j, 128:256], k3[:, g, :],
                                         start=False, stop=True, skip_group_check=True)
                        ins.then_inc(mx_ready, 1)
                    shift_t(G0 + G1 + g)
                units_done(NP)
                behind = None
                for g in range(G1):
                    e.wait_ge(shift_ready, b * NG + G0 + G1 + g + 1)
                    for c in range(2):
                        i = TILE3 + 2 * g + c
                        scores(i, 3, g, c)
                        if behind is not None:
                            values(behind)
                            if c == 0:
                                norm(G0 + G1 + g - 1)
                        behind = i
                values(behind)
                norm(NG - 1)
                e.wait_ge(att_ready, b * NG + NG + FREE)
                misc_free("wo3")
                for q in range(QT):
                    for g in range(G1):
                        ins = mm(misc[:, q * 128:(q + 1) * 128], att[:, g, q * 128:(q + 1) * 128], wp3[:, g, :],
                                 start=(g == 0), stop=(g == G1 - 1))
                ins.then_inc(misc_ready, 1)
                transpose_xn(4, "xnT4")
                misc_free("router")
                for q in range(QT):
                    ins = mm(misc[:, q * E:(q + 1) * E], xnT[:, q * 128:(q + 1) * 128], gate_w[:, :], start=True, stop=True)
                ins.then_inc(misc_ready, 1)

        @block.scalar
        def _(e):
            e.sem_inc(p_ready, FREE)
            e.sem_inc(kept, FREE)
            with e.Fori(0, B) as b:
                def exps(i, n, width, scale):
                    e.wait_ge(st_ready, b * NT + i + 1)
                    e.wait_ge(av_done, b * NT + max(i - 1, 0) + FREE)
                    if 2 <= i < TILE1:
                        e.wait_ge(sum_done, b * TILE1 + i - 1)
                    elif TILE1 <= i < TILE1 + 2:
                        e.wait_ge(sum_done, b * TILE1 + TILE1)
                    e.activation(probs[0:n, i % 2, 0:width],
                                 st[0:n, 2 * (i % 2):2 * (i % 2) + 2, :].rearrange("p a n -> p (a n)")[:, 0:width],
                                 ACT.Exp, scale=scale).then_inc(p_ready, 1)

                def copy_xnT(n):
                    e.wait_ge(misc_ready, b * NM + M[f"xnT{n}"] + 1)
                    if n == 0:
                        e.wait_ge(kept, b * 32 + FREE)
                    e.copy(xnT[:, :], misc[:, 0:T]).then_inc(misc_used, 1)

                def slots(k, bias, which):
                    e.wait_ge(pj_ready, b * NP + k + 1)
                    for j in range(2):
                        g = 2 * ((k - Q1_U) % 2) + j
                        ins = e.activation(xb[:, which, g, :], st[:, k % 4, j * T:(j + 1) * T], ACT.Identity, bias=bias[:, g:g + 1])
                    ins.then_inc(pj_used_act, 1)

                for k, (c0, c1) in enumerate(CTX_UNITS):
                    e.wait_ge(pj_ready, b * NP + k + 1)
                    w = OFF[c1] - OFF[c0]
                    ins = e.copy(ctx_hi[:, OFF[c0]:OFF[c1]], st[:, k, 0:w])
                    if c1 == C:
                        ins = e.copy(ctx_hi[:, S:SP], st[:, k, w - 1:w])
                    ins.then_inc(hi_ready, 1)
                copy_xnT(0)
                for k in range(4):
                    e.wait_ge(pj_ready, b * NP + QP_U + k + 1)
                    e.copy(q0_hi[:, 2 * k:2 * k + 2, :].rearrange("p h t -> p (h t)"), st[:, k, :]).then_inc(hi_ready, 1)
                for k in range(V0_U, V1_U):
                    e.wait_ge(pj_ready, b * NP + k + 1)
                    if k < K1_U:
                        c = k - V0_U
                        e.copy(v0[0:ROWS[c], c, :], st[0:ROWS[c], k % 4, :]).then_inc(pj_used_act, 1)
                    else:
                        g, u = divmod(k - K1_U, 4)
                        e.copy(k1[:, g, MXO[u]:MXO[u] + MXW[u]], st[:, k % 4, 0:MXW[u]]).then_inc(hi_ready, 1)
                for i in range(TILE1):
                    exps(i, ROWS[i % C], 4 * T, SCALE0)
                copy_xnT(1)
                for k in range(2):
                    e.wait_ge(pj_ready, b * NP + UP_U + k + 1)
                    e.activation(relu[:, 2 * k:2 * k + 2, :].rearrange("p m t -> p (m t)"), st[:, (UP_U + k) % 4, :],
                                 ACT.Relu).then_inc(relu_ready, 1)
                copy_xnT(2)
                slots(Q1_U, bias_q1, 0)
                slots(Q1_U + 1, bias_q1, 0)
                for i in range(TILE1, TILE3):
                    exps(i, ROWS[(i - TILE1) % C], 4 * T, SCALE1)
                copy_xnT(3)
                for k in range(Q3_U, V3_U):
                    slots(k, bias_q3 if k < K3_U else bias_k3, 0 if k < K3_U else 1)
                for i in range(TILE3, NT):
                    exps(i, 128, 4 * T if i % 2 == 0 else 4 * 128, SCALE1)
                copy_xnT(4)
                e.wait_ge(misc_used, b * NM + M["xnT4"] + 1 + FREE)
                e.dma_start(h_keep[b], xnT[:, :]).then_inc(kept, 16)
                e.wait_ge(x4_ready, b + 1)
                e.dma_start(x_keep[b], xr[:, :, :].rearrange("p q d -> p (q d)")).then_inc(kept, 16)
                e.wait_ge(gap_ready, b + 1)
                e.activation(gap[:, :], gap[:, :], ACT.Exp).then_inc(gap_exp, 1)
            e.wait_ge(kept, B * 32 + FREE)

        @block.vector
        def _(e):
            for freed in (misc_used, mx_used, av_copied, att_ready):
                e.sem_inc(freed, FREE)
            def step(ins):
                ins.then_inc(setup_dve, 1)
                step.n += 1
                e.wait_ge(setup_dve, step.n)
            step.n = 0
            e.wait_ge(w_loaded, W_ALL)
            e.wait_ge(setup_pool, NPOOL)
            e.wait_ge(setup_mm, 2)
            for r in range(2):
                step(e.tensor_copy(m_qk[:, :, :].rearrange("p (a c r) d -> p a c r d", a=2, r=2)[:, :, :, r, :],
                                   st[:, 2 * r:2 * r + 2, 0:256].rearrange("p a (c d) -> p a c d", c=2)))
            step(e.tensor_scalar(low_rank[0:RANK, :], misc[0:RANK, 0:128], raw["gate"][0:RANK, :], None, ALU.mult))
            assert step.n == S_LR
            step(e.tensor_copy(ident_bf[:, :], ident[:, :]))
            step(e.tensor_copy(aug_w[:, :], raw["aug_w"]))
            step(e.tensor_copy(lens[:, :], lens_i[:, :]))
            for w, r in ((wv0, raw["wv0"]), (wk1, raw["wk1"]), (wv1, raw["wv1"])):
                step(e.tensor_copy(w[:, 0, :], r))
                step(e.tensor_tensor(w[:, 1, :], r, w[:, 0, :].bitcast(F32), ALU.subtract))

            def ternary(dst, src, scale):
                width = src.shape[-1]
                step(e.tensor_reduce(scale, src, AX.X, ALU.add, apply_absolute_value=True))
                step(e.tensor_scalar(scale, scale, 1.0 / width, 1e-5, ALU.mult, ALU.max))
                step(e.tensor_scalar(t_c[:, 8:9], scale, 0.5, None, ALU.mult))
                step(e.tensor_scalar(t_c[:, 9:10], scale, -0.5, None, ALU.mult))
                step(e.tensor_scalar(dst, src, t_c[:, 9:10], None, ALU.is_lt))
                step(e.scalar_tensor_tensor(dst, src, t_c[:, 8:9], dst, ALU.is_gt, ALU.subtract))
                step(e.tensor_tensor(dst, dst, src, ALU.subtract))
                step(e.tensor_tensor(dst, dst, src, ALU.add))
                step(e.tensor_scalar(dst, dst, scale, None, ALU.mult))

            for k in range(4):
                ternary(t_a[:, k * 128:(k + 1) * 128], raw["wfc"][:, k * 128:(k + 1) * 128], t_c[:, k:k + 1])
            e.wait_ge(setup_mm, 3)
            step(e.tensor_tensor(t_a, t_a, mx[:, 0, :], ALU.add))
            assert step.n == S_FC, step.n
            ternary(t_b, raw["wproj"], t_c[:, 4:5])
            assert step.n == S_PR, step.n
            e.wait_ge(setup_mm, 4)
            step(e.tensor_copy(wfc[:, :], av[:, :]))
            e.wait_ge(setup_mm, 5)
            step(e.tensor_copy(wpr[:, :, :].rearrange("p m d -> p (m d)"), mx[:, 1, :]))
            assert step.n == NSETUP, step.n

            with e.Fori(0, B) as b:
                def link(ins):
                    ins.then_inc(chain, 1)
                    link.n += 1
                    e.wait_ge(chain, b * ND + link.n)
                link.n = 0

                def layernorm(x, gain=None, offset=None, to=xn):
                    for q in range(QT):
                        ins = e.bn_stats(stats[:, q, :], x[:, q, :])
                    link(ins)
                    e.sem_inc(idle, 1)
                    for q in range(QT):
                        ins = e.bn_aggr(mv[:, q, :], stats[:, q, :])
                    link(ins)
                    link(e.tensor_scalar(veps[:, :], mv[:, :, 1], EPS, None, ALU.add))
                    link(e.tensor_scalar(rt[:, :].bitcast(I32), veps[:, :].bitcast(I32), 1, None, ALU.logical_shift_right))
                    link(e.tensor_scalar(rs[:, :].bitcast(I32), rt[:, :].bitcast(I32), -1.0, RSQRT_SEED, ALU.mult, ALU.add))
                    for _ in range(3):
                        link(e.scalar_tensor_tensor(rt[:, :], rs[:, :], -0.5, rs[:, :], ALU.mult, ALU.mult))
                        link(e.tensor_tensor(rt[:, :], rt[:, :], veps[:, :], ALU.mult))
                        link(e.scalar_tensor_tensor(rs[:, :], rt[:, :], 1.5, rs[:, :], ALU.add, ALU.mult))
                    for q in range(QT):
                        ins = e.tensor_scalar(to[:, q, :], x[:, q, :], mv[:, q, 0:1], rs[:, q:q + 1], ALU.subtract, ALU.mult)
                        if gain is not None or to is not xn:
                            link(ins)
                    if to is not xn:
                        return
                    if gain is not None:
                        link(e.tensor_tensor(xn[:, :, :], xn[:, :, :], gain.unsqueeze(1).broadcast_to([128, QT, D]), ALU.mult))
                        ins = e.tensor_tensor(xn[:, :, :], xn[:, :, :], offset.unsqueeze(1).broadcast_to([128, QT, D]), ALU.add)
                    ins.then_inc(xn_ready, 1)

                def max_unit(i, n):
                    e.wait_ge(mx_ready, b * NU + i + 1)
                    hq, u = divmod(n, 4)
                    e.tensor_reduce(mpart[:, hq, u:u + 1], mx[:, i % 2, 0:MXW[u]], AX.X, ALU.max).then_inc(mx_used, 1)

                def negmax(gg, i_end):
                    e.wait_ge(mx_used, b * NU + i_end + FREE)
                    if gg < G0:
                        o = mx0[:, :, 0:4].rearrange("p q h -> p h q")
                    else:
                        o = mx1[:, :, :].rearrange("p q (j s) -> p j q s", s=32)[:, :, :, 25]
                    e.tensor_reduce(o, mpart[:, :, :].rearrange("p (h q) u -> p h q u", h=4), AX.X, ALU.max,
                                    negate=True).then_inc(negmax_ready, 1)

                def shift(gg):
                    e.wait_ge(misc_ready, b * NM + M[f"shift{gg}"] + 1)
                    if gg < G0:
                        link(e.tensor_tensor(neg_shift[0:32, :, :], misc[0:32, 0:T].unsqueeze(1).broadcast_to([32, 4, T]),
                                             ident[0:32, 0:4].unsqueeze(2).broadcast_to([32, 4, T]), ALU.mult))
                    else:
                        g = (gg - G0) % G1
                        for j in range(4):
                            r = slice(32 * j, 32 * j + 32)
                            ins = e.tensor_tensor(q1[r, g, j, :], misc[r, 0:T], q1[r, g, j, :].bitcast(F32), ALU.add)
                        link(ins)
                    e.sem_inc(shift_ready, 1)
                    e.sem_inc(misc_used, 1)

                def av_copy(gg):
                    last = C * (gg + 1) if gg < G0 + G1 else TILE3 + 2 * (gg - G0 - G1 + 1)
                    e.wait_ge(av_done, b * NT + last + FREE)
                    w = 2 if gg < G0 else 1
                    e.wait_ge(att_ready, b * NG + gg + FREE)
                    e.tensor_copy(av_sb[:, 0:w, :].rearrange("p a t -> p (a t)"), av[:, 0:w * T]).then_inc(av_copied, 1)

                def norm(gg):
                    w = 2 if gg < G0 else 1
                    e.wait_ge(misc_ready, b * NM + M[f"norm{gg}"] + 1)
                    e.reciprocal(rden[:, 0:w, :].rearrange("p a t -> p (a t)"), misc[:, 0:w * T]).then_inc(misc_used, 1)
                    e.wait_ge(misc_used, b * NM + M[f"norm{gg}"] + 1 + FREE)
                    e.wait_ge(av_copied, b * NG + gg + 1 + FREE)
                    if gg < G0:
                        o = att[:, 2 * gg:2 * gg + 2, :]
                    else:
                        g = (gg - G0) % G1
                        o = att[:, g:g + 1, :]
                    e.tensor_tensor(o, av_sb[:, 0:w, :], rden[:, 0:w, :], ALU.mult).then_inc(att_ready, 1)

                def attention(groups, group0, unit0):
                    for g in range(groups):
                        if g + 1 < groups:
                            for c in range(C):
                                if c == 1 and g > 0:
                                    norm(group0 + g - 1)
                                for n in units_at(c):
                                    max_unit(unit0 + (g + 1) * 32 + n, n)
                            negmax(group0 + g + 1, unit0 + (g + 2) * 32)
                            shift(group0 + g + 1)
                        elif g > 0:
                            norm(group0 + g - 1)
                        av_copy(group0 + g)
                    norm(group0 + groups - 1)

                def residual(name, base):
                    e.wait_ge(misc_ready, b * NM + M[name] + 1)
                    return e.tensor_tensor(xr[:, :, :], misc[:, 0:T].rearrange("p (q d) -> p q d", q=QT), base, ALU.add)

                e.wait_ge(x_loaded, b * 16 + 16)
                layernorm(x_in)
                e.tensor_scalar(aug_x[0:1, :], key_id[:, :], lens[:, bass.ds(b, 1)], MASK, ALU.is_ge, ALU.mult).then_inc(aug_ready, 1)
                for k, (c0, c1) in enumerate(CTX_UNITS):
                    e.wait_ge(hi_ready, b * NHI + k + 1)
                    w = OFF[c1] - OFF[c0]
                    ins = e.tensor_tensor(ctx_lo[:, OFF[c0]:OFF[c1]], st[:, k, 0:w], ctx_hi[:, OFF[c0]:OFF[c1]].bitcast(F32), ALU.subtract)
                    if c1 == C:
                        ins = e.tensor_tensor(ctx_lo[:, S:SP], st[:, k, w - 1:w], ctx_hi[:, S:SP].bitcast(F32), ALU.subtract)
                    ins.then_inc(pj_used_dve, 1)
                for k in range(4):
                    e.wait_ge(hi_ready, b * NHI + 4 + k + 1)
                    e.tensor_tensor(q0_lo[:, 2 * k:2 * k + 2, :].rearrange("p h t -> p (h t)"), st[:, k, :],
                                    q0_hi[:, 2 * k:2 * k + 2, :].rearrange("p h t -> p (h t)").bitcast(F32),
                                    ALU.subtract).then_inc(pj_used_dve, 1)
                for k in range(V0_U, UP_U):
                    if K1_U <= k < V1_U:
                        g, u = divmod(k - K1_U, 4)
                        kk = k1[:, g, MXO[u]:MXO[u] + MXW[u]]
                        e.wait_ge(hi_ready, b * NHI + 8 + k - K1_U + 1)
                        e.scalar_tensor_tensor(kk, kk.bitcast(F32), low_k, st[:, k % 4, 0:MXW[u]], ALU.mult, ALU.add).then_inc(pj_used_dve, 1)
                    elif k >= V1_U:
                        c0, c1 = V1_UNITS[k - V1_U]
                        n = ROWS[c0]
                        e.wait_ge(pj_ready, b * NP + k + 1)
                        e.tensor_copy(v1[0:n, c0:c1, :, 0:HD1],
                                      st[0:n, k % 4, 0:(c1 - c0) * 128].rearrange("p (c h d) -> p c h d", h=H1, d=HD1)).then_inc(pj_used_dve, 1)
                    if k - V0_U < 32:
                        max_unit(k - V0_U, k - V0_U)
                negmax(0, 32)
                shift(0)
                attention(G0, 0, 0)
                e.wait_ge(kept, b * 32 + FREE)
                e.wait_ge(xbo_ready, b + 1)
                residual("wo0", x_bo[:, :, :]).then_inc(misc_used, 1)
                e.wait_ge(misc_used, b * NM + M["wo0"] + 1 + FREE)
                layernorm(xr)
                for k in range(2):
                    e.wait_ge(relu_ready, b * 2 + k + 1)
                    e.scalar_tensor_tensor(relu2[:, 2 * k:2 * k + 2, :].rearrange("p m t -> p (m t)"), st[:, (UP_U + k) % 4, :], 0.0,
                                           relu[:, 2 * k:2 * k + 2, :].rearrange("p m t -> p (m t)"), ALU.max, ALU.mult).then_inc(pj_used_dve, 1)
                residual("ffn", xr[:, :, :]).then_inc(misc_used, 1)
                e.wait_ge(misc_used, b * NM + M["ffn"] + 1 + FREE)
                layernorm(xr)

                def halves(which, seen):
                    e.wait_ge(pj_used_act, b * NPA + seen)
                    link(e.tensor_copy(hi_tmp, xb[:, which, :, :]))

                def block_diagonal():
                    for j in range(4):
                        r = slice(32 * j, 32 * j + 32)
                        ins = e.scalar_tensor_tensor(q1[r, :, j, :], hi_tmp[r, :, :].bitcast(F32), low_q[r, :], xb[r, 0, :, :], ALU.mult, ALU.add)
                    ins.then_inc(q_ready, 1)

                halves(0, C + 2)
                block_diagonal()
                for n in range(32):
                    max_unit(UNIT1 + n, n)
                negmax(G0, UNIT1 + 32)
                shift(G0)
                attention(G1, G0, UNIT1)
                residual("wo1", xr[:, :, :]).then_inc(misc_used, 1)
                e.wait_ge(misc_used, b * NM + M["wo1"] + 1 + FREE)
                layernorm(xr, to=x_bo)
                layernorm(x_bo, g1, b1)
                halves(0, C + 4)
                block_diagonal()
                e.wait_ge(q_ready, b * 3 + 2)
                halves(1, C + 6)
                e.scalar_tensor_tensor(k3[:, :, :], hi_tmp[:, :, :].bitcast(F32), low_k, xb[:, 1, :, :], ALU.mult, ALU.add).then_inc(q_ready, 1)
                e.wait_ge(pj_ready, b * NP + NP)
                e.tensor_tensor(v3[:, :, :, 0:HD1], st[:, V3_U % 4, 0:256].rearrange("p (c h d) -> p c h d", c=2, d=HD1),
                                bv.rearrange("p (h d) -> p h d", d=HD1).unsqueeze(1).broadcast_to([128, 2, H1, HD1]), ALU.add).then_inc(pj_used_dve, 1)
                for g in range(G1):
                    mj = mx1[:, :, :].rearrange("p q (j s) -> p q j s", s=32)
                    for n in range(3):
                        i = UNIT3 + 3 * g + n
                        e.wait_ge(mx_ready, b * NU + i + 1)
                        if n == 0:
                            e.tensor_reduce(mj[:, 0, :, 25], mx[:, i % 2, :].rearrange("p (j k) -> p j k", j=4), AX.X, ALU.max,
                                            negate=True).then_inc(mx_used, 1)
                        else:
                            e.tensor_reduce(mj[:, 1, 2 * (n - 1):2 * n, 25], mx[:, i % 2, :].rearrange("p (j k) -> p j k", j=2), AX.X, ALU.max,
                                            negate=True).then_inc(mx_used, 1)
                    e.wait_ge(mx_used, b * NU + UNIT3 + 3 * (g + 1) + FREE)
                    e.sem_inc(negmax_ready, 1)
                    shift(G0 + G1 + g)
                for g in range(G1):
                    if g > 0:
                        norm(G0 + G1 + g - 1)
                    av_copy(G0 + G1 + g)
                norm(NG - 1)
                link(e.tensor_tensor(x_bo[:, :, :], x_bo[:, :, :], bp.unsqueeze(1).broadcast_to([128, QT, D]), ALU.add))
                e.wait_ge(misc_ready, b * NM + M["wo3"] + 1)
                e.tensor_tensor(x_bo[:, :, :], misc[:, 0:T].rearrange("p (q d) -> p q d", q=QT), x_bo[:, :, :], ALU.add).then_inc(misc_used, 1)
                e.wait_ge(misc_used, b * NM + M["wo3"] + 1 + FREE)
                layernorm(x_bo, g2, b2)
                e.tensor_tensor(xr[:, :, :], xr[:, :, :], x_bo[:, :, :], ALU.add).then_inc(x4_ready, 1)
                e.wait_ge(misc_ready, b * NM + M["router"] + 1)
                e.tensor_tensor(logit[:, :, :], misc[:, 0:QT * E].rearrange("p (q x) -> p q x", q=QT),
                                gate_b.unsqueeze(1).broadcast_to([128, QT, E]), ALU.add).then_inc(misc_used, 1)
                e.wait_ge(misc_used, b * NM + NM + FREE)
                e.sem_inc(idle, 1)
                for q in range(QT):
                    ins = e.max(top[:, q, :], logit[:, q, :])
                link(ins)
                e.sem_inc(idle, 1)
                for q in range(QT):
                    ins = e.max_index(top_i[:, q, :], top[:, q, :], logit[:, q, :])
                link(ins)
                link(e.tensor_copy(top_f[:, :, :], top_i[:, :, :]))
                e.tensor_tensor(gap[:, :], top[:, :, 1], top[:, :, 0], ALU.subtract).then_inc(gap_ready, 1)
                e.wait_ge(gap_exp, b + 1)
                link(e.tensor_scalar(wgt[:, :, 1], gap[:, :], 1.0, None, ALU.add))
                link(e.reciprocal(wgt[:, :, 0], wgt[:, :, 1]))
                link(e.tensor_tensor(wgt[:, :, 1], wgt[:, :, 0], gap[:, :], ALU.mult))
                for q in range(QT):
                    for t in range(2):
                        link(e.tensor_scalar(sel[:, q, t, :], expert_id[:, :], top_f[:, q, t:t + 1], wgt[:, q, t:t + 1], ALU.is_equal, ALU.mult))
                link(e.tensor_tensor(w_all[:, bass.ds(b * QT, QT), :], sel[:, :, 0, :], sel[:, :, 1, :], ALU.add))
                assert link.n == ND, link.n

        layers.close()
        experts(nc, a, out, x_keep, h_keep, w_all, ident)


def experts(nc, a, out, x_keep, h_keep, w_all, ident):
    with ExitStack() as ctx:
        def sb(name, shape, dt=F32):
            return ctx.enter_context(nc.sbuf_tensor(name, shape, dt))

        def sem(name):
            return ctx.enter_context(nc.semaphore(name))

        KB = HID // 128
        PIECES = 4
        EP = E // PIECES
        HIGH, LOW = 0, 1
        w1 = sb("w1", [128, 2, E, HID], F32R)
        w2 = sb("w2", [128, 2, E, HID], F32R)
        w1_raw = sb("w1_raw", [128, E, HID])
        w2_raw = sb("w2_raw", [128, E, HID])
        eb1 = sb("eb1", [128, E * KB])
        eb2 = sb("eb2", [128, E])
        h_raw = sb("h_raw", [128, 2, TT])
        h_t = sb("h_t", [128, 2, 2, TT], F32R)
        acc = sb("acc", [128, 2, 4, D])
        act_out = sb("act_out", [128, KB, TT])
        mid = sb("mid", [128, 2, 2, KB, TT], F32R)
        y_sb = sb("y_sb", [128, 2, TT])
        up = ctx.enter_context(nc.psum_tensor("up", [128, 4, TT], F32))
        y_t = ctx.enter_context(nc.psum_tensor("y_t", [128, 2, TT], F32))
        down = ctx.enter_context(nc.psum_tensor("down", [128, 2, 4, D], F32))

        bias_loaded = sem("bias_loaded")
        w1_loaded = [sem(f"w1_loaded{i}") for i in range(PIECES)]
        w2_loaded = [sem(f"w2_loaded{i}") for i in range(PIECES)]
        h_loaded = [sem(f"h_loaded{s}") for s in range(2)]
        acc_loaded = [sem(f"acc_loaded{s}") for s in range(2)]
        w_high = sem("w_high")
        w1_ready = sem("w1_ready")
        w2_ready = sem("w2_ready")
        h_high = sem("h_high")
        h_ready = sem("h_ready")
        up_ready = sem("up_ready")
        gelu_ready = sem("gelu_ready")
        low_ready = sem("low_ready")
        y_ready = sem("y_ready")
        y_taken = sem("y_taken")
        down_ready = sem("down_ready")
        down_used = sem("down_used")
        stored = [sem(f"stored{s}") for s in range(2)]
        SPARE = 2

        def chain_of_blocks(e, run):
            with e.Fori(0, NTT // 2 - 1) as pair:
                for s in range(2):
                    run(pair, s, False)
            run(NTT // 2 - 1, 0, False)
            run(NTT // 2 - 1, 1, True)

        with nc.Block() as block:
            @block.sync
            def _(e):
                def load_h(t, s):
                    e.dma_start(h_raw[:, s, :].rearrange("p (b t) -> p b t", b=2),
                                h_keep[bass.ds(t * 2, 2), :, :].rearrange("b d t -> d b t")).then_inc(h_loaded[s], 16)

                def load_acc(t, s):
                    e.dma_start(acc[:, s, :, :].rearrange("p (b q) d -> p b (q d)", b=2),
                                x_keep[bass.ds(t * 2, 2), :, :].rearrange("b p n -> p b n")).then_inc(acc_loaded[s], 16)

                load_h(0, 0)
                e.dma_start(eb1[:, :], a["eb1"]).then_inc(bias_loaded, 16)
                e.dma_start(eb2[:, :], a["eb2"]).then_inc(bias_loaded, 16)
                load_acc(0, 0)
                load_h(1, 1)
                load_acc(1, 1)
                with e.Fori(1, NTT // 2) as tt:
                    for s in range(2):
                        t = tt * 2 + s
                        e.wait_ge(up_ready, (t - 1) * (E * KB))
                        load_h(t, s)
                        e.wait_ge(stored[s], tt * 32)
                        load_acc(t, s)

            @block.gpsimd
            def _(e):
                for i in range(PIECES):
                    e.dma_start(w2_raw[:, i * EP:(i + 1) * EP, :].rearrange("p x (k d) -> p x k d", k=KB),
                                a["w2"][i * EP:(i + 1) * EP].rearrange("x (k p) d -> p x k d", p=128)).then_inc(w2_loaded[i], 16)
                with e.Fori(0, NTT // 2) as tt:
                    for s in range(2):
                        n = tt * 2 + s
                        e.wait_ge(down_used, (n + 1) * E + SPARE)
                        for h in range(2):
                            e.dma_start(out[bass.ds(n * 2 + h, 1), :, :].rearrange("b (q p) d -> p (b q) d", p=128),
                                        acc[:, s, 2 * h:2 * h + 2, :]).then_inc(stored[s], 16)
                for s in range(2):
                    e.wait_ge(stored[s], NTT * 16)

            @block.tensor
            def _(e):
                def ups(n, s, x, ks, first=False):
                    for k in ks:
                        if not first:
                            e.wait_ge(gelu_ready, n * (E * KB) + (x * KB + k - 3))
                        w = slice(k * 128, (k + 1) * 128)
                        e.matmul(up[:, k, :], w1[:, HIGH, x, w], h_t[:, s, HIGH, :], start=True, stop=False)
                        e.matmul(up[:, k, :], w1[:, HIGH, x, w], h_t[:, s, LOW, :], start=False, stop=False)
                        e.matmul(up[:, k, :], w1[:, LOW, x, w], h_t[:, s, HIGH, :], start=False, stop=True).then_inc(up_ready, 1)

                def downs(n, x):
                    e.wait_ge(y_taken, n * E + (x - 1 + SPARE))
                    for k in range(KB):
                        e.wait_ge(low_ready, n * (E * KB) + (x * KB + k + 1 + KB))
                        w = slice(k * 128, (k + 1) * 128)
                        o = y_t[:, x % 2, :]
                        e.matmul(o, w2[:, HIGH, x, w], mid[:, x % 2, HIGH, k, :], start=(k == 0), stop=False)
                        e.matmul(o, w2[:, LOW, x, w], mid[:, x % 2, HIGH, k, :], start=False, stop=False)
                        ins = e.matmul(o, w2[:, HIGH, x, w], mid[:, x % 2, LOW, k, :], start=False, stop=(k == KB - 1))
                    ins.then_inc(y_ready, 1)

                def turn(n, x):
                    e.wait_ge(y_taken, n * E + (x + 1 + SPARE))
                    e.wait_ge(down_used, n * E + (x - 1 + SPARE))
                    for q in range(4):
                        ins = e.transpose(down[:, x % 2, q, :], y_sb[:, x % 2, q * 128:(q + 1) * 128], ident[:, :])
                    ins.then_inc(down_ready, 1)

                def run(pair, s, last):
                    n = pair * 2 + s
                    for x in range(E):
                        step_after = (n, s, x + 1) if x + 1 < E else (n + 1, 1 - s, 0)
                        if x + 1 == E and not last:
                            e.wait_ge(h_ready, n + 2)
                        if not (x + 1 == E and last):
                            ups(*step_after, range(0, KB // 2))
                        downs(n, x)
                        if not (x + 1 == E and last):
                            ups(*step_after, range(KB // 2, KB))
                        turn(n, x)

                e.sem_inc(y_ready, SPARE)
                e.wait_ge(w1_ready, PIECES)
                e.wait_ge(h_ready, 1)
                ups(0, 0, 0, range(KB), first=True)
                e.wait_ge(w2_ready, PIECES)
                chain_of_blocks(e, run)

            @block.scalar
            def _(e):
                def high_of_h(pair, s):
                    e.wait_ge(h_loaded[s], pair * 16 + 16)
                    e.copy(h_t[:, s, HIGH, :], h_raw[:, s, :]).then_inc(h_high, 1)

                def run(pair, s, last):
                    n = pair * 2 + s
                    for x in range(E):
                        e.wait_ge(y_ready, n * E + (x - 1 + SPARE))
                        for k in range(KB):
                            e.wait_ge(low_ready, n * (E * KB) + (x * KB + k + 1))
                            i = x * KB + k
                            e.wait_ge(up_ready, n * (E * KB) + (i + 1))
                            e.activation(act_out[:, k, :], up[:, k, :], ACT.Gelu, bias=eb1[:, i:i + 1])
                            e.activation(mid[:, x % 2, HIGH, k, :], up[:, k, :], ACT.Gelu, bias=eb1[:, i:i + 1]).then_inc(gelu_ready, 1)
                        if x == E // 2 and not last:
                            high_of_h(pair + s, 1 - s)

                for i in range(PIECES):
                    e.dma_start(w1_raw[:, i * EP:(i + 1) * EP, :],
                                a["w1"][i * EP:(i + 1) * EP].rearrange("x p n -> p x n")).then_inc(w1_loaded[i], 16)
                high_of_h(0, 0)
                for w, raw, loaded in ((w1, w1_raw, w1_loaded), (w2, w2_raw, w2_loaded)):
                    for i in range(PIECES):
                        e.wait_ge(loaded[i], 16)
                        xs = slice(i * EP, (i + 1) * EP)
                        e.copy(w[:, HIGH, xs, :].rearrange("p x n -> p (x n)"),
                               raw[:, xs, :].rearrange("p x n -> p (x n)")).then_inc(w_high, 1)
                e.wait_ge(bias_loaded, 32)
                chain_of_blocks(e, run)

            @block.vector
            def _(e):
                def low_of_h(n, s):
                    e.wait_ge(h_high, n + 1)
                    e.tensor_tensor(h_t[:, s, LOW, :], h_raw[:, s, :], h_t[:, s, HIGH, :].bitcast(F32),
                                    ALU.subtract).then_inc(h_ready, 1)

                def lows(n, x, ks):
                    for k in ks:
                        e.wait_ge(gelu_ready, n * (E * KB) + (x * KB + k + 1))
                        m = mid[:, x % 2, :, k, :]
                        e.tensor_tensor(m[:, LOW, :], act_out[:, k, :], m[:, HIGH, :].bitcast(F32),
                                        ALU.subtract).then_inc(low_ready, 1)

                def run(pair, s, last):
                    n = pair * 2 + s
                    for x in range(E):
                        step_after = (n, x + 1) if x + 1 < E else (n + 1, 0)
                        if not (x + 1 == E and last):
                            lows(*step_after, range(0, KB // 2))
                        e.wait_ge(y_ready, n * E + (x + 1 + SPARE))
                        e.tensor_scalar(y_sb[:, x % 2, :], y_t[:, x % 2, :], eb2[:, x:x + 1], None, ALU.add).then_inc(y_taken, 1)
                        if not (x + 1 == E and last):
                            lows(*step_after, range(KB // 2, KB))
                        if x == E // 2 and not last:
                            low_of_h(n + 1, 1 - s)
                        if x == 0:
                            e.wait_ge(acc_loaded[s], pair * 16 + 16)
                        e.wait_ge(down_ready, n * E + (x + 1))
                        e.wait_ge(down_used, n * E + (x + SPARE))
                        for q in range(4):
                            w = w_all[:, bass.ds(n * 4 + q, 1), x:x + 1].rearrange("p a b -> p (a b)")
                            ins = e.scalar_tensor_tensor(acc[:, s, q, :], down[:, x % 2, q, :], w, acc[:, s, q, :], ALU.mult, ALU.add)
                        ins.then_inc(down_used, 1)

                e.sem_inc(y_taken, SPARE)
                e.sem_inc(low_ready, KB)
                e.sem_inc(down_used, SPARE)
                low_of_h(0, 0)
                for j, (w, raw, ready) in enumerate(((w1, w1_raw, w1_ready), (w2, w2_raw, w2_ready))):
                    for i in range(PIECES):
                        e.wait_ge(w_high, j * PIECES + i + 1)
                        xs = slice(i * EP, (i + 1) * EP)
                        whole, hi = (v.rearrange("p x n -> p (x n)") for v in (raw[:, xs, :], w[:, HIGH, xs, :].bitcast(F32)))
                        e.tensor_tensor(w[:, LOW, xs, :].rearrange("p x n -> p (x n)"), whole, hi,
                                        ALU.subtract).then_inc(ready, 1)
                e.wait_ge(bias_loaded, 32)
                lows(0, 0, range(KB))
                chain_of_blocks(e, run)


_IN = ["x", "ctx", "lens", "wqT0", "wkT0", "wv0", "wo0", "wfc", "wproj", "uT", "fastT", "v", "gate",
       "wq1", "wk1", "wv1", "wo1", "wq3", "wk3", "wv3", "wp3", "gate_w", "rows", "slot_c", "aug_w",
       "w1", "w2", "eb1", "eb2"]


def _slots(w, places):
    w = np.asarray(w)
    o = np.zeros((w.shape[0], H1, 32), w.dtype)
    for at in places:
        o[:, :, at:at + HD1] = w.reshape(w.shape[0], H1, HD1)
    return o.reshape(w.shape[0], H1 * 32)


def kernel(**inputs):
    import concourse.bacc as bacc
    from concourse.bass_utils import run_bass_kernel_spmd

    i = {k: np.asarray(v) for k, v in inputs.items()}
    f = i["x"].dtype
    three, one = (0, HD1, 2 * HD1), (0,)

    def columns(v):
        return v.reshape(G1, 128).T

    signs = np.zeros((128, 2), f)
    const = np.zeros((128, 3 * G1), f)
    aug = np.zeros((128, 128), f)
    for j in range(4):
        signs[32 * j + HD1:32 * j + 2 * HD1, 0] = -1
        signs[32 * j + 2 * HD1:32 * j + 3 * HD1, 1] = -1
        const[32 * j + 24, 0:G1] = 1
        const[32 * j + 25, 2 * G1:] = 1
        aug[0, 32 * j + 24] = 1
        aug[32, 32 * j + 25] = 1
    biases = np.concatenate([np.zeros((128, G1), f), columns(_slots(i["L1_ffn_bq"][None], three)),
                             columns(_slots(i["L1_ffn_bk"][None], three))], axis=1)
    slot_c = np.concatenate([signs, np.where(const != 0, const, biases)], axis=1)
    every = lambda v: np.broadcast_to(v.reshape(1, -1), (128, v.size))
    rows_of_slots = lambda w: _slots(w.T, one).T.reshape(G1, 128, D)
    arrays = {
        "x": i["x"], "ctx": i["ctx_1024"], "lens": i["_lenS2"].reshape(1, B),
        "wqT0": i["L0_xattn_Wq"].T, "wkT0": i["L0_xattn_Wk"].T, "wv0": i["L0_xattn_Wv"], "wo0": i["L0_xattn_Wo"],
        "wfc": i["L0_ffn_w_fc"], "wproj": i["L0_ffn_w_proj"], "uT": i["L0_ffn_u"].T, "fastT": i["L0_ffn_fast_b"].T,
        "v": i["L0_ffn_v"], "gate": every(i["L0_ffn_gate"]),
        "wq1": _slots(i["L1_xattn_Wq"], three), "wk1": _slots(i["L1_xattn_Wk"], three), "wv1": i["L1_xattn_Wv"],
        "wo1": rows_of_slots(i["L1_xattn_Wo"]),
        "wq3": _slots(i["L1_ffn_Wq"], three), "wk3": _slots(i["L1_ffn_Wk"], three), "wv3": i["L1_ffn_Wv"],
        "wp3": rows_of_slots(i["L1_ffn_Wp"]), "gate_w": i["L1_ffn_gate_W"],
        "rows": np.concatenate([every(i[k]) for k in (
            "L0_xattn_bo", "L1_ffn_bv", "L1_ffn_bp", "L1_ffn_ln1_g", "L1_ffn_ln1_b", "L1_ffn_ln2_g", "L1_ffn_ln2_b",
            "L1_ffn_gate_b")], axis=1),
        "slot_c": slot_c, "aug_w": aug,
        "w1": i["L1_ffn_exp_W1"], "w2": i["L1_ffn_exp_W2"],
        "eb1": i["L1_ffn_exp_b1"].reshape(E * 4, 128).T, "eb2": i["L1_ffn_exp_b2"].T,
    }
    nc = bacc.Bacc("TRN2", target_bir_lowering=False, num_devices=1)
    given, aps = {}, {}
    for name in _IN:
        v = np.ascontiguousarray(arrays[name])
        given[f"in_{name}"] = v
        aps[name] = nc.dram_tensor(f"in_{name}", v.shape, mybir.dt.from_np(v.dtype), kind="ExternalInput").ap()
    out = nc.dram_tensor("out", (B, T, D), F32, kind="ExternalOutput").ap()
    build(nc, aps, out)
    r = run_bass_kernel_spmd(nc, [given], core_ids=[0])
    return r.results[0]["out"]
```

```python
from contextlib import ExitStack

import concourse.bass as bass
import numpy as np
from concourse import mybir

F32 = mybir.dt.float32
F32R = mybir.dt.float32r
BF16 = mybir.dt.bfloat16
F16 = mybir.dt.float16
I32 = mybir.dt.int32
U32 = mybir.dt.uint32
ALU = mybir.AluOpType
ACT = mybir.ActivationFunctionType
AX = mybir.AxisListType

B, T, D, S = 16, 256, 128, 1601
QT = T // 128
C = 13
ROWS = [-(-(S - c) // C) for c in range(C)]
OFF = [sum(ROWS[:c]) for c in range(C + 1)]
SP = S + 1
H0, HD0 = 8, 64
H1, HD1 = 16, 8
G0, G1 = H0 // 4, H1 // 4
SCALE0, SCALE1 = HD0 ** -0.5, HD1 ** -0.5
MASK = -1e6 * HD1 ** 0.5
CAUSAL = -1e30
EPS = 1e-5
RSQRT_SEED = float(0x5F3759DF)
HID, E = 512, 8
RANK = 16

NT = (G0 + G1) * C + G1 * 2
TILE1, TILE3 = G0 * C, (G0 + G1) * C
MXW = [402, 400, 400, 400]
MXO = [sum(MXW[:i]) for i in range(4)]
NW = 16
WIDE = MXW[0]
NU = (G0 + G1 - 1) * 32 + G1 * 3
UNIT1, UNIT3 = (G0 - 1) * 32, (G0 + G1 - 1) * 32
NG = G0 + 2 * G1
FRONT = ["ctx"] * 4 + ["qp"] * 4 + ["v0"] * C
BETWEEN = ["k", "k", "k", "k", "v", "v", "k", "k", "up", "up", "k", "k", "v", "v", "k", "k", "q", "q"] + ["k"] * 6
V0_EARLY = 6
LAST = ["ctx"] * 4 + ["qp"] * 4 + ["v0"] * V0_EARLY + ["q3", "q3", "k3", "k3", "v3"] + ["v0"] * (C - V0_EARLY)
UNITS = FRONT + BETWEEN + LAST
B_U, L_U = len(FRONT), len(FRONT) + len(BETWEEN)
NP = len(UNITS) - B_U


def places(kind, start, stop):
    return [k for k in range(start, stop) if UNITS[k] == kind]


K1, V1, UP, Q1 = (places(kind, B_U, L_U) for kind in ("k", "v", "up", "q"))
Q3, K3, (V3,) = (places(kind, L_U, len(UNITS)) for kind in ("q3", "k3", "v3"))
AHEAD = {kind: places(kind, 0, B_U) for kind in ("ctx", "qp", "v0")}
NEXT = {kind: places(kind, L_U, len(UNITS)) for kind in ("ctx", "qp", "v0")}
CTX_UNITS = [(0, 4), (4, 8), (8, 12), (12, 13)]
V1_UNITS = [(0, 2), (2, 6), (6, 10), (10, 13)]
BY_ACT = [k for k in range(len(UNITS)) if UNITS[k] in ("v0", "v", "q", "q3", "k3")]
BY_DVE = [k for k in range(len(UNITS)) if k not in BY_ACT]
NPA, NPD = (sum(k >= B_U for k in by) for by in (BY_ACT, BY_DVE))
MISC = (["xnT_ahead", "shift_ahead", "shift1", "norm0", "norm1", "wo0", "xnT1", "ffn", "xnT2"]
        + ["shift2", "shift3", "norm2", "shift4", "norm3", "shift5", "norm4", "xnT0", "norm5", "attT1", "wo1", "xnT3"]
        + ["shift6", "shift7", "shift8", "shift9", "norm6", "norm7", "norm8", "norm9", "shift0", "attT3", "wo3", "xnT4", "router"])
NM = len(MISC) - 2
M = {name: i for i, name in enumerate(MISC)}
NORMS = ["xnT_ahead", "xnT1", "xnT2", "xnT0", "xnT3", "xnT4"]
NX = len(NORMS) - 1
NHI = 4 + 4 + 16
ND = 104
TT, NTT = 512, B * T // 512
FREE = 1


DVE_SLOTS, ACT_SLOTS = (0, 1), (2, 3)
K = 6


LEAD = 1.2


def units_at(layer, t):
    if layer == 0:
        done = [min(32, max(0, 32 * (u - K) // (C - 1 - K))) for u in (t, t + 1)]
    else:
        done = [min(32 * (G1 - 1), int(32 * (u + LEAD) / C)) if u else 0 for u in (t, t + 1)]
    return list(range(*done))


for _t in range(C, G1 * C):
    assert all(_n // 32 > _t // C or _t % C <= C - 2 for _n in units_at(1, _t))


NSETUP, S_LR, S_FC, S_PR, NPOOL = 60, 3, 49, 58, 20


def build(nc, a, out):
    ctx = ExitStack()
    with ctx:
        def sb(name, shape, dt=F32):
            return ctx.enter_context(nc.sbuf_tensor(name, shape, dt))

        def sem(name):
            return ctx.enter_context(nc.semaphore(name))

        x_keep = nc.dram_tensor("x_keep", [B, 128, QT * D], F32).ap()
        h_keep = nc.dram_tensor("h_keep", [B, D, T], F32).ap()

        ident = sb("ident", [128, 128])
        w_all = sb("w_all", [128, B * QT, E])

        layers = ctx.enter_context(ExitStack())

        def sb(name, shape, dt=F32):
            return layers.enter_context(nc.sbuf_tensor(name, shape, dt))

        ident_bf = sb("ident_bf", [128, 128], BF16)
        ones = sb("ones", [128, 64])
        ones_bf = sb("ones_bf", [128, 128], BF16)
        mask_k = sb("mask_k", [128, 256], BF16)
        mask_q = sb("mask_q", [128, 256], BF16)
        key_id = sb("key_id", [1, SP], F16)
        lens_i = sb("lens_i", [1, B], I32)
        lens = sb("lens", [1, B])
        aug_w = sb("aug_w", [128, 128], BF16)
        aug_x = sb("aug_x", [128, SP], BF16)
        slot_c = sb("slot_c", [128, 2 + 3 * G1])
        low_q, low_k = slot_c[:, 0:1], slot_c[:, 1:2]
        bias_q1, bias_q3, bias_k3 = (slot_c[:, 2 + i * G1:2 + (i + 1) * G1] for i in range(3))
        rows = sb("rows", [128, 7 * 128 + E])
        bo, bv, bp, g1, b1, g2, b2 = (rows[:, i * 128:(i + 1) * 128] for i in range(7))
        gate_b = rows[:, 7 * 128:7 * 128 + E]
        m_qk = sb("m_qk", [128, H0, 128])
        wv0 = sb("wv0", [128, 2, 512], F32R)
        wk1 = sb("wk1", [128, 2, G1 * 128], F32R)
        wv1 = sb("wv1", [128, 2, 128], F32R)
        wq1 = sb("wq1", [128, G1 * 128])
        wo0 = sb("wo0", [128, 4, 128])
        wo1 = sb("wo1", [128, 128])
        wfc = sb("wfc", [128, HID])
        wpr = sb("wpr", [128, 4, 128])
        wq3 = sb("wq3", [128, G1 * 128])
        wk3 = sb("wk3", [128, G1 * 128])
        wv3 = sb("wv3", [128, 128])
        wp3 = sb("wp3", [128, 128])
        gate_w = sb("gate_w", [128, E])
        expert_id = sb("expert_id", [128, E])

        ctx_raw = sb("ctx_raw", [128, C, 128])
        ctx_hi = sb("ctx_hi", [128, SP], F32R)
        ctx_lo = sb("ctx_lo", [128, SP], F32R)
        q0_hi = sb("q0_hi", [128, H0, T], F32R)
        q0_lo = sb("q0_lo", [128, H0, T], F32R)
        q1 = sb("q1", [128, G1, 4, T], F32R)
        k1 = sb("k1", [128, G1, SP], F32R)
        k3 = k1[:, 0, 0:G1 * T].rearrange("p (g t) -> p g t", g=G1)
        v0 = sb("v0", [128, C, 512])
        v1 = sb("v1", [128, C, H1, 32])
        v3 = sb("v3", [128, 2, H1, 32])
        probs = sb("probs", [128, 2, 4 * T])
        prob_sum = sb("prob_sum", [128, 2, 4 * T])
        neg_shift = sb("neg_shift", [128, G0, 4, T], BF16)
        mpart = sb("mpart", [128, 8, 4])
        mx0 = sb("mx0", [128, QT, 32])
        mx1 = sb("mx1", [128, QT, 128])
        av_sb = sb("av_sb", [128, 2, T])
        rden = sb("rden", [128, 2, T])
        att = sb("att", [128, 4, T])
        att_q = att[:, 1, :].rearrange("p (q n) -> p q n", q=QT)
        att_t = att[:, 0, :]
        x_in = sb("x_in", [128, QT, D])
        x_bo = sb("x_bo", [128, QT, D])
        xr = sb("xr", [128, QT, D])
        xn = rden[:, 0, :].rearrange("p (q d) -> p q d", q=QT)
        xnT = sb("xnT", [128, T])
        xb = prob_sum[:, :, :].rearrange("p w (g t) -> p w g t", g=G1)
        hi_tmp = att[:, :, :].bitcast(F32R)
        relu = xb[:, 0, :, :]
        relu2 = xb[:, 1, :, :]
        stats = sb("stats", [128, QT, 6])
        mv = sb("mv", [128, QT, 2])
        veps = sb("veps", [128, QT])
        nveps = sb("nveps", [128, QT])
        rs = sb("rs", [128, QT])
        rsum = sb("rsum", [128, QT, 4])
        rt = sb("rt", [128, QT])
        logit = sb("logit", [128, QT, E])
        top = sb("top", [128, QT, 8])
        top_i = sb("top_i", [128, QT, 8], U32)
        top_f = sb("top_f", [128, QT, 8])
        gap = sb("gap", [128, QT])
        wgt = sb("wgt", [128, QT, 2])
        sel = sb("sel", [128, QT, 2, E])
        st = layers.enter_context(nc.psum_tensor("st", [128, 4, 512], F32))
        mx = layers.enter_context(nc.psum_tensor("mx", [128, 2, 512], F32))
        av = layers.enter_context(nc.psum_tensor("av", [128, 512], F32))
        misc = layers.enter_context(nc.psum_tensor("misc", [128, 512], F32))

        w_loaded = sem("w_loaded")
        ctx_loaded = sem("ctx_loaded")
        x_loaded = sem("x_loaded")
        setup_mm = sem("setup_mm")
        setup_dve = sem("setup_dve")
        setup_pool = sem("setup_pool")
        pj_ready = sem("pj_ready")
        pj_used_act = sem("pj_used_act")
        pj_used_dve = sem("pj_used_dve")
        hi_ready = sem("hi_ready")
        misc_ready = sem("misc_ready")
        misc_used = sem("misc_used")
        xn_ready = sem("xn_ready")
        aug_ready = sem("aug_ready")
        relu_ready = sem("relu_ready")
        q_ready = sem("q_ready")
        slots_ready = sem("slots_ready")
        q_ready_act = sem("q_ready_act")
        mx_ready = sem("mx_ready")
        mx_used = sem("mx_used")
        wide_ready = sem("wide_ready")
        wide_used = sem("wide_used")
        negmax_ready = sem("negmax_ready")
        shift_ready = sem("shift_ready")
        st_ready = sem("st_ready")
        p_ready = sem("p_ready")
        av_done = sem("av_done")
        sum_done = sem("sum_done")
        av_copied = sem("av_copied")
        att_ready = sem("att_ready")
        xbo_ready = sem("xbo_ready")
        x4_ready = sem("x4_ready")
        kept = sem("kept")
        gap_exp = sem("gap_exp")
        gap_ready = sem("gap_ready")
        chain = sem("chain")
        idle = sem("idle")

        block = layers.enter_context(nc.Block())

        ctx_v = a["ctx"]

        def load_ctx(e, b):
            full = ROWS[-1]
            e.dma_start(ctx_raw[0:full, :, :], ctx_v[b, 0:full * C, :].rearrange("(p c) d -> p c d", c=C)).then_inc(ctx_loaded, 16)
            e.dma_start(ctx_raw[full:full + 1, 0:S - full * C, :],
                        ctx_v[b, full * C:S, :].unsqueeze(0)).then_inc(ctx_loaded, 16)

        stage = v0[:, :, :].rearrange("p c n -> p (c n)")
        raw = {}
        at = 0
        for name, width in (("wqT0", 512), ("wkT0", 512), ("wv0", 512), ("wk1", 512), ("wv1", 128),
                            ("wfc", 512), ("wproj", 512), ("uT", 512), ("fastT", RANK), ("v", 128), ("gate", 1), ("aug_w", 128)):
            raw[name] = stage[:, at:at + width]
            at += width
        stage1 = v1[:, :, :, :].rearrange("p c h n -> p (c h n)")
        pT0 = stage1[:, 0:512]
        t_a, t_b, t_c = (stage1[:, 512 * i:512 * (i + 1)] for i in range(1, 4))
        low_rank = stage1[:, 2048:2176]

        LOADS = [
            (raw["wqT0"].rearrange("p (a d) -> p a d", a=4), a["wqT0"].rearrange("(a p) d -> p a d", p=128)),
            (raw["wkT0"].rearrange("p (a d) -> p a d", a=4), a["wkT0"].rearrange("(a p) d -> p a d", p=128)),
            (raw["wv0"], a["wv0"]), (raw["wk1"], a["wk1"]), (raw["wv1"], a["wv1"]),
            (raw["wfc"].rearrange("p (a d) -> p a d", a=4), a["wfc"].rearrange("(a p) d -> p a d", p=128)),
            (raw["wproj"], a["wproj"]), (raw["uT"][0:RANK, :], a["uT"]), (raw["fastT"][0:RANK, :], a["fastT"]),
            (raw["v"][0:RANK, :], a["v"]), (raw["gate"], a["gate"]),
            (wo0[:, :, :], a["wo0"].rearrange("(a p) d -> p a d", p=128)),
            (wq1[:, :], a["wq1"]), (wo1[:, :], a["wo1"]),
            (wq3[:, :], a["wq3"]), (wk3[:, :], a["wk3"]), (wv3[:, :], a["wv3"]),
            (wp3[:, :], a["wp3"]), (gate_w[:, :], a["gate_w"]),
            (rows[:, :], a["rows"]), (slot_c[:, :], a["slot_c"]), (raw["aug_w"], a["aug_w"]), (lens_i[:, :], a["lens"]),
        ]
        W_ALL = 16 * len(LOADS)

        @block.sync
        def _(e):
            for dst, src in LOADS:
                e.dma_start(dst, src).then_inc(w_loaded, 16)
            def load_x(b):
                e.dma_start(x_in[:, :, :], a["x"][b].rearrange("(q p) d -> p q d", p=128)).then_inc(x_loaded, 16)

            load_ctx(e, 0)
            load_x(0)
            e.wait_ge(pj_ready, AHEAD["ctx"][-1] + 1)
            load_ctx(e, 1)

            def after(b, x_next, ctx_next):
                e.wait_ge(misc_used, b * NM + M["wo0"] + 1 + FREE)
                load_x(x_next)
                if ctx_next is not None:
                    e.wait_ge(pj_ready, b * NP + NEXT["ctx"][-1] + 1)
                    load_ctx(e, ctx_next)

            with e.Fori(0, B - 2) as b:
                after(b, b + 1, b + 2)
            after(B - 2, B - 1, B - 1)
            after(B - 1, B - 1, None)

        @block.gpsimd
        def _(e):
            def step(ins):
                ins.then_inc(setup_pool, 1)
                step.n += 1
                e.wait_ge(setup_pool, step.n)
            step.n = 0
            step(e.memset(ident[:, :], 0.0))
            step(e.affine_select(out=ident[:, :], in_=ident[:, :], compare_op=ALU.not_equal, fill=1.0, base=0,
                                 pattern=[[-1, 128]], channel_multiplier=1))
            step(e.memset(mask_k[:, :], 0.0))
            step(e.affine_select(out=mask_k[:, 0:128], in_=mask_k[:, 0:128], compare_op=ALU.is_ge, fill=CAUSAL,
                                 base=0, pattern=[[1, 128]], channel_multiplier=-1))
            step(e.memset(mask_q[:, :], 0.0))
            step(e.affine_select(out=mask_q[:, 128:256], in_=mask_q[:, 128:256], compare_op=ALU.is_ge, fill=CAUSAL,
                                 base=0, pattern=[[-1, 128]], channel_multiplier=1))
            two = ROWS[0] * 2
            step(e.iota(key_id[:, 0:two], [[1, 2], [C, ROWS[0]]], base=0, channel_multiplier=0,
                        allow_small_or_imprecise_dtypes=True))
            step(e.iota(key_id[:, two:S], [[1, C - 2], [C, ROWS[-1]]], base=2, channel_multiplier=0,
                        allow_small_or_imprecise_dtypes=True))
            step(e.iota(key_id[:, S:SP], [[1, 1]], base=(ROWS[-1] - 1) * C + C - 1, channel_multiplier=0,
                        allow_small_or_imprecise_dtypes=True))
            step(e.iota(expert_id[:, :], [[1, E]], base=0, channel_multiplier=0, allow_small_or_imprecise_dtypes=True))
            step(e.memset(ones[:, :], 1.0))
            step(e.memset(ones_bf[:, :], 1.0))
            step(e.memset(aug_x[:, :], 0.0))
            step(e.memset(aug_x[32:33, :], 1.0))
            step(e.memset(neg_shift[:, :, :, :], 0.0))
            step(e.memset(mx0[:, :, :], 0.0))
            step(e.memset(mx1[:, :, :], 0.0))
            step(e.memset(v3[:, :, :, :], 0.0))
            step(e.memset(v3[:, :, :, HD1:HD1 + 1], 1.0))
            step(e.memset(q1[:, :, :, :].bitcast(F32), 0.0))
            assert step.n == NPOOL
            e.wait_ge(setup_dve, NSETUP)
            step(e.memset(v1[:, :, :, :], 0.0))
            step(e.memset(v1[:, :, :, HD1:HD1 + 1], 1.0))

            def share(b, i):
                g, c = divmod(i, C)
                n = ROWS[c]
                e.wait_ge(p_ready, b * NT + (i + 1 + FREE))
                if c == 0:
                    e.sem_inc(idle, 1)
                    e.tensor_copy(prob_sum[0:n, g, :], probs[0:n, i % 2, :]).then_inc(sum_done, 1)
                else:
                    e.wait_ge(sum_done, b * TILE1 + i)
                    e.tensor_tensor(prob_sum[0:n, g, :], prob_sum[0:n, g, :], probs[0:n, i % 2, :],
                                    ALU.add).then_inc(sum_done, 1)

            with e.Fori(0, B) as b:
                for i in range(C):
                    share(b, i)
                e.wait_ge(x_loaded, b * 16 + 16)
                e.wait_ge(misc_used, b * NM + M["shift1"] + FREE)
                e.tensor_tensor(x_bo[:, :, :], x_in[:, :, :], bo.unsqueeze(1).broadcast_to([128, QT, D]),
                                ALU.add).then_inc(xbo_ready, 1)
                for i in range(C, TILE1):
                    share(b, i)
            for i in range(K):
                share(B, i)

        @block.tensor
        def _(e):
            mm = e.matmul
            e.sem_inc(av_done, FREE)
            e.wait_ge(w_loaded, W_ALL)
            e.wait_ge(setup_pool, NPOOL)
            for h in range(H0):
                r, p = 64 * (h % 2), h // 2
                ins = mm(st[:, 2 * (h % 2) + h // 4, (p % 2) * 128:(p % 2) * 128 + 128],
                         raw["wqT0"][r:r + 64, p * 128:(p + 1) * 128], raw["wkT0"][r:r + 64, p * 128:(p + 1) * 128],
                         start=True, stop=True)
            ins.then_inc(setup_mm, 1)
            mm(misc[0:RANK, 0:128], raw["fastT"][0:RANK, :], raw["v"][0:RANK, :], start=True, stop=True).then_inc(setup_mm, 1)
            e.wait_ge(setup_dve, S_LR)
            for k in range(4):
                ins = mm(mx[:, 0, k * 128:(k + 1) * 128], raw["uT"][0:RANK, k * 128:(k + 1) * 128],
                         low_rank[0:RANK, :], start=True, stop=True)
            ins.then_inc(setup_mm, 1)
            e.wait_ge(setup_dve, S_FC)
            for k in range(4):
                ins = e.transpose(av[:, k * 128:(k + 1) * 128], t_a[:, k * 128:(k + 1) * 128], ident[:, :])
            ins.then_inc(setup_mm, 1)
            e.wait_ge(setup_dve, S_PR)
            for k in range(4):
                ins = e.transpose(mx[:, 1, k * 128:(k + 1) * 128], t_b[:, k * 128:(k + 1) * 128], ident[:, :])
            ins.then_inc(setup_mm, 1)
            e.wait_ge(setup_dve, NSETUP)
            e.wait_ge(setup_pool, NPOOL + 2)

            def misc_free(name):
                e.wait_ge(misc_used, b * NM + M[name] + FREE)

            def bank_free(k):
                if k - 4 in BY_ACT:
                    e.wait_ge(pj_used_act, b * NPA + BY_ACT.index(k - 4) + 1)
                else:
                    e.wait_ge(pj_used_dve, b * NPD + BY_DVE.index(k - 4) + 1)

            def units_done(k):
                e.wait_ge(pj_used_act, b * NPA + sum(u < k for u in BY_ACT))
                e.wait_ge(pj_used_dve, b * NPD + sum(u < k for u in BY_DVE))

            def transpose_xn(name):
                e.wait_ge(xn_ready, b * NX + NORMS.index(name) + 1)
                misc_free(name)
                for q in range(QT):
                    ins = e.transpose(misc[:, q * 128:(q + 1) * 128], xn[:, q, :], ident[:, :])
                ins.then_inc(misc_ready, 1)

            def max_unit(base, layer, g, n):
                i = base + g * 32 + n
                hq, u = n // 4, n % 4
                h, q = hq // QT, hq % QT
                cols = slice(MXO[u], MXO[u] + MXW[u])
                e.wait_ge(mx_used, b * NU + max(i - 1, 0) + FREE)
                if layer == 0:
                    w, m = q0_hi[:, 4 * g + h, q * 128:(q + 1) * 128], ctx_hi[:, cols]
                else:
                    w, m = q1[:, g, h, q * 128:(q + 1) * 128], k1[:, g, cols]
                mm(mx[:, i % 2, 0:MXW[u]], w, m, start=True, stop=True).then_inc(mx_ready, 1)

            def shift_t(gg, name=None, seen=0):
                e.wait_ge(negmax_ready, b * NG + (seen + gg + 1))
                misc_free(name or f"shift{gg}")
                for q in range(QT):
                    if gg < G0:
                        ins = e.transpose(misc[0:32, q * 128:(q + 1) * 128], mx0[:, q, :], ident[:, :])
                    else:
                        ins = e.transpose(misc[:, q * 128:(q + 1) * 128], mx1[:, q, :], ident[:, :])
                ins.then_inc(misc_ready, 1)

            def values(i, between=lambda: None):
                t = i % NT
                if t < TILE1:
                    g, c = divmod(t, C)
                    gg = g
                elif t < TILE3:
                    g, c = divmod(t - TILE1, C)
                    gg = G0 + g
                else:
                    g, c = divmod(t - TILE3, 2)
                    gg = G0 + G1 + g
                e.wait_ge(p_ready, b * NT + i + 1 + FREE)
                if c == 0:
                    e.wait_ge(av_copied, b * NG + (i // NT * NG + gg + FREE))
                pr = probs[:, i % 2, :]
                for j in range(4):
                    if j == 2:
                        between()
                    if t < TILE1:
                        n = ROWS[c]
                        h = 4 * g + j
                        ins = mm(av[64 * (j % 2):64 * (j % 2) + 64, (j // 2) * T:(j // 2 + 1) * T],
                                 v0[0:n, c, h * HD0:(h + 1) * HD0], pr[0:n, j * T:(j + 1) * T],
                                 start=(c == 0 and j < 2), stop=(c == C - 1), skip_group_check=True)
                    elif t < TILE3:
                        n = ROWS[c]
                        ins = mm(av[32 * j:32 * j + 32, 0:T], v1[0:n, c, 4 * g + j, :], pr[0:n, j * T:(j + 1) * T],
                                 start=(c == 0), stop=(c == C - 1), tile_position=(0, 32 * j), skip_group_check=True)
                    elif c == 0:
                        ins = mm(av[32 * j:32 * j + 32, 0:T], v3[:, 0, 4 * g + j, :], pr[:, j * T:(j + 1) * T],
                                 start=True, stop=False, tile_position=(0, 32 * j), skip_group_check=True)
                    else:
                        ins = mm(av[32 * j:32 * j + 32, 128:T], v3[:, 1, 4 * g + j, :], pr[:, j * 128:(j + 1) * 128],
                                 start=False, stop=True, tile_position=(0, 32 * j), skip_group_check=True)
                ins.then_inc(av_done, 1)

            def norm(gg):
                misc_free(f"norm{gg}")
                if gg < G0:
                    e.wait_ge(sum_done, b * TILE1 + (gg + 1) * C)
                    for j in range(4):
                        n = ROWS[0]
                        ins = mm(misc[64 * (j % 2):64 * (j % 2) + 64, (j // 2) * T:(j // 2 + 1) * T],
                                 ones[0:n, :], prob_sum[0:n, gg, j * T:(j + 1) * T],
                                 start=True, stop=True, skip_group_check=True)
                else:
                    e.wait_ge(av_copied, b * NG + gg + 1 + FREE)
                    for q in range(QT):
                        ins = e.transpose(misc[:, q * 128:(q + 1) * 128], av_sb[:, 0, q * 128:(q + 1) * 128], ident[:, :])
                ins.then_inc(misc_ready, 1)

            def turn_att(n):
                misc_free(f"attT{n}")
                for q in range(QT):
                    ins = e.transpose(misc[:, q * 128:(q + 1) * 128], att_q[:, q, :], ident[:, :])
                ins.then_inc(misc_ready, 1)

            def project(n, w):
                misc_free(f"wo{n}")
                for q in range(QT):
                    ins = mm(misc[:, q * 128:(q + 1) * 128], att_t[:, q * 128:(q + 1) * 128], w[:, :], start=True, stop=True)
                ins.then_inc(misc_ready, 1)

            def scores(i, layer, g, c, between=lambda: None):
                k = i % 2
                e.wait_ge(p_ready, b * NT + max(i - 1, 0) + FREE)
                if layer == 0:
                    n = ROWS[c]
                    keys = slice(OFF[c], OFF[c] + n)
                    for half in range(2):
                        if half == 1:
                            between()
                        o = st[0:n, 2 * k + half, :]
                        hs = slice(4 * g + 2 * half, 4 * g + 2 * half + 2)
                        mm(o, ctx_hi[:, keys], q0_hi[:, hs, :], start=True, stop=False)
                        mm(o, ctx_hi[:, keys], q0_lo[:, hs, :], start=False, stop=False)
                        mm(o, ctx_lo[:, keys], q0_hi[:, hs, :], start=False, stop=False)
                        ins = mm(o, ones_bf[:, 0:n], neg_shift[:, g, 2 * half:2 * half + 2, :], start=False, stop=True)
                elif layer == 1:
                    n = ROWS[c]
                    for half in range(2):
                        if half == 1:
                            between()
                        ins = mm(st[0:n, 2 * k + half, :], k1[:, g, OFF[c]:OFF[c] + n],
                                 q1[:, g, 2 * half:2 * half + 2, :], start=True, stop=True)
                elif c == 0:
                    for half in range(2):
                        o = st[:, 2 * k + half, :]
                        mm(o, ident_bf[:, :], mask_k[:, :].unsqueeze(1).broadcast_to([128, 2, T]), start=True, stop=False)
                        ins = mm(o, k3[:, g, 0:128], q1[:, g, 2 * half:2 * half + 2, :], start=False, stop=True)
                else:
                    o = st[:, 2 * k, :]
                    mm(o, ident_bf[:, :], mask_k[:, 0:128].unsqueeze(1).broadcast_to([128, 4, 128]), start=True, stop=False)
                    ins = mm(o, k3[:, g, 128:256], q1[:, g, :, 128:256], start=False, stop=True)
                ins.then_inc(st_ready, 1)

            def k1_unit(j):
                k = K1[j]
                if j >= 4:
                    bank_free(k)
                g, u = divmod(j, 4)
                cols = slice(MXO[u], MXO[u] + MXW[u])
                w = slice(g * 128, (g + 1) * 128)
                o = st[:, k % 4, 0:MXW[u]]
                mm(o, wk1[:, 0, w], ctx_hi[:, cols], start=True, stop=False)
                mm(o, wk1[:, 0, w], ctx_lo[:, cols], start=False, stop=False)
                mm(o, wk1[:, 1, w], ctx_hi[:, cols], start=False, stop=False)
                mm(o, aug_w[:, :], aug_x[:, cols], start=False, stop=True).then_inc(pj_ready, 1)

            def v1_unit(j):
                k = V1[j]
                bank_free(k)
                c0, c1 = V1_UNITS[j]
                for c in range(c0, c1):
                    n, keys = ROWS[c], slice(OFF[c], OFF[c + 1])
                    o = st[0:n, k % 4, (c - c0) * 128:(c - c0 + 1) * 128]
                    mm(o, ctx_hi[:, keys], wv1[:, 0, :], start=True, stop=False)
                    mm(o, ctx_hi[:, keys], wv1[:, 1, :], start=False, stop=False)
                    ins = mm(o, ctx_lo[:, keys], wv1[:, 0, :], start=False, stop=True)
                ins.then_inc(pj_ready, 1)

            def attention(layer, groups, tile0, group0, unit0):
                behind = K - 1 if layer == 0 else None
                for t in range(K if layer == 0 else 0, groups * C):
                    g, c = divmod(t, C)
                    if c == 0:
                        e.wait_ge(shift_ready, b * NG + group0 + g + 1)
                    units = units_at(layer, t)

                    def some(part):
                        for m, n in enumerate(units):
                            if m * 5 // len(units) == part:
                                max_unit(unit0, layer, 1 + n // 32, n % 32)

                    some(0)
                    scores(tile0 + t, layer, g, c, lambda: some(1))
                    some(2)
                    if c == 1 and g > 0:
                        norm(group0 + g - 1)
                    if behind is None:
                        some(3)
                    else:
                        values(behind, lambda: some(3))
                    behind = tile0 + t
                    some(4)
                    if c == C - 2 and g + 1 < groups:
                        shift_t(group0 + g + 1)
                    if layer == 1 and g + 1 == groups and c == C - 3:
                        transpose_xn("xnT0")
                values(behind)
                norm(group0 + groups - 1)

            def turn_context(units):
                for k, (c0, c1) in zip(units, CTX_UNITS):
                    for c in range(c0, c1):
                        n = ROWS[c]
                        ins = e.transpose(st[:, k % 4, OFF[c] - OFF[c0]:OFF[c] - OFF[c0] + n], ctx_raw[0:n, c, :], ident[0:n, 0:n])
                    ins.then_inc(pj_ready, 1)

            def q0_units(units):
                for i, k in enumerate(units):
                    bank_free(k)
                    for h in (2 * i, 2 * i + 1):
                        ins = mm(st[:, k % 4, (h % 2) * T:(h % 2 + 1) * T], m_qk[:, h, :], xnT[:, :], start=True, stop=True)
                    ins.then_inc(pj_ready, 1)

            def v0_unit(k, c):
                bank_free(k)
                n, keys = ROWS[c], slice(OFF[c], OFF[c + 1])
                o = st[0:n, k % 4, :]
                mm(o, ctx_hi[:, keys], wv0[:, 0, :], start=True, stop=False)
                mm(o, ctx_hi[:, keys], wv0[:, 1, :], start=False, stop=False)
                mm(o, ctx_lo[:, keys], wv0[:, 0, :], start=False, stop=True).then_inc(pj_ready, 1)

            b = 0
            e.wait_ge(ctx_loaded, 32)
            turn_context(AHEAD["ctx"])
            transpose_xn("xnT_ahead")
            e.wait_ge(misc_used, M["xnT_ahead"] + 1 + FREE)
            q0_units(AHEAD["qp"])
            e.wait_ge(hi_ready, 8)
            for c, k in enumerate(AHEAD["v0"]):
                v0_unit(k, c)
                for n in range(32 * c // C, 32 * (c + 1) // C):
                    max_unit(0, 0, 0, n)

            def ahead(t, i):
                scores(i, 0, 0, t)
                if t > 0:
                    values(i - 1)

            shift_t(0, "shift_ahead")
            units_done(B_U)
            e.wait_ge(shift_ready, 1)
            for t in range(K):
                ahead(t, t)

            with e.Fori(0, B) as b:
                attention(0, G0, 0, 0, 0)
                e.wait_ge(p_ready, b * NT + TILE1 + FREE)
                e.wait_ge(aug_ready, b + 1)
                for j in range(4):
                    k1_unit(j)
                e.wait_ge(att_ready, b * NG + G0 + FREE)
                misc_free("wo0")
                for q in range(QT):
                    for p in range(4):
                        ins = mm(misc[:, q * 128:(q + 1) * 128], att[:, p, q * 128:(q + 1) * 128], wo0[:, p, :],
                                 start=(p == 0), stop=(p == 3))
                ins.then_inc(misc_ready, 1)
                v1_unit(0)
                v1_unit(1)
                k1_unit(4)
                k1_unit(5)
                transpose_xn("xnT1")
                e.wait_ge(misc_used, b * NM + M["xnT1"] + 1 + FREE)
                for i, k in enumerate(UP):
                    bank_free(k)
                    for j in range(2):
                        m = 2 * i + j
                        ins = mm(st[:, k % 4, j * T:(j + 1) * T], wfc[:, m * 128:(m + 1) * 128], xnT[:, :], start=True, stop=True)
                    ins.then_inc(pj_ready, 1)
                k1_unit(6)
                k1_unit(7)
                e.wait_ge(pj_used_dve, b * NPD + BY_DVE.index(UP[1]) + 1)
                misc_free("ffn")
                for q in range(QT):
                    for m in range(4):
                        ins = mm(misc[:, q * 128:(q + 1) * 128], relu2[:, m, q * 128:(q + 1) * 128], wpr[:, m, :],
                                 start=(m == 0), stop=(m == 3))
                ins.then_inc(misc_ready, 1)
                v1_unit(2)
                v1_unit(3)
                k1_unit(8)
                k1_unit(9)
                transpose_xn("xnT2")
                e.wait_ge(misc_used, b * NM + M["xnT2"] + 1 + FREE)
                for i, k in enumerate(Q1):
                    bank_free(k)
                    for j in range(2):
                        g = 2 * i + j
                        ins = mm(st[:, k % 4, j * T:(j + 1) * T], wq1[:, g * 128:(g + 1) * 128], xnT[:, :], start=True, stop=True)
                    ins.then_inc(pj_ready, 1)
                for j in range(10, 16):
                    k1_unit(j)
                e.wait_ge(q_ready, b * 3 + 1)
                e.wait_ge(q_ready_act, b * 2 + 1)
                units_done(L_U)
                for m in range(NW):
                    hq, pair = divmod(m, 2)
                    h, q = hq // QT, hq % QT
                    e.wait_ge(wide_used, b * NW + max(m - 1, 0) + FREE)
                    for u in range(2):
                        cols = slice((2 * pair + u) * (WIDE - 2), (2 * pair + u) * (WIDE - 2) + WIDE)
                        ins = mm(st[:, 2 * (m % 2) + u, 0:WIDE], q1[:, 0, h, q * 128:(q + 1) * 128], k1[:, 0, cols], start=True, stop=True)
                    ins.then_inc(wide_ready, 1)
                shift_t(G0)
                units_done(L_U)
                attention(1, G1, TILE1, G0, UNIT1)
                e.wait_ge(ctx_loaded, b * 32 + 64)
                e.wait_ge(p_ready, b * NT + TILE3 + FREE)
                turn_context(NEXT["ctx"])
                e.wait_ge(att_ready, b * NG + G0 + G1 + FREE)
                turn_att(1)
                project(1, wo1)
                q0_units(NEXT["qp"])
                e.wait_ge(hi_ready, b * NHI + NHI + 8)
                for c in range(V0_EARLY):
                    v0_unit(NEXT["v0"][c], c)
                transpose_xn("xnT3")
                e.wait_ge(misc_used, b * NM + M["xnT3"] + 1 + FREE)
                for units, w in ((Q3, wq3), (K3, wk3)):
                    for i, k in enumerate(units):
                        bank_free(k)
                        for j in range(2):
                            g = 2 * i + j
                            ins = mm(st[:, k % 4, j * T:(j + 1) * T], w[:, g * 128:(g + 1) * 128], xnT[:, :], start=True, stop=True)
                        ins.then_inc(pj_ready, 1)
                bank_free(V3)
                for q in range(2):
                    ins = mm(st[:, V3 % 4, q * 128:(q + 1) * 128], xnT[:, q * 128:(q + 1) * 128], wv3[:, :], start=True, stop=True)
                ins.then_inc(pj_ready, 1)
                for c in range(V0_EARLY, C):
                    v0_unit(NEXT["v0"][c], c)
                e.wait_ge(q_ready, b * 3 + 3)
                e.wait_ge(q_ready_act, b * 2 + 2)
                for g in range(G1):
                    for n in range(3):
                        i = UNIT3 + 3 * g + n
                        e.wait_ge(mx_used, b * NU + i - 1 + FREE)
                        if n == 0:
                            mm(mx[:, i % 2, :], ident_bf[:, :], mask_q[:, 128:256].unsqueeze(1).broadcast_to([128, 4, 128]),
                               start=True, stop=False, skip_group_check=True)
                            for j in range(4):
                                ins = mm(mx[:, i % 2, j * 128:(j + 1) * 128], q1[:, g, j, 0:128], k3[:, g, 0:128],
                                         start=False, stop=True, skip_group_check=True)
                        else:
                            mm(mx[:, i % 2, :], ident_bf[:, :], mask_q[:, :].unsqueeze(1).broadcast_to([128, 2, T]),
                               start=True, stop=False, skip_group_check=True)
                            for j in range(2):
                                ins = mm(mx[:, i % 2, j * T:(j + 1) * T], q1[:, g, 2 * (n - 1) + j, 128:256], k3[:, g, :],
                                         start=False, stop=True, skip_group_check=True)
                        ins.then_inc(mx_ready, 1)
                    shift_t(G0 + G1 + g)
                units_done(len(UNITS))
                behind = None
                for g in range(G1):
                    e.wait_ge(shift_ready, b * NG + G0 + G1 + g + 1)
                    for c in range(2):
                        i = TILE3 + 2 * g + c
                        scores(i, 3, g, c)
                        if behind is not None:
                            values(behind)
                        for n in range(8 * g + 4 * c, 8 * g + 4 * c + 2):
                            max_unit(NU, 0, 0, n)
                        if behind is not None and c == 0:
                            norm(G0 + G1 + g - 1)
                        for n in range(8 * g + 4 * c + 2, 8 * g + 4 * c + 4):
                            max_unit(NU, 0, 0, n)
                        behind = i
                values(behind)
                norm(NG - 1)
                shift_t(0, seen=NG)
                e.wait_ge(att_ready, b * NG + NG + FREE)
                turn_att(3)
                e.wait_ge(shift_ready, b * NG + NG + 1)
                ahead(0, NT)
                project(3, wp3)
                for t in range(1, 4):
                    ahead(t, NT + t)
                transpose_xn("xnT4")
                ahead(4, NT + 4)
                misc_free("router")
                for q in range(QT):
                    ins = mm(misc[:, q * E:(q + 1) * E], xnT[:, q * 128:(q + 1) * 128], gate_w[:, :], start=True, stop=True)
                ins.then_inc(misc_ready, 1)
                ahead(5, NT + 5)

        @block.scalar
        def _(e):
            e.sem_inc(p_ready, FREE)
            e.sem_inc(kept, FREE)
            def exps(i, n, width, scale):
                e.wait_ge(st_ready, b * NT + i + 1)
                e.wait_ge(av_done, b * NT + max(i - 1, 0) + FREE)
                if 2 <= i % NT < TILE1:
                    e.wait_ge(sum_done, b * TILE1 + (i // NT * TILE1 + i % NT - 1))
                elif TILE1 <= i < TILE1 + 2:
                    e.wait_ge(sum_done, b * TILE1 + TILE1)
                e.activation(probs[0:n, i % 2, 0:width],
                             st[0:n, 2 * (i % 2):2 * (i % 2) + 2, :].rearrange("p a n -> p (a n)")[:, 0:width],
                             ACT.Exp, scale=scale).then_inc(p_ready, 1)

            def copy_xnT(name):
                e.wait_ge(misc_ready, b * NM + M[name] + 1)
                if name == "xnT1":
                    e.wait_ge(kept, b * 32 + FREE)
                e.copy(xnT[:, :], misc[:, 0:T]).then_inc(misc_used, 1)

            def copy_att(n):
                e.wait_ge(misc_ready, b * NM + M[f"attT{n}"] + 1)
                e.copy(att_t, misc[:, 0:T]).then_inc(misc_used, 1)

            def high_k1(j0, j1):
                for j in range(j0, j1):
                    g, u = divmod(j, 4)
                    e.wait_ge(pj_ready, b * NP + K1[j] + 1)
                    e.copy(k1[:, g, MXO[u]:MXO[u] + MXW[u]], st[:, K1[j] % 4, 0:MXW[u]]).then_inc(hi_ready, 1)

            def take_v1(j):
                c0, c1 = V1_UNITS[j]
                n = ROWS[c0]
                e.wait_ge(pj_ready, b * NP + V1[j] + 1)
                e.copy(v1[0:n, c0:c1, :, 0:HD1], st[0:n, V1[j] % 4, 0:(c1 - c0) * 128].rearrange(
                    "p (c h d) -> p c h d", h=H1, d=HD1)).then_inc(pj_used_act, 1)

            def block_diagonal(n):
                e.wait_ge(slots_ready, b * 2 + n)
                for j in ACT_SLOTS:
                    r = slice(32 * j, 32 * j + 32)
                    ins = e.copy(q1[r, :, j, :], xb[r, 0, :, :])
                ins.then_inc(q_ready_act, 1)

            def slots(k, pair, bias, which):
                e.wait_ge(pj_ready, b * NP + k + 1)
                for j in range(2):
                    g = 2 * pair + j
                    high = hi_tmp if which == 0 else k3
                    e.activation(xb[:, which, g, :], st[:, k % 4, j * T:(j + 1) * T], ACT.Identity, bias=bias[:, g:g + 1])
                    ins = e.activation(high[:, g, :], st[:, k % 4, j * T:(j + 1) * T], ACT.Identity, bias=bias[:, g:g + 1])
                ins.then_inc(pj_used_act, 1)

            def high_ctx(units):
                for k, (c0, c1) in zip(units, CTX_UNITS):
                    e.wait_ge(pj_ready, b * NP + k + 1)
                    w = OFF[c1] - OFF[c0]
                    ins = e.copy(ctx_hi[:, OFF[c0]:OFF[c1]], st[:, k % 4, 0:w])
                    if c1 == C:
                        ins = e.copy(ctx_hi[:, S:SP], st[:, k % 4, w - 1:w])
                    ins.then_inc(hi_ready, 1)

            def high_q0(units):
                for i, k in enumerate(units):
                    e.wait_ge(pj_ready, b * NP + k + 1)
                    e.copy(q0_hi[:, 2 * i:2 * i + 2, :].rearrange("p h t -> p (h t)"), st[:, k % 4, :]).then_inc(hi_ready, 1)

            def take_v0(k, c):
                e.wait_ge(pj_ready, b * NP + k + 1)
                e.copy(v0[0:ROWS[c], c, :], st[0:ROWS[c], k % 4, :]).then_inc(pj_used_act, 1)

            b = 0
            high_ctx(AHEAD["ctx"])
            copy_xnT("xnT_ahead")
            high_q0(AHEAD["qp"])
            for c, k in enumerate(AHEAD["v0"]):
                take_v0(k, c)
            for t in range(K):
                exps(t, ROWS[t], 4 * T, SCALE0)

            with e.Fori(0, B) as b:
                for i in range(K, TILE1):
                    exps(i, ROWS[i % C], 4 * T, SCALE0)
                high_k1(0, 4)
                take_v1(0)
                take_v1(1)
                high_k1(4, 6)
                copy_xnT("xnT1")
                for i, k in enumerate(UP):
                    e.wait_ge(pj_ready, b * NP + k + 1)
                    e.activation(relu[:, 2 * i:2 * i + 2, :].rearrange("p m t -> p (m t)"), st[:, k % 4, :],
                                 ACT.Relu).then_inc(relu_ready, 1)
                high_k1(6, 8)
                take_v1(2)
                take_v1(3)
                high_k1(8, 10)
                copy_xnT("xnT2")
                slots(Q1[0], 0, bias_q1, 0)
                slots(Q1[1], 1, bias_q1, 0)
                high_k1(10, 16)
                block_diagonal(1)
                for i in range(TILE1, TILE3):
                    exps(i, ROWS[(i - TILE1) % C], 4 * T, SCALE1)
                    if i == TILE3 - 3:
                        copy_xnT("xnT0")
                high_ctx(NEXT["ctx"])
                copy_att(1)
                high_q0(NEXT["qp"])
                for c in range(V0_EARLY):
                    take_v0(NEXT["v0"][c], c)
                copy_xnT("xnT3")
                for i in range(2):
                    slots(Q3[i], i, bias_q3, 0)
                for i in range(2):
                    slots(K3[i], i, bias_k3, 1)
                block_diagonal(2)
                for c in range(V0_EARLY, C):
                    take_v0(NEXT["v0"][c], c)
                for i in range(TILE3, NT):
                    exps(i, 128, 4 * T if i % 2 == 0 else 4 * 128, SCALE1)
                copy_att(3)
                for t in range(4):
                    exps(NT + t, ROWS[t], 4 * T, SCALE0)
                copy_xnT("xnT4")
                e.wait_ge(misc_used, b * NM + M["xnT4"] + 1 + FREE)
                e.dma_start(h_keep[b], xnT[:, :]).then_inc(kept, 16)
                e.wait_ge(x4_ready, b + 1)
                e.dma_start(x_keep[b], xr[:, :, :].rearrange("p q d -> p (q d)")).then_inc(kept, 16)
                for t in range(4, K):
                    exps(NT + t, ROWS[t], 4 * T, SCALE0)
                e.wait_ge(gap_ready, b + 1)
                e.activation(gap[:, :], gap[:, :], ACT.Exp).then_inc(gap_exp, 1)
            e.wait_ge(kept, B * 32 + FREE)

        @block.vector
        def _(e):
            for freed in (misc_used, mx_used, wide_used, av_copied, att_ready):
                e.sem_inc(freed, FREE)
            def step(ins):
                ins.then_inc(setup_dve, 1)
                step.n += 1
                e.wait_ge(setup_dve, step.n)
            step.n = 0
            e.wait_ge(w_loaded, W_ALL)
            e.wait_ge(setup_pool, NPOOL)
            e.wait_ge(setup_mm, 2)
            for r in range(2):
                step(e.tensor_copy(m_qk[:, :, :].rearrange("p (a c r) d -> p a c r d", a=2, r=2)[:, :, :, r, :],
                                   st[:, 2 * r:2 * r + 2, 0:256].rearrange("p a (c d) -> p a c d", c=2)))
            step(e.tensor_scalar(low_rank[0:RANK, :], misc[0:RANK, 0:128], raw["gate"][0:RANK, :], None, ALU.mult))
            assert step.n == S_LR
            step(e.tensor_copy(ident_bf[:, :], ident[:, :]))
            step(e.tensor_copy(aug_w[:, :], raw["aug_w"]))
            step(e.tensor_copy(lens[:, :], lens_i[:, :]))
            for w, r in ((wv0, raw["wv0"]), (wk1, raw["wk1"]), (wv1, raw["wv1"])):
                step(e.tensor_copy(w[:, 0, :], r))
                step(e.tensor_tensor(w[:, 1, :], r, w[:, 0, :].bitcast(F32), ALU.subtract))

            def ternary(dst, src, scale):
                width = src.shape[-1]
                step(e.tensor_reduce(scale, src, AX.X, ALU.add, apply_absolute_value=True))
                step(e.tensor_scalar(scale, scale, 1.0 / width, 1e-5, ALU.mult, ALU.max))
                step(e.tensor_scalar(t_c[:, 8:9], scale, 0.5, None, ALU.mult))
                step(e.tensor_scalar(t_c[:, 9:10], scale, -0.5, None, ALU.mult))
                step(e.tensor_scalar(dst, src, t_c[:, 9:10], None, ALU.is_lt))
                step(e.scalar_tensor_tensor(dst, src, t_c[:, 8:9], dst, ALU.is_gt, ALU.subtract))
                step(e.tensor_tensor(dst, dst, src, ALU.subtract))
                step(e.tensor_tensor(dst, dst, src, ALU.add))
                step(e.tensor_scalar(dst, dst, scale, None, ALU.mult))

            for k in range(4):
                ternary(t_a[:, k * 128:(k + 1) * 128], raw["wfc"][:, k * 128:(k + 1) * 128], t_c[:, k:k + 1])
            e.wait_ge(setup_mm, 3)
            step(e.tensor_tensor(t_a, t_a, mx[:, 0, :], ALU.add))
            assert step.n == S_FC, step.n
            ternary(t_b, raw["wproj"], t_c[:, 4:5])
            assert step.n == S_PR, step.n
            e.wait_ge(setup_mm, 4)
            step(e.tensor_copy(wfc[:, :], av[:, :]))
            e.wait_ge(setup_mm, 5)
            step(e.tensor_copy(wpr[:, :, :].rearrange("p m d -> p (m d)"), mx[:, 1, :]))
            assert step.n == NSETUP, step.n

            def link(ins):
                ins.then_inc(chain, 1)
                link.n += 1
                e.wait_ge(chain, b * ND + link.n)
            link.n = 0

            def layernorm(x, gain=None, offset=None, to=xn):
                for q in range(QT):
                    ins = e.bn_stats(stats[:, q, :], x[:, q, :])
                link(ins)
                e.sem_inc(idle, 1)
                for q in range(QT):
                    ins = e.bn_aggr(mv[:, q, :], stats[:, q, :])
                link(ins)
                link(e.tensor_scalar(veps[:, :], mv[:, :, 1], EPS, None, ALU.add))
                e.tensor_scalar(nveps[:, :], veps[:, :], -0.5, None, ALU.mult)
                link(e.tensor_scalar(rt[:, :].bitcast(I32), veps[:, :].bitcast(I32), 1, None, ALU.logical_shift_right))
                link(e.tensor_scalar(rs[:, :].bitcast(I32), rt[:, :].bitcast(I32), -1.0, RSQRT_SEED, ALU.mult, ALU.add))
                for _ in range(3):
                    for q in range(QT):
                        ins = e.scalar_tensor_tensor(rt[:, q:q + 1], rs[:, q:q + 1], nveps[:, q:q + 1], rs[:, q:q + 1], ALU.mult, ALU.mult)
                    link(ins)
                    link(e.scalar_tensor_tensor(rs[:, :], rt[:, :], 1.5, rs[:, :], ALU.add, ALU.mult))
                for q in range(QT):
                    ins = e.tensor_scalar(to[:, q, :], x[:, q, :], mv[:, q, 0:1], rs[:, q:q + 1], ALU.subtract, ALU.mult)
                    if gain is not None or to is not xn:
                        link(ins)
                if to is not xn:
                    return
                if gain is not None:
                    link(e.tensor_tensor(xn[:, :, :], xn[:, :, :], gain.unsqueeze(1).broadcast_to([128, QT, D]), ALU.mult))
                    ins = e.tensor_tensor(xn[:, :, :], xn[:, :, :], offset.unsqueeze(1).broadcast_to([128, QT, D]), ALU.add)
                ins.then_inc(xn_ready, 1)

            def max_unit(i, n):
                e.wait_ge(mx_ready, b * NU + i + 1)
                hq, u = divmod(n, 4)
                e.tensor_reduce(mpart[:, hq, u:u + 1], mx[:, i % 2, 0:MXW[u]], AX.X, ALU.max).then_inc(mx_used, 1)

            def negmax(gg, i_end, used=mx_used, a_batch=NU):
                e.wait_ge(used, b * a_batch + i_end + FREE)
                if gg < G0:
                    o = mx0[:, :, 0:4].rearrange("p q h -> p h q")
                else:
                    o = mx1[:, :, :].rearrange("p q (j s) -> p j q s", s=32)[:, :, :, 25]
                e.tensor_reduce(o, mpart[:, :, :].rearrange("p (h q) u -> p h q u", h=4), AX.X, ALU.max,
                                negate=True).then_inc(negmax_ready, 1)

            def shift(gg, name=None):
                e.wait_ge(misc_ready, b * NM + M[name or f"shift{gg}"] + 1)
                if gg < G0:
                    link(e.tensor_tensor(neg_shift[0:32, gg, :, :], misc[0:32, 0:T].unsqueeze(1).broadcast_to([32, 4, T]),
                                         ident[0:32, 0:4].unsqueeze(2).broadcast_to([32, 4, T]), ALU.mult))
                else:
                    g = (gg - G0) % G1
                    for j in range(4):
                        r = slice(32 * j, 32 * j + 32)
                        ins = e.tensor_tensor(q1[r, g, j, :], misc[r, 0:T], q1[r, g, j, :].bitcast(F32), ALU.add)
                    link(ins)
                e.sem_inc(shift_ready, 1)
                e.sem_inc(misc_used, 1)

            def av_copy(gg):
                last = C * (gg + 1) if gg < G0 + G1 else TILE3 + 2 * (gg - G0 - G1 + 1)
                e.wait_ge(av_done, b * NT + last + FREE)
                w = 2 if gg < G0 else 1
                e.wait_ge(att_ready, b * NG + gg + FREE)
                e.tensor_copy(av_sb[:, 0:w, :].rearrange("p a t -> p (a t)"), av[:, 0:w * T]).then_inc(av_copied, 1)

            def norm(gg):
                e.wait_ge(misc_ready, b * NM + M[f"norm{gg}"] + 1)
                if gg < G0:
                    e.reciprocal(rden[:, :, :].rearrange("p a t -> p (a t)"), misc[:, 0:2 * T]).then_inc(misc_used, 1)
                    e.wait_ge(misc_used, b * NM + M[f"norm{gg}"] + 1 + FREE)
                    e.wait_ge(av_copied, b * NG + gg + 1 + FREE)
                    e.tensor_tensor(att[:, 2 * gg:2 * gg + 2, :], av_sb[:, :, :], rden[:, :, :], ALU.mult).then_inc(att_ready, 1)
                else:
                    g = (gg - G0) % G1
                    o = att_q[:, :, 32 * g:32 * g + 32].rearrange("p q (j d) -> p q j d", j=4)
                    turned = misc[:, 0:T].rearrange("p (q j s) -> p q j s", q=QT, j=4)
                    link(e.reciprocal(rsum[:, :, :], turned[:, :, :, HD1]))
                    e.tensor_tensor(o, turned[:, :, :, 0:HD1], rsum[:, :, :].unsqueeze(3).broadcast_to([128, QT, 4, HD1]),
                                    ALU.mult).then_inc(att_ready, 1)
                    e.wait_ge(att_ready, b * NG + gg + 1 + FREE)
                    e.sem_inc(misc_used, 1)

            def attention(layer, groups, group0, unit0):
                for t in range(K if layer == 0 else 0, groups * C):
                    g, c = divmod(t, C)
                    for n in units_at(layer, t):
                        if n and n % 32 == 0:
                            e.wait_ge(negmax_ready, b * NG + group0 + n // 32 + 1)
                        max_unit(unit0 + 32 + n, n % 32)
                        if n % 32 == 31:
                            negmax(group0 + 1 + n // 32, unit0 + 32 + n + 1)
                    if c == C - 2 and g + 1 < groups:
                        shift(group0 + g + 1)
                    if c == 0 and g > 0:
                        av_copy(group0 + g - 1)
                    if c == 1 and g > 0:
                        norm(group0 + g - 1)
                if layer == 1:
                    e.wait_ge(x_loaded, b * 16 + 32)
                    layernorm(x_in)
                av_copy(group0 + groups - 1)
                norm(group0 + groups - 1)

            def low_k1(j0, j1):
                for j in range(j0, j1):
                    g, u = divmod(j, 4)
                    kk = k1[:, g, MXO[u]:MXO[u] + MXW[u]]
                    e.wait_ge(hi_ready, b * NHI + 8 + j + 1)
                    e.scalar_tensor_tensor(kk, kk.bitcast(F32), low_k, st[:, K1[j] % 4, 0:MXW[u]],
                                           ALU.mult, ALU.add).then_inc(pj_used_dve, 1)

            def residual(name, base):
                e.wait_ge(misc_ready, b * NM + M[name] + 1)
                return e.tensor_tensor(xr[:, :, :], misc[:, 0:T].rearrange("p (q d) -> p q d", q=QT), base, ALU.add)

            def low_ctx(units, seen):
                for i, (k, (c0, c1)) in enumerate(zip(units, CTX_UNITS)):
                    e.wait_ge(hi_ready, b * NHI + seen + i + 1)
                    w = OFF[c1] - OFF[c0]
                    ins = e.tensor_tensor(ctx_lo[:, OFF[c0]:OFF[c1]], st[:, k % 4, 0:w], ctx_hi[:, OFF[c0]:OFF[c1]].bitcast(F32), ALU.subtract)
                    if c1 == C:
                        ins = e.tensor_tensor(ctx_lo[:, S:SP], st[:, k % 4, w - 1:w], ctx_hi[:, S:SP].bitcast(F32), ALU.subtract)
                    ins.then_inc(pj_used_dve, 1)

            def low_q0(units, seen):
                for i, k in enumerate(units):
                    e.wait_ge(hi_ready, b * NHI + seen + 4 + i + 1)
                    e.tensor_tensor(q0_lo[:, 2 * i:2 * i + 2, :].rearrange("p h t -> p (h t)"), st[:, k % 4, :],
                                    q0_hi[:, 2 * i:2 * i + 2, :].rearrange("p h t -> p (h t)").bitcast(F32),
                                    ALU.subtract).then_inc(pj_used_dve, 1)

            b = 0
            e.wait_ge(x_loaded, 16)
            layernorm(x_in)
            low_ctx(AHEAD["ctx"], 0)
            low_q0(AHEAD["qp"], 0)
            for n in range(32):
                max_unit(n, n)
            negmax(0, 32)
            shift(0, "shift_ahead")
            ahead = link.n

            with e.Fori(0, B) as b:
                e.tensor_scalar(aug_x[0:1, :], key_id[:, :], lens[:, bass.ds(b, 1)], MASK, ALU.is_ge, ALU.mult).then_inc(aug_ready, 1)
                attention(0, G0, 0, 0)
                low_k1(0, 4)
                e.wait_ge(kept, b * 32 + FREE)
                e.wait_ge(xbo_ready, b + 1)
                residual("wo0", x_bo[:, :, :]).then_inc(misc_used, 1)
                e.wait_ge(misc_used, b * NM + M["wo0"] + 1 + FREE)
                layernorm(xr)
                low_k1(4, 6)
                for k in range(2):
                    e.wait_ge(relu_ready, b * 2 + k + 1)
                    e.scalar_tensor_tensor(relu2[:, 2 * k:2 * k + 2, :].rearrange("p m t -> p (m t)"), st[:, UP[k] % 4, :], 0.0,
                                           relu[:, 2 * k:2 * k + 2, :].rearrange("p m t -> p (m t)"), ALU.max, ALU.mult).then_inc(pj_used_dve, 1)
                low_k1(6, 8)
                residual("ffn", xr[:, :, :]).then_inc(misc_used, 1)
                e.wait_ge(misc_used, b * NM + M["ffn"] + 1 + FREE)
                layernorm(xr)

                def block_diagonal(last, n):
                    e.wait_ge(pj_used_act, b * NPA + BY_ACT.index(last) + 1)
                    e.scalar_tensor_tensor(xb[:, 0, :, :], hi_tmp[:, :, :].bitcast(F32), low_q, xb[:, 0, :, :],
                                           ALU.mult, ALU.add).then_inc(slots_ready, 1)
                    e.wait_ge(slots_ready, b * 2 + n)
                    for j in DVE_SLOTS:
                        r = slice(32 * j, 32 * j + 32)
                        ins = e.tensor_copy(q1[r, :, j, :], xb[r, 0, :, :])
                    ins.then_inc(q_ready, 1)

                low_k1(8, 12)
                block_diagonal(Q1[1], 1)
                low_k1(12, 16)
                for m in range(NW):
                    hq, pair = divmod(m, 2)
                    e.wait_ge(wide_ready, b * NW + m + 1)
                    e.tensor_reduce(mpart[:, hq, 2 * pair:2 * pair + 2], st[:, 2 * (m % 2):2 * (m % 2) + 2, 0:WIDE],
                                    AX.X, ALU.max).then_inc(wide_used, 1)
                negmax(G0, NW, wide_used, NW)
                shift(G0)
                attention(1, G1, G0, UNIT1)
                low_ctx(NEXT["ctx"], NHI)
                residual("wo1", xr[:, :, :]).then_inc(misc_used, 1)
                e.wait_ge(misc_used, b * NM + M["wo1"] + 1 + FREE)
                layernorm(xr, to=x_bo)
                low_q0(NEXT["qp"], NHI)
                layernorm(x_bo, g1, b1)
                block_diagonal(Q3[-1], 2)
                e.wait_ge(pj_used_act, b * NPA + BY_ACT.index(K3[-1]) + 1)
                e.scalar_tensor_tensor(k3[:, :, :], k3[:, :, :].bitcast(F32), low_k, xb[:, 1, :, :], ALU.mult, ALU.add).then_inc(q_ready, 1)
                e.wait_ge(pj_ready, b * NP + V3 + 1)
                e.tensor_tensor(v3[:, :, :, 0:HD1], st[:, V3 % 4, 0:256].rearrange("p (c h d) -> p c h d", c=2, d=HD1),
                                bv.rearrange("p (h d) -> p h d", d=HD1).unsqueeze(1).broadcast_to([128, 2, H1, HD1]), ALU.add).then_inc(pj_used_dve, 1)
                for g in range(G1):
                    mj = mx1[:, :, :].rearrange("p q (j s) -> p q j s", s=32)
                    for n in range(3):
                        i = UNIT3 + 3 * g + n
                        e.wait_ge(mx_ready, b * NU + i + 1)
                        if n == 0:
                            e.tensor_reduce(mj[:, 0, :, 25], mx[:, i % 2, :].rearrange("p (j k) -> p j k", j=4), AX.X, ALU.max,
                                            negate=True).then_inc(mx_used, 1)
                        else:
                            e.tensor_reduce(mj[:, 1, 2 * (n - 1):2 * n, 25], mx[:, i % 2, :].rearrange("p (j k) -> p j k", j=2), AX.X, ALU.max,
                                            negate=True).then_inc(mx_used, 1)
                    e.wait_ge(mx_used, b * NU + UNIT3 + 3 * (g + 1) + FREE)
                    e.sem_inc(negmax_ready, 1)
                    shift(G0 + G1 + g)
                for g in range(G1):
                    for n in range(8 * g, 8 * g + 4):
                        max_unit(NU + n, n)
                    if g > 0:
                        norm(G0 + G1 + g - 1)
                    for n in range(8 * g + 4, 8 * g + 8):
                        max_unit(NU + n, n)
                    av_copy(G0 + G1 + g)
                negmax(0, NU + 32)
                norm(NG - 1)
                shift(0)
                link(e.tensor_tensor(x_bo[:, :, :], x_bo[:, :, :], bp.unsqueeze(1).broadcast_to([128, QT, D]), ALU.add))
                e.wait_ge(misc_ready, b * NM + M["wo3"] + 1)
                e.tensor_tensor(x_bo[:, :, :], misc[:, 0:T].rearrange("p (q d) -> p q d", q=QT), x_bo[:, :, :], ALU.add).then_inc(misc_used, 1)
                e.wait_ge(misc_used, b * NM + M["wo3"] + 1 + FREE)
                layernorm(x_bo, g2, b2)
                e.tensor_tensor(xr[:, :, :], xr[:, :, :], x_bo[:, :, :], ALU.add).then_inc(x4_ready, 1)
                e.wait_ge(misc_ready, b * NM + M["router"] + 1)
                e.tensor_tensor(logit[:, :, :], misc[:, 0:QT * E].rearrange("p (q x) -> p q x", q=QT),
                                gate_b.unsqueeze(1).broadcast_to([128, QT, E]), ALU.add).then_inc(misc_used, 1)
                e.wait_ge(misc_used, b * NM + M["router"] + 1 + FREE)
                e.sem_inc(idle, 1)
                for q in range(QT):
                    ins = e.max(top[:, q, :], logit[:, q, :])
                link(ins)
                e.sem_inc(idle, 1)
                for q in range(QT):
                    ins = e.max_index(top_i[:, q, :], top[:, q, :], logit[:, q, :])
                link(ins)
                link(e.tensor_copy(top_f[:, :, :], top_i[:, :, :]))
                e.tensor_tensor(gap[:, :], top[:, :, 1], top[:, :, 0], ALU.subtract).then_inc(gap_ready, 1)
                e.wait_ge(gap_exp, b + 1)
                link(e.tensor_scalar(wgt[:, :, 1], gap[:, :], 1.0, None, ALU.add))
                link(e.reciprocal(wgt[:, :, 0], wgt[:, :, 1]))
                link(e.tensor_tensor(wgt[:, :, 1], wgt[:, :, 0], gap[:, :], ALU.mult))
                for q in range(QT):
                    for t in range(2):
                        link(e.tensor_scalar(sel[:, q, t, :], expert_id[:, :], top_f[:, q, t:t + 1], wgt[:, q, t:t + 1], ALU.is_equal, ALU.mult))
                link(e.tensor_tensor(w_all[:, bass.ds(b * QT, QT), :], sel[:, :, 0, :], sel[:, :, 1, :], ALU.add))
                assert link.n - ahead == ND, link.n - ahead

        layers.close()
        experts(nc, a, out, x_keep, h_keep, w_all, ident)


def experts(nc, a, out, x_keep, h_keep, w_all, ident):
    with ExitStack() as ctx:
        def sb(name, shape, dt=F32):
            return ctx.enter_context(nc.sbuf_tensor(name, shape, dt))

        def sem(name):
            return ctx.enter_context(nc.semaphore(name))

        KB = HID // 128
        PIECES = 4
        EP = E // PIECES
        HIGH, LOW = 0, 1
        w1 = sb("w1", [128, 2, E, HID], F32R)
        w2 = sb("w2", [128, 2, E, HID], F32R)
        w1_raw = sb("w1_raw", [128, E, HID])
        w2_raw = sb("w2_raw", [128, E, HID])
        eb1 = sb("eb1", [128, E * KB])
        eb2 = sb("eb2", [128, E])
        h_raw = sb("h_raw", [128, 2, TT])
        h_t = sb("h_t", [128, 2, 2, TT], F32R)
        acc = sb("acc", [128, 2, 4, D])
        act_out = sb("act_out", [128, KB, TT])
        mid = sb("mid", [128, 2, 2, KB, TT], F32R)
        y_sb = sb("y_sb", [128, 2, TT])
        up = ctx.enter_context(nc.psum_tensor("up", [128, 4, TT], F32))
        y_t = ctx.enter_context(nc.psum_tensor("y_t", [128, 2, TT], F32))
        down = ctx.enter_context(nc.psum_tensor("down", [128, 2, 4, D], F32))

        bias_loaded = sem("bias_loaded")
        w1_loaded = [sem(f"w1_loaded{i}") for i in range(PIECES)]
        w2_loaded = [sem(f"w2_loaded{i}") for i in range(PIECES)]
        h_loaded = [sem(f"h_loaded{s}") for s in range(2)]
        acc_loaded = [sem(f"acc_loaded{s}") for s in range(2)]
        w_high = sem("w_high")
        w1_ready = sem("w1_ready")
        w2_ready = sem("w2_ready")
        h_high = sem("h_high")
        h_ready = sem("h_ready")
        up_ready = sem("up_ready")
        gelu_ready = sem("gelu_ready")
        low_ready = sem("low_ready")
        y_ready = sem("y_ready")
        y_taken = sem("y_taken")
        down_ready = sem("down_ready")
        down_used = sem("down_used")
        stored = [sem(f"stored{s}") for s in range(2)]
        SPARE = 2

        def chain_of_blocks(e, run):
            with e.Fori(0, NTT // 2 - 1) as pair:
                for s in range(2):
                    run(pair, s, False)
            run(NTT // 2 - 1, 0, False)
            run(NTT // 2 - 1, 1, True)

        with nc.Block() as block:
            @block.sync
            def _(e):
                def load_h(t, s):
                    e.dma_start(h_raw[:, s, :].rearrange("p (b t) -> p b t", b=2),
                                h_keep[bass.ds(t * 2, 2), :, :].rearrange("b d t -> d b t")).then_inc(h_loaded[s], 16)

                def load_acc(t, s):
                    e.dma_start(acc[:, s, :, :].rearrange("p (b q) d -> p b (q d)", b=2),
                                x_keep[bass.ds(t * 2, 2), :, :].rearrange("b p n -> p b n")).then_inc(acc_loaded[s], 16)

                load_h(0, 0)
                e.dma_start(eb1[:, :], a["eb1"]).then_inc(bias_loaded, 16)
                e.dma_start(eb2[:, :], a["eb2"]).then_inc(bias_loaded, 16)
                load_acc(0, 0)
                load_h(1, 1)
                load_acc(1, 1)
                with e.Fori(1, NTT // 2) as tt:
                    for s in range(2):
                        t = tt * 2 + s
                        e.wait_ge(up_ready, (t - 1) * (E * KB))
                        load_h(t, s)
                        e.wait_ge(stored[s], tt * 32)
                        load_acc(t, s)

            @block.gpsimd
            def _(e):
                for i in range(PIECES):
                    e.dma_start(w2_raw[:, i * EP:(i + 1) * EP, :].rearrange("p x (k d) -> p x k d", k=KB),
                                a["w2"][i * EP:(i + 1) * EP].rearrange("x (k p) d -> p x k d", p=128)).then_inc(w2_loaded[i], 16)
                with e.Fori(0, NTT // 2) as tt:
                    for s in range(2):
                        n = tt * 2 + s
                        e.wait_ge(down_used, (n + 1) * E + SPARE)
                        for h in range(2):
                            e.dma_start(out[bass.ds(n * 2 + h, 1), :, :].rearrange("b (q p) d -> p (b q) d", p=128),
                                        acc[:, s, 2 * h:2 * h + 2, :]).then_inc(stored[s], 16)
                for s in range(2):
                    e.wait_ge(stored[s], NTT * 16)

            @block.tensor
            def _(e):
                def ups(n, s, x, ks, first=False):
                    for k in ks:
                        if not first:
                            e.wait_ge(gelu_ready, n * (E * KB) + (x * KB + k - 3))
                        w = slice(k * 128, (k + 1) * 128)
                        e.matmul(up[:, k, :], w1[:, HIGH, x, w], h_t[:, s, HIGH, :], start=True, stop=False)
                        e.matmul(up[:, k, :], w1[:, HIGH, x, w], h_t[:, s, LOW, :], start=False, stop=False)
                        e.matmul(up[:, k, :], w1[:, LOW, x, w], h_t[:, s, HIGH, :], start=False, stop=True).then_inc(up_ready, 1)

                def downs(n, x):
                    e.wait_ge(y_taken, n * E + (x - 1 + SPARE))
                    for k in range(KB):
                        e.wait_ge(low_ready, n * (E * KB) + (x * KB + k + 1 + KB))
                        w = slice(k * 128, (k + 1) * 128)
                        o = y_t[:, x % 2, :]
                        e.matmul(o, w2[:, HIGH, x, w], mid[:, x % 2, HIGH, k, :], start=(k == 0), stop=False)
                        e.matmul(o, w2[:, LOW, x, w], mid[:, x % 2, HIGH, k, :], start=False, stop=False)
                        ins = e.matmul(o, w2[:, HIGH, x, w], mid[:, x % 2, LOW, k, :], start=False, stop=(k == KB - 1))
                    ins.then_inc(y_ready, 1)

                def turn(n, x):
                    e.wait_ge(y_taken, n * E + (x + 1 + SPARE))
                    e.wait_ge(down_used, n * E + (x - 1 + SPARE))
                    for q in range(4):
                        ins = e.transpose(down[:, x % 2, q, :], y_sb[:, x % 2, q * 128:(q + 1) * 128], ident[:, :])
                    ins.then_inc(down_ready, 1)

                def run(pair, s, last):
                    n = pair * 2 + s
                    for x in range(E):
                        step_after = (n, s, x + 1) if x + 1 < E else (n + 1, 1 - s, 0)
                        if x + 1 == E and not last:
                            e.wait_ge(h_ready, n + 2)
                        if not (x + 1 == E and last):
                            ups(*step_after, range(0, KB // 2))
                        downs(n, x)
                        if not (x + 1 == E and last):
                            ups(*step_after, range(KB // 2, KB))
                        turn(n, x)

                e.sem_inc(y_ready, SPARE)
                e.wait_ge(w1_ready, PIECES)
                e.wait_ge(h_ready, 1)
                ups(0, 0, 0, range(KB), first=True)
                e.wait_ge(w2_ready, PIECES)
                chain_of_blocks(e, run)

            @block.scalar
            def _(e):
                def high_of_h(pair, s):
                    e.wait_ge(h_loaded[s], pair * 16 + 16)
                    e.copy(h_t[:, s, HIGH, :], h_raw[:, s, :]).then_inc(h_high, 1)

                def run(pair, s, last):
                    n = pair * 2 + s
                    for x in range(E):
                        e.wait_ge(y_ready, n * E + (x - 1 + SPARE))
                        for k in range(KB):
                            e.wait_ge(low_ready, n * (E * KB) + (x * KB + k + 1))
                            i = x * KB + k
                            e.wait_ge(up_ready, n * (E * KB) + (i + 1))
                            e.activation(act_out[:, k, :], up[:, k, :], ACT.Gelu, bias=eb1[:, i:i + 1])
                            e.activation(mid[:, x % 2, HIGH, k, :], up[:, k, :], ACT.Gelu, bias=eb1[:, i:i + 1]).then_inc(gelu_ready, 1)
                        if x == E // 2 and not last:
                            high_of_h(pair + s, 1 - s)

                for i in range(PIECES):
                    e.dma_start(w1_raw[:, i * EP:(i + 1) * EP, :],
                                a["w1"][i * EP:(i + 1) * EP].rearrange("x p n -> p x n")).then_inc(w1_loaded[i], 16)
                high_of_h(0, 0)
                for w, raw, loaded in ((w1, w1_raw, w1_loaded), (w2, w2_raw, w2_loaded)):
                    for i in range(PIECES):
                        e.wait_ge(loaded[i], 16)
                        xs = slice(i * EP, (i + 1) * EP)
                        e.copy(w[:, HIGH, xs, :].rearrange("p x n -> p (x n)"),
                               raw[:, xs, :].rearrange("p x n -> p (x n)")).then_inc(w_high, 1)
                e.wait_ge(bias_loaded, 32)
                chain_of_blocks(e, run)

            @block.vector
            def _(e):
                def low_of_h(n, s):
                    e.wait_ge(h_high, n + 1)
                    e.tensor_tensor(h_t[:, s, LOW, :], h_raw[:, s, :], h_t[:, s, HIGH, :].bitcast(F32),
                                    ALU.subtract).then_inc(h_ready, 1)

                def lows(n, x, ks):
                    for k in ks:
                        e.wait_ge(gelu_ready, n * (E * KB) + (x * KB + k + 1))
                        m = mid[:, x % 2, :, k, :]
                        e.tensor_tensor(m[:, LOW, :], act_out[:, k, :], m[:, HIGH, :].bitcast(F32),
                                        ALU.subtract).then_inc(low_ready, 1)

                def run(pair, s, last):
                    n = pair * 2 + s
                    for x in range(E):
                        step_after = (n, x + 1) if x + 1 < E else (n + 1, 0)
                        if not (x + 1 == E and last):
                            lows(*step_after, range(0, KB // 2))
                        e.wait_ge(y_ready, n * E + (x + 1 + SPARE))
                        e.tensor_scalar(y_sb[:, x % 2, :], y_t[:, x % 2, :], eb2[:, x:x + 1], None, ALU.add).then_inc(y_taken, 1)
                        if not (x + 1 == E and last):
                            lows(*step_after, range(KB // 2, KB))
                        if x == E // 2 and not last:
                            low_of_h(n + 1, 1 - s)
                        if x == 0:
                            e.wait_ge(acc_loaded[s], pair * 16 + 16)
                        e.wait_ge(down_ready, n * E + (x + 1))
                        e.wait_ge(down_used, n * E + (x + SPARE))
                        for q in range(4):
                            w = w_all[:, bass.ds(n * 4 + q, 1), x:x + 1].rearrange("p a b -> p (a b)")
                            ins = e.scalar_tensor_tensor(acc[:, s, q, :], down[:, x % 2, q, :], w, acc[:, s, q, :], ALU.mult, ALU.add)
                        ins.then_inc(down_used, 1)

                e.sem_inc(y_taken, SPARE)
                e.sem_inc(low_ready, KB)
                e.sem_inc(down_used, SPARE)
                low_of_h(0, 0)
                for j, (w, raw, ready) in enumerate(((w1, w1_raw, w1_ready), (w2, w2_raw, w2_ready))):
                    for i in range(PIECES):
                        e.wait_ge(w_high, j * PIECES + i + 1)
                        xs = slice(i * EP, (i + 1) * EP)
                        whole, hi = (v.rearrange("p x n -> p (x n)") for v in (raw[:, xs, :], w[:, HIGH, xs, :].bitcast(F32)))
                        e.tensor_tensor(w[:, LOW, xs, :].rearrange("p x n -> p (x n)"), whole, hi,
                                        ALU.subtract).then_inc(ready, 1)
                e.wait_ge(bias_loaded, 32)
                lows(0, 0, range(KB))
                chain_of_blocks(e, run)


_IN = ["x", "ctx", "lens", "wqT0", "wkT0", "wv0", "wo0", "wfc", "wproj", "uT", "fastT", "v", "gate",
       "wq1", "wk1", "wv1", "wo1", "wq3", "wk3", "wv3", "wp3", "gate_w", "rows", "slot_c", "aug_w",
       "w1", "w2", "eb1", "eb2"]


def _slots(w, places):
    w = np.asarray(w)
    o = np.zeros((w.shape[0], H1, 32), w.dtype)
    for at in places:
        o[:, :, at:at + HD1] = w.reshape(w.shape[0], H1, HD1)
    return o.reshape(w.shape[0], H1 * 32)


def kernel(**inputs):
    import concourse.bacc as bacc
    from concourse.bass_utils import run_bass_kernel_spmd

    i = {k: np.asarray(v) for k, v in inputs.items()}
    f = i["x"].dtype
    three = (0, HD1, 2 * HD1)

    def columns(v):
        return v.reshape(G1, 128).T

    signs = np.zeros((128, 2), f)
    const = np.zeros((128, 3 * G1), f)
    aug = np.zeros((128, 128), f)
    for j in range(4):
        signs[32 * j + HD1:32 * j + 2 * HD1, 0] = -1
        signs[32 * j + 2 * HD1:32 * j + 3 * HD1, 1] = -1
        const[32 * j + 24, 0:G1] = 1
        const[32 * j + 25, 2 * G1:] = 1
        aug[0, 32 * j + 24] = 1
        aug[32, 32 * j + 25] = 1
    biases = np.concatenate([np.zeros((128, G1), f), columns(_slots(i["L1_ffn_bq"][None], three)),
                             columns(_slots(i["L1_ffn_bk"][None], three))], axis=1)
    slot_c = np.concatenate([signs, np.where(const != 0, const, biases)], axis=1)
    every = lambda v: np.broadcast_to(v.reshape(1, -1), (128, v.size))
    arrays = {
        "x": i["x"], "ctx": i["ctx_1024"], "lens": i["_lenS2"].reshape(1, B),
        "wqT0": i["L0_xattn_Wq"].T, "wkT0": i["L0_xattn_Wk"].T, "wv0": i["L0_xattn_Wv"], "wo0": i["L0_xattn_Wo"],
        "wfc": i["L0_ffn_w_fc"], "wproj": i["L0_ffn_w_proj"], "uT": i["L0_ffn_u"].T, "fastT": i["L0_ffn_fast_b"].T,
        "v": i["L0_ffn_v"], "gate": every(i["L0_ffn_gate"]),
        "wq1": _slots(i["L1_xattn_Wq"], three), "wk1": _slots(i["L1_xattn_Wk"], three), "wv1": i["L1_xattn_Wv"],
        "wo1": i["L1_xattn_Wo"],
        "wq3": _slots(i["L1_ffn_Wq"], three), "wk3": _slots(i["L1_ffn_Wk"], three), "wv3": i["L1_ffn_Wv"],
        "wp3": i["L1_ffn_Wp"], "gate_w": i["L1_ffn_gate_W"],
        "rows": np.concatenate([every(i[k]) for k in (
            "L0_xattn_bo", "L1_ffn_bv", "L1_ffn_bp", "L1_ffn_ln1_g", "L1_ffn_ln1_b", "L1_ffn_ln2_g", "L1_ffn_ln2_b",
            "L1_ffn_gate_b")], axis=1),
        "slot_c": slot_c, "aug_w": aug,
        "w1": i["L1_ffn_exp_W1"], "w2": i["L1_ffn_exp_W2"],
        "eb1": i["L1_ffn_exp_b1"].reshape(E * 4, 128).T, "eb2": i["L1_ffn_exp_b2"].T,
    }
    nc = bacc.Bacc("TRN2", target_bir_lowering=False, num_devices=1)
    given, aps = {}, {}
    for name in _IN:
        v = np.ascontiguousarray(arrays[name])
        given[f"in_{name}"] = v
        aps[name] = nc.dram_tensor(f"in_{name}", v.shape, mybir.dt.from_np(v.dtype), kind="ExternalInput").ap()
    out = nc.dram_tensor("out", (B, T, D), F32, kind="ExternalOutput").ap()
    build(nc, aps, out)
    r = run_bass_kernel_spmd(nc, [given], core_ids=[0])
    return r.results[0]["out"]
```
